# Optimizing a Trainium2 kernel written in Bass

```python
import numpy as np
import jax
import jax.numpy as jnp

def _softmax(x, axis=-1):
    return jax.nn.softmax(x, axis=axis)

def _gelu(x):
    return jax.nn.gelu(x, approximate=True)

def _silu(x):
    return jax.nn.silu(x)

def _sigmoid(x):
    return jax.nn.sigmoid(x)

def _layernorm(x, axis=-1, eps=1e-05):
    m = jnp.mean(x, axis=axis, keepdims=True)
    v = jnp.var(x, axis=axis, keepdims=True)
    return (x - m) / jnp.sqrt(v + eps)

def _scatter_add(tgt, idx, src, axis=0):
    return tgt.at[idx].add(src)

def _segment_sum(src, seg, n):
    return jax.ops.segment_sum(src, seg, n)
kernel_name = 'mk_perceiver_d1_seqx_r2_02f293'

def setup_inputs(seed: int=0):
    np.random.seed(seed)
    _w = jnp.asarray

    def _rec_inputs():
        import jax
        import jax.numpy as jnp
        _rk = jax.random.key(seed)
        x = -0.000125 + 0.9999 * jax.random.normal(jax.random.fold_in(_rk, 1), (16, 64, 512), jnp.float32)
        _lenS = 64 - jax.random.randint(jax.random.fold_in(_rk, 7), (16,), 0, max(1, 64 // 4) + 1, jnp.int32)
        _lenS2 = 512 - jax.random.randint(jax.random.fold_in(_rk, 8), (16,), 0, max(1, 512 // 4) + 1, jnp.int32)
        _ctx_768P = jax.random.normal(jax.random.fold_in(_rk, 11), (16, 16, 384), jnp.float32)
        _ctx_768c = jax.random.dirichlet(jax.random.fold_in(_rk, 511), 0.3 * jnp.ones((16,), jnp.float32), (16, 512))
        _ctx_768t = jnp.einsum('bsk,bkd->bsd', _ctx_768c, _ctx_768P)
        _ctx_768t = _ctx_768t * jax.lax.rsqrt(jnp.mean(jnp.square(_ctx_768t)) + 1e-12) * 0.953939
        ctx_768 = 0.00272024 + 0.999456 * (_ctx_768t + 0.3 * jax.random.normal(jax.random.fold_in(_rk, 611), (16, 512, 384), jnp.float32))
        return (x, ctx_768)
    x, ctx_768 = _rec_inputs()

    def _L0_xattn_setup():
        import jax, jax.numpy as jnp
        import numpy as np
        QUERY_DIM = 512
        CONTEXT_DIM = 384
        HEADS = 8
        DIM_HEAD = 64
        INNER = HEADS * DIM_HEAD
        key = jax.random.key(seed)
        ks = jax.random.split(key, 7)
        B, S, L = (8, 2048, 77)
        x = jax.random.normal(ks[0], (B, S, QUERY_DIM), dtype=jnp.float32)
        context = jax.random.normal(ks[1], (B, L, CONTEXT_DIM), dtype=jnp.float32)
        Wq = jax.random.normal(ks[2], (QUERY_DIM, INNER), dtype=jnp.float32) * QUERY_DIM ** (-0.5)
        Wk = jax.random.normal(ks[3], (CONTEXT_DIM, INNER), dtype=jnp.float32) * CONTEXT_DIM ** (-0.5)
        Wv = jax.random.normal(ks[4], (CONTEXT_DIM, INNER), dtype=jnp.float32) * CONTEXT_DIM ** (-0.5)
        Wo = jax.random.normal(ks[5], (INNER, QUERY_DIM), dtype=jnp.float32) * INNER ** (-0.5)
        bo = jax.random.normal(ks[6], (QUERY_DIM,), dtype=jnp.float32) * 0.01
        return {'x': x, 'context': context, 'Wq': Wq, 'Wk': Wk, 'Wv': Wv, 'Wo': Wo, 'bo': bo}
    _L0_xattn_all = _L0_xattn_setup()
    _L0_xattn_in = {k: v for k, v in _L0_xattn_all.items() if k in ('Wq', 'Wk', 'Wv', 'Wo', 'bo')}
    del _L0_xattn_all

    def _L0_attn_setup():
        import jax, jax.numpy as jnp
        import numpy as np
        B, N, D, H = (4, 2048, 512, 16)
        HD = D // H
        EPS_NORM = 1e-12
        EPS_LN = 1e-05

        def _silu(x):
            return x * jax.nn.sigmoid(x)

        def _simple_gla(q, k, v, f):
            qT = jnp.moveaxis(q, 1, 0)
            kT = jnp.moveaxis(k, 1, 0)
            vT = jnp.moveaxis(v, 1, 0)
            fT = jnp.moveaxis(f, 1, 0)

            def step(S, inp):
                qt, kt, vt, ft = inp
                S = jnp.exp(ft)[..., None, None] * S + kt[..., :, None] * vt[..., None, :]
                o = jnp.einsum('bhk,bhkv->bhv', qt, S)
                return (S, o)
            S0 = jnp.zeros((q.shape[0], q.shape[2], q.shape[3], v.shape[3]), q.dtype)
            _, o = jax.lax.scan(step, S0, (qT, kT, vT, fT))
            return jnp.moveaxis(o, 0, 1)
        key = jax.random.key(seed)
        ks = jax.random.split(key, 9)
        s = 0.02
        return {'x': jax.random.normal(ks[0], (B, N, D), jnp.float32), 'Wq': jax.random.normal(ks[1], (D, D), jnp.float32) * s, 'Wk': jax.random.normal(ks[2], (D, D), jnp.float32) * s, 'Wv': jax.random.normal(ks[3], (D, D), jnp.float32) * s, 'Wf': jax.random.normal(ks[4], (H, D), jnp.float32) * s, 'Wg1': jax.random.normal(ks[5], (HD, D), jnp.float32) * s, 'Wg2': jax.random.normal(ks[6], (D, HD), jnp.float32) * s, 'ln_w': jnp.ones((D,), jnp.float32), 'Wo': jax.random.normal(ks[7], (D, D), jnp.float32) * s}
    _L0_attn_all = _L0_attn_setup()
    _L0_attn_in = {k: v for k, v in _L0_attn_all.items() if k in ('Wq', 'Wk', 'Wv', 'Wf', 'Wg1', 'Wg2', 'ln_w', 'Wo')}
    del _L0_attn_all

    def _L0_ffn_setup():
        import jax, jax.numpy as jnp
        import numpy as np
        TOP_K = 2
        key = jax.random.key(seed)
        ks = jax.random.split(key, 6)
        B, S, D, F, E = (4, 1024, 512, 2048, 8)
        sd = 1.0 / np.sqrt(D)
        sf = 1.0 / np.sqrt(F)
        return {'x': jax.random.normal(ks[0], (B, S, D), dtype=jnp.float32), 'gate_w': jax.random.normal(ks[1], (D, E), dtype=jnp.float32) * sd, 'w1': jax.random.normal(ks[2], (E, D, F), dtype=jnp.float32) * sd, 'b1': jax.random.normal(ks[3], (E, F), dtype=jnp.float32) * 0.01, 'w2': jax.random.normal(ks[4], (E, F, D), dtype=jnp.float32) * sf, 'b2': jax.random.normal(ks[5], (E, D), dtype=jnp.float32) * 0.01}
    _L0_ffn_all = _L0_ffn_setup()
    _L0_ffn_in = {k: v for k, v in _L0_ffn_all.items() if k in ('gate_w', 'w1', 'b1', 'w2', 'b2')}
    del _L0_ffn_all
    return {'x': x, 'ctx_768': ctx_768, 'L0_xattn_Wq': _L0_xattn_in['Wq'], 'L0_xattn_Wk': _L0_xattn_in['Wk'], 'L0_xattn_Wv': _L0_xattn_in['Wv'], 'L0_xattn_Wo': _L0_xattn_in['Wo'], 'L0_xattn_bo': _L0_xattn_in['bo'], 'L0_attn_Wq': _L0_attn_in['Wq'], 'L0_attn_Wk': _L0_attn_in['Wk'], 'L0_attn_Wv': _L0_attn_in['Wv'], 'L0_attn_Wf': _L0_attn_in['Wf'], 'L0_attn_Wg1': _L0_attn_in['Wg1'], 'L0_attn_Wg2': _L0_attn_in['Wg2'], 'L0_attn_ln_w': _L0_attn_in['ln_w'], 'L0_attn_Wo': _L0_attn_in['Wo'], 'L0_ffn_gate_w': _L0_ffn_in['gate_w'], 'L0_ffn_w1': _L0_ffn_in['w1'], 'L0_ffn_b1': _L0_ffn_in['b1'], 'L0_ffn_w2': _L0_ffn_in['w2'], 'L0_ffn_b2': _L0_ffn_in['b2']}

def reference(x, ctx_768, L0_xattn_Wq, L0_xattn_Wk, L0_xattn_Wv, L0_xattn_Wo, L0_xattn_bo, L0_attn_Wq, L0_attn_Wk, L0_attn_Wv, L0_attn_Wf, L0_attn_Wg1, L0_attn_Wg2, L0_attn_ln_w, L0_attn_Wo, L0_ffn_gate_w, L0_ffn_w1, L0_ffn_b1, L0_ffn_w2, L0_ffn_b2):
    import jax
    import jax.numpy as jnp

    def _L0_xattn_ref(x, context, Wq, Wk, Wv, Wo, bo):
        import jax, jax.numpy as jnp
        import numpy as np
        QUERY_DIM = 512
        CONTEXT_DIM = 384
        HEADS = 8
        DIM_HEAD = 64
        INNER = HEADS * DIM_HEAD
        B, S, _ = x.shape
        L = context.shape[1]
        scale = DIM_HEAD ** (-0.5)
        q = (x @ Wq).reshape(B, S, HEADS, DIM_HEAD).transpose(0, 2, 1, 3)
        k = (context @ Wk).reshape(B, L, HEADS, DIM_HEAD).transpose(0, 2, 1, 3)
        v = (context @ Wv).reshape(B, L, HEADS, DIM_HEAD).transpose(0, 2, 1, 3)
        attn = jnp.einsum('bhsd,bhld->bhsl', q, k) * scale
        attn = jax.nn.softmax(attn, axis=-1)
        out = jnp.einsum('bhsl,bhld->bhsd', attn, v)
        out = out.transpose(0, 2, 1, 3).reshape(B, S, INNER)
        return out @ Wo + bo

    def _L0_attn_ref(x, Wq, Wk, Wv, Wf, Wg1, Wg2, ln_w, Wo):
        import jax, jax.numpy as jnp
        import numpy as np
        B, N, D, H = (4, 2048, 512, 16)
        HD = D // H
        EPS_NORM = 1e-12
        EPS_LN = 1e-05

        def _silu(x):
            return x * jax.nn.sigmoid(x)

        def _simple_gla(q, k, v, f):
            qT = jnp.moveaxis(q, 1, 0)
            kT = jnp.moveaxis(k, 1, 0)
            vT = jnp.moveaxis(v, 1, 0)
            fT = jnp.moveaxis(f, 1, 0)

            def step(S, inp):
                qt, kt, vt, ft = inp
                S = jnp.exp(ft)[..., None, None] * S + kt[..., :, None] * vt[..., None, :]
                o = jnp.einsum('bhk,bhkv->bhv', qt, S)
                return (S, o)
            S0 = jnp.zeros((q.shape[0], q.shape[2], q.shape[3], v.shape[3]), q.dtype)
            _, o = jax.lax.scan(step, S0, (qT, kT, vT, fT))
            return jnp.moveaxis(o, 0, 1)
        b, n, d = x.shape
        q = _silu(x @ Wq.T).reshape(b, n, H, HD)
        k = _silu(x @ Wk.T).reshape(b, n, H, HD)
        v = _silu(x @ Wv.T).reshape(b, n, H, HD)
        f = jax.nn.log_sigmoid(x @ Wf.T)
        k = k / jnp.maximum(jnp.linalg.norm(k, axis=-1, keepdims=True), EPS_NORM)
        o = _simple_gla(q, k, v, f).reshape(b, n, d)
        gate = jax.nn.sigmoid(x @ Wg1.T @ Wg2.T)
        o = o * gate
        mu = jnp.mean(o, axis=-1, keepdims=True)
        xc = o - mu
        var = jnp.mean(xc * xc, axis=-1, keepdims=True)
        o = xc / jnp.sqrt(var + EPS_LN) * ln_w
        return o @ Wo.T

    def _L0_ffn_ref(x, gate_w, w1, b1, w2, b2):
        import jax, jax.numpy as jnp
        import numpy as np
        TOP_K = 2
        B, S, D = x.shape
        E = gate_w.shape[1]
        xf = x.reshape(-1, D)
        T = xf.shape[0]
        logits = xf @ gate_w
        top_vals, top_idx = jax.lax.top_k(logits, TOP_K)
        wts = jax.nn.softmax(top_vals.astype(jnp.float32), axis=-1).astype(x.dtype)
        rows = jnp.arange(T)[:, None]
        combine = jnp.zeros((T, E), dtype=x.dtype).at[rows, top_idx].add(wts)
        out = jnp.zeros_like(xf)
        for e in range(E):
            h = jax.nn.gelu(xf @ w1[e] + b1[e], approximate=False)
            out = out + combine[:, e:e + 1] * (h @ w2[e] + b2[e])
        return out.reshape(B, S, D)
    x = x + _L0_xattn_ref(_layernorm(x, axis=-1), ctx_768, L0_xattn_Wq, L0_xattn_Wk, L0_xattn_Wv, L0_xattn_Wo, L0_xattn_bo)
    x = x + _L0_attn_ref(_layernorm(x, axis=-1), L0_attn_Wq, L0_attn_Wk, L0_attn_Wv, L0_attn_Wf, L0_attn_Wg1, L0_attn_Wg2, L0_attn_ln_w, L0_attn_Wo)
    x = x + _L0_ffn_ref(_layernorm(x, axis=-1), L0_ffn_gate_w, L0_ffn_w1, L0_ffn_b1, L0_ffn_w2, L0_ffn_b2)
    return x

_drawn_inputs = setup_inputs


def setup_inputs(seed=0):
    import zlib

    import numpy as np

    out = dict(_drawn_inputs(seed))
    spreads = {'L0_attn_ln_w': (1.0, 0.2)}
    factors = {'L0_ffn_b1': 8.0, 'L0_ffn_b2': 8.0}
    for name, (base, spread) in spreads.items():
        noise = np.random.default_rng([zlib.crc32(name.encode()), seed]).standard_normal(out[name].shape)
        drawn = base * np.exp(spread * noise) if base else spread * noise
        out[name] = jnp.asarray(drawn.astype(out[name].dtype))
    for name, factor in factors.items():
        out[name] = (out[name] * factor).astype(out[name].dtype)
    return out
```

```python
import concourse.bass as bass
from concourse import mybir
from contextlib import ExitStack


def perceiver_layer(
    nc: bass.Bass,
    x: bass.AP,
    ctxT: bass.AP,
    xWq: bass.AP,
    xWk: bass.AP,
    xWv: bass.AP,
    xWo: bass.AP,
    xbo: bass.AP,
    aWqT: bass.AP,
    aWkT: bass.AP,
    aWvT: bass.AP,
    aWfT: bass.AP,
    aWg1T: bass.AP,
    aWg2T: bass.AP,
    a_ln_w: bass.AP,
    aWoT: bass.AP,
    gate_w: bass.AP,
    w1: bass.AP,
    b1T: bass.AP,
    w2: bass.AP,
    b2: bass.AP,
    out: bass.AP,
    slots: bass.AP,
):
    fp32 = mybir.dt.float32
    i32 = mybir.dt.int32
    u32 = mybir.dt.uint32
    ALU = mybir.AluOpType
    ACT = mybir.ActivationFunctionType
    AX = mybir.AxisListType

    P = 128
    D = x.shape[1]
    NT = x.shape[0] // P
    KD = D // P
    NB, C, L = ctxT.shape
    S = x.shape[0] // NB
    KC = C // P
    LC = L // P
    XH = 8
    DH = D // XH
    PAIRS = XH // 2
    SCALE = DH ** -0.5
    H = 16
    HD = D // H
    HR = P // HD
    E, _, F = w1.shape
    KF = F // P
    MAX_TILES = 2 * NT + E - 1
    EPS = 1e-5
    KB = 1024
    BASE = 16512

    ctx = ExitStack()
    with ctx:
        used = [0]
        ctx.enter_context(nc.sbuf_tensor("arena", [P, 52000], fp32))

        def at(name, shape, offset, dt=fp32):
            return nc.alloc_sbuf_tensor_at(name, shape, dt, offset=BASE + offset)

        def const(name, shape, dt=fp32):
            n = 4
            for s in shape[1:]:
                n *= s
            n = (n + 31) // 32 * 32
            h = at(name, shape, 192 * KB + used[0], dt)
            used[0] += n
            return h

        def sem(name):
            return ctx.enter_context(nc.semaphore(name))

        xs = at("xs", [P, NT, D], 144 * KB)
        xn = at("xn", [P, NT, D], 160 * KB)
        xnT = at("xnT", [P, KD, NT * P], 176 * KB)
        ident = const("ident", [P, P])
        causal = const("causal", [P, P])
        after = const("after", [P, P])
        before = const("before", [P, P])
        ones = const("ones", [P, P])
        bo_rows = const("bo_rows", [P, D])
        lnw_rows = const("lnw_rows", [P, D])
        gw = const("gw", [P, KD, E])
        wf = const("wf", [P, KD, H])
        stats = const("stats", [P, 2, 6])
        mv = const("mv", [P, 4, NT, 2])
        vare = const("vare", [P, 4, NT])
        rstd = const("rstd", [P, 4, NT])
        mhalf = const("mhalf", [P, H])
        rowmax = const("rowmax", [P, PAIRS])
        negmax = const("negmax", [P, PAIRS])
        rowsum = const("rowsum", [P, PAIRS])
        rowinv = const("rowinv", [P, PAIRS])
        zf = const("zf", [P, NT, H])
        fa = const("fa", [P, NT, H])
        fb = const("fb", [P, NT, H])
        ksum = const("ksum", [P, 2, H])
        knorm = const("knorm", [P, 2, H])
        logit = const("logit", [P, NT, E])
        tcount = const("tcount", [P, E])
        tstart = const("tstart", [P, E + 1])
        bounds = const("bounds", [P, 16], i32)
        wgt = const("wgt", [P, 2, NT])
        slot_u = const("slot_u", [P, 2, NT], u32)
        b1_sb = const("b1_sb", [P, E, KF])
        b2_sb = const("b2_sb", [E, D])
        zeros = const("zeros", [P, D])
        lower = const("lower", [P, E, E])
        steps = const("steps", [P, NT])
        assert used[0] <= 15 * KB + 800, used[0]

        OT = at("OT", [P, PAIRS, NT * P], 0)
        wo1 = at("wo1", [P, KD, D], 16 * KB)
        wqT2 = at("wqT2", [P, KD, D], 24 * KB)
        wkT2 = at("wkT2", [P, KD, D], 32 * KB)
        wvT2 = at("wvT2", [P, KD, D], 40 * KB)
        wg1 = at("wg1", [P, KD, 32], 48 * KB)
        wg2 = at("wg2", [32, D], 49 * KB)
        wq1 = at("wq1", [P, KD, D], 56 * KB)
        wk1 = at("wk1", [P, KC, D], 64 * KB)
        wv1 = at("wv1", [P, KC, D], 70 * KB)
        cT = [at(f"cT{u}", [P, KC, L], (76 + 6 * u) * KB) for u in range(2)]
        KT = at("KT", [P, PAIRS, L], 88 * KB)
        V = [at(f"V{u}", [P, LC, D], (96 + 8 * u) * KB) for u in range(2)]
        prob = at("prob", [P, PAIRS, L], 112 * KB)
        PT = [at(f"PT{u}", [P, LC, P], (120 + 2 * u) * KB) for u in range(2)]
        qbd = [at(f"qbd{u}", [P, PAIRS, P], (124 + 2 * u) * KB) for u in range(2)]
        qT1 = at("qT1", [P, PAIRS, NT * P], 128 * KB)
        ksil = at("ksil", [P, NT, D], 0)
        t1T = at("t1T", [32, NT * P], 51 * KB)
        Mf = at("Mf", [P, HR, HR, P], 55 * KB)
        ksq = at("ksq", [P, D], 128 * KB)
        qT2 = at("qT2", [P, KD, NT * P], 64 * KB)
        kT2 = at("kT2", [P, KD, NT * P], 80 * KB)
        vt = at("vt", [P, NT, D], 96 * KB)
        dec = [at(f"dec{u}", [P, HR, HR, P], (112 + 8 * u) * KB) for u in range(2)]
        Wt = at("Wt", [P, HR, HR, P], 128 * KB)
        woT2 = at("woT2", [P, KD, D], 136 * KB)
        W1 = [at(f"W1_{u}", [P, KD, F], 64 * u * KB) for u in range(2)]
        W2 = [at(f"W2_{u}", [P, KF, D], (64 * u + 32) * KB) for u in range(2)]
        hT = at("hT", [P, KF, P], 176 * KB)
        xT = at("xT", [P, KD, P], 184 * KB)
        combT = at("combT", [E, NT * P], 128 * KB)
        yg = at("yg", [P, NT, 2, D], 0)
        xrow = at("xrow", [P, D], 188 * KB)
        yrow = at("yrow", [P, D], 190 * KB)
        cmp = at("cmp", [P, NT, E, E], 134 * KB)
        tie = at("tie", [P, NT, E, E], 136 * KB)
        rank = at("rank", [P, NT, E], 138 * KB + 512)
        m0 = at("m0", [P, NT, E], 138 * KB + 768)
        m1 = at("m1", [P, NT, E], 139 * KB)
        selm = at("selm", [P, NT, E], 139 * KB + 256)
        posn = at("posn", [P, NT, E], 139 * KB + 512)
        tsum = at("tsum", [P, NT, E], 139 * KB + 768)
        comb = at("comb", [P, NT, E], 140 * KB)
        lv = at("lv", [P, 2, NT], 140 * KB + 256)
        slotf = at("slotf", [P, 2, NT], 140 * KB + 384)
        ge = at("ge", [P, E, NT], 140 * KB + 576)

        ps = ctx.enter_context(nc.psum_tensor("ps", [P, 8, 512], fp32))

        filled = [sem(f"bank{b}_filled") for b in range(8)]
        emptied = [sem(f"bank{b}_emptied") for b in range(8)]
        plan = {}

        def place(*key):
            plan[key] = (len(plan) % 8, len(plan) // 8)

        def bank(*key):
            return ps[:, plan[key][0], :]

        def claim(pe, *key):
            b, n = plan[key]
            if n:
                pe.wait_ge(emptied[b], n)

        def fill(ins, *key):
            ins.then_inc(filled[plan[key][0]], 1)

        def arrive(eng, *key):
            b, n = plan[key]
            eng.wait_ge(filled[b], n + 1)

        def empty(ins, *key):
            ins.then_inc(emptied[plan[key][0]], 1)

        def taken(eng, *key):
            b, n = plan[key]
            eng.wait_ge(emptied[b], n + 1)

        for t in range(NT):
            place("T1", t)
        for half in range(2):
            for c in range(PAIRS):
                place("q1", half, c)
        RING1 = len(plan)
        for t in range(NT + 2):
            if t < NT:
                place("wo1", t)
            if t >= 2:
                place("T2", t - 2)
        for t in range(NT):
            place("z", t)
        for half in range(2):
            place("t1", half)
        for t in range(NT):
            for what in ("k", "v", "q"):
                place(what, t)
        for t in range(NT):
            place("gate", t)
            place("kT", t)
        LAG_O, LAG_T4, LAG_W, LAG_T5, LAG_R = 1, 2, 2, 4, 4
        for t in range(NT + LAG_R):
            if t < NT:
                for r in range(HR):
                    place("seg", t, r)
                    place("A", t, r)
            if 0 <= t - LAG_O < NT:
                place("o", t - LAG_O)
            if 0 <= t - LAG_T4 < NT:
                place("T4", t - LAG_T4)
                place("wo2", t - LAG_W)
            if 0 <= t - LAG_T5 < NT:
                place("T5", t - LAG_T5)
                place("logit", t - LAG_R)
        place("prefix")
        place("total")
        place("combT", 0)
        place("combT", 1)
        for t in range(NT):
            place("b2", t)
        RING_ALL = len(plan)

        x_in = sem("x_in")
        w_in = sem("w_in")
        w2_in = sem("w2_in")
        woT_in = sem("woT_in")
        consts_ready = sem("consts_ready")
        pool_own = sem("pool_own")
        dve_own = sem("dve_own")
        var_ready = [sem(f"var_ready{k}") for k in range(4)]
        rstd_ready = [sem(f"rstd_ready{k}") for k in range(4)]
        xn_ready = [sem(f"xn_ready{k}") for k in range(4)]
        xnT_ready = [sem(f"xnT_ready{k}") for k in range(4)]
        ctx_in = [sem(f"ctx_in{u}") for u in range(2)]
        v_proj = sem("v_proj")
        k_proj = sem("k_proj")
        k_evac = sem("k_evac")
        v_evac = sem("v_evac")
        qbd_ready = sem("qbd_ready")
        scores = sem("scores")
        raw_max = sem("raw_max")
        neg_max = sem("neg_max")
        exp_done = sem("exp_done")
        inv_done = sem("inv_done")
        norm_done = sem("norm_done")
        pt_done = sem("pt_done")
        pt_evac = sem("pt_evac")
        pv_done = sem("pv_done")
        o_evac = sem("o_evac")
        bo_added = sem("bo_added")
        k_ready = sem("k_ready")
        knorm_in = sem("knorm_in")
        v_ready = sem("v_ready")
        v_scaled = sem("v_scaled")
        q_ready = sem("q_ready")
        f_ready = sem("f_ready")
        f_exp = sem("f_exp")
        f_in = sem("f_in")
        f_ln = sem("f_ln")
        Mf_ready = sem("Mf_ready")
        dec_ready = sem("dec_ready")
        sel_ready = sem("sel_ready")
        p01 = sem("p01")
        e01 = sem("e01")
        comb_ready = sem("comb_ready")
        bounds_ready = sem("bounds_ready")
        slots_ready = sem("slots_ready")
        zero_sent = sem("zero_sent")
        scattered = sem("scattered")
        xrow_in = sem("xrow_in")
        xT_ready = sem("xT_ready")
        up_done = sem("up_done")
        gelu_done = sem("gelu_done")
        down_done = sem("down_done")
        y_sent = sem("y_sent")
        g_in = [sem(f"g_in{t}") for t in range(NT)]
        x_turned = sem("x_turned")
        y_evac = sem("y_evac")
        yrow_free = sem("yrow_free")
        w1_in = [sem(f"w1_in{u}") for u in range(2)]
        w2e_in = [sem(f"w2e_in{u}") for u in range(2)]
        out_ready = sem("out_ready")
        out_sent = sem("out_sent")

        def wait(eng, s, v):
            if not (isinstance(v, int) and v <= 0):
                eng.wait_ge(s, v)

        block = ctx.enter_context(nc.Block())
        blk = lambda w, k: w.rearrange("(k p) n -> p k n", p=P)

        @block.sync
        def _(sp):
            for t in range(NT):
                sp.dma_start(xs[:, t, :], x[t * P:(t + 1) * P, :]).then_inc(x_in, 16)
            sp.dma_start(wq1[:], blk(xWq, KD)).then_inc(w_in, 16)
            sp.dma_start(wk1[:], blk(xWk, KC)).then_inc(w_in, 16)
            for u in range(2):
                sp.dma_start(cT[u][:], ctxT[u].rearrange("(k p) l -> p k l", p=P)).then_inc(ctx_in[u], 16)
            sp.dma_start(wv1[:], blk(xWv, KC)).then_inc(w_in, 16)
            sp.dma_start(bo_rows[:], xbo.to_broadcast([P, D])).then_inc(w_in, 16)
            for dst, src in ((wo1, xWo), (wqT2, aWqT), (wkT2, aWkT), (wvT2, aWvT), (wg1, aWg1T),
                             (wf, aWfT), (gw, gate_w)):
                sp.dma_start(dst[:], src.rearrange("(k p) n -> p k n", p=P)).then_inc(w2_in, 16)
            sp.dma_start(wg2[:], aWg2T).then_inc(w2_in, 16)
            sp.dma_start(lnw_rows[:], a_ln_w.to_broadcast([P, D])).then_inc(w2_in, 16)
            sp.dma_start(b1_sb[:], b1T).then_inc(w2_in, 16)
            sp.dma_start(b2_sb[:], b2).then_inc(w2_in, 16)
            with sp.Fori(1, NB // 2) as p:
                for u in range(2):
                    sp.wait_ge(v_proj, (2 * p + u - 1) * LC)
                    sp.dma_start(cT[u][:], ctxT[bass.ds(2 * p + u, 1)].rearrange("b (k p) l -> p (b k) l", p=P)
                                 ).then_inc(ctx_in[u], 16)
            sp.wait_ge(o_evac, NB)
            sp.dma_start(woT2[:], blk(aWoT, KD)).then_inc(woT_in, 16)
            sp.wait_ge(consts_ready, 2)
            sp.dma_start(slots.rearrange("(t p) n -> p t n", p=P),
                         zeros[:].unsqueeze(1).to_broadcast([P, slots.shape[0] // P, D])).then_inc(zero_sent, 16)
            w1e = w1.rearrange("e (k p) f -> e p k f", p=P)
            w2e = w2.rearrange("e (k p) d -> e p k d", p=P)
            arrive(sp, "kT", NT - 1)
            sp.dma_start(W1[0][:], w1e[0]).then_inc(w1_in[0], 16)
            arrive(sp, "seg", NT - 1, HR - 1)
            sp.dma_start(W2[0][:], w2e[0]).then_inc(w2e_in[0], 16)
            arrive(sp, "A", NT - 1, HR - 1)
            sp.dma_start(W1[1][:], w1e[1]).then_inc(w1_in[1], 16)
            arrive(sp, "o", NT - 1)
            sp.dma_start(W2[1][:], w2e[1]).then_inc(w2e_in[1], 16)
            sp.wait_ge(bounds_ready, 1)
            with sp.Fori(1, E // 2) as p:
                for u in range(2):
                    end = sp.value_load(bounds[0:1, bass.ds(2 * p + u - 1, 1)], min_val=1, max_val=MAX_TILES)
                    sp.wait_ge(down_done, end)
                    sp.dma_start(W1[u][:], w1e[bass.ds(2 * p + u, 1)].rearrange("e p k f -> p (e k) f")
                                 ).then_inc(w1_in[u], 16)
                    sp.dma_start(W2[u][:], w2e[bass.ds(2 * p + u, 1)].rearrange("e p k f -> p (e k) f")
                                 ).then_inc(w2e_in[u], 16)
            for t in range(NT):
                sp.wait_ge(out_ready, t + 1)
                sp.dma_start(out[t * P:(t + 1) * P, :], xs[:, t, :]).then_inc(out_sent, 16)
            sp.wait_ge(out_sent, 16 * NT)

        @block.gpsimd
        def _(pool):
            own = [0]

            def link(ins):
                own[0] += 1
                ins.then_inc(pool_own, 1)
                pool.wait_ge(pool_own, own[0])

            def select(m, pattern, cm, op, base=0, fill=0.0):
                return pool.affine_select(out=m, in_=m, compare_op=op, fill=fill, base=base,
                                          pattern=pattern, channel_multiplier=cm)

            pool.memset(mhalf[:], -0.5).then_inc(consts_ready, 1)
            link(pool.memset(ident[:], 0.0))
            link(select(ident[:], [[-1, P]], 1, ALU.not_equal, fill=1.0))
            for m in (causal, after, before):
                link(pool.memset(m[:], 1.0))
            link(select(causal[:], [[1, P]], -1, ALU.is_ge))
            link(select(after[:], [[-1, P]], 1, ALU.is_gt))
            link(select(before[:], [[1, P]], -1, ALU.is_gt))
            link(pool.memset(causal[0:S, S:P], 0.0))
            link(pool.memset(after[S:P, 0:S], 0.0))
            for u in range(2):
                link(pool.memset(qbd[u][:], 0.0))
            link(pool.memset(zeros[:], 0.0))
            link(pool.memset(lower[:], 1.0))
            link(select(lower[:], [[1, E], [-1, E]], 0, ALU.is_gt))
            for m in range(NT):
                link(pool.memset(steps[:, m:m + 1], float(P * m + 1)))
            pool.memset(ones[:], 1.0).then_inc(consts_ready, 1)

            def powers(kind, t, n=1):
                pool.wait_ge(var_ready[kind], t + n)
                pool.tensor_tensor(rstd[:, kind, t:t + n], vare[:, kind, t:t + n], mhalf[:, 0:n], ALU.pow
                                   ).then_inc(rstd_ready[kind], n)

            for t in range(NT):
                powers(0, t)
            pool.wait_ge(w_in, 4 * 16)
            for t in range(NT):
                pool.wait_ge(xn_ready[0], t + 1)
                pool.tensor_tensor(xs[:, t, :], xs[:, t, :], bo_rows[:], ALU.add).then_inc(bo_added, 1)

            def normalise(b):
                for c in range(PAIRS):
                    pool.wait_ge(inv_done, PAIRS * b + c + 1)
                    pool.tensor_tensor(prob[:, c, :], prob[:, c, :], rowinv[:, c:c + 1].to_broadcast([P, L]), ALU.mult
                                       ).then_inc(norm_done, 1)

            normalise(0)
            normalise(1)
            with pool.Fori(1, NB // 2 - 1) as p:
                for u in range(2):
                    normalise(2 * p + u)
            normalise(NB - 2)
            normalise(NB - 1)

            for t in range(NT):
                powers(1, t)
            for t in range(NT):
                pool.wait_ge(knorm_in, t + 1)
                if t:
                    pool.wait_ge(v_scaled, t)
                link(pool.tensor_tensor(knorm[:, t % 2, :], ksum[:, t % 2, :], mhalf[:], ALU.pow))
                taken(pool, "v", t)
                v3 = vt[:, t, :].rearrange("p (h d) -> p h d", d=HD)
                pool.tensor_tensor(v3, v3, knorm[:, t % 2, :].unsqueeze(2).to_broadcast([P, H, HD]), ALU.mult
                                   ).then_inc(v_scaled, 1)

            def masked_f(t):
                if t:
                    arrive(pool, "seg", t - 1, HR - 1)
                fv = fa[:, t, :].rearrange("p (c r) -> p r c", r=HR)
                for r in range(HR):
                    pool.tensor_tensor(Mf[:, r], after[:].unsqueeze(1).to_broadcast([P, HR, P]),
                                       fv[:, r, :].unsqueeze(2).to_broadcast([P, HR, P]), ALU.mult
                                       ).then_inc(Mf_ready, 1)

            def mask_decay(t):
                for r in range(HR):
                    taken(pool, "seg", t, r)
                    pool.tensor_tensor(dec[t % 2][:, r], dec[t % 2][:, r],
                                       causal[:].unsqueeze(1).to_broadcast([P, HR, P]), ALU.mult
                                       ).then_inc(dec_ready, 1)

            pool.wait_ge(f_ready, 1)
            for t in range(NT + LAG_R):
                if t < NT:
                    masked_f(t)
                    mask_decay(t)
                if 0 <= t - 1 < NT:
                    powers(2, t - 1)
                if 0 <= t - 2 < NT:
                    powers(3, t - 2)

            pool.wait_ge(slots_ready, 1)
            pool.wait_ge(zero_sent, 16)
            for t in range(NT):
                for k in range(2):
                    pool.indirect_dma_start(
                        out=slots, out_offset=bass.IndirectOffsetOnAxis(ap=slot_u[:, k, t:t + 1], axis=0),
                        in_=xn[:, t, :], in_offset=None).then_inc(scattered, 16)
            pool.wait_ge(scattered, 16 * 2 * NT)
            total = pool.value_load(bounds[0:1, E:E + 1], min_val=E, max_val=MAX_TILES)
            taken(pool, "T5", NT - 1)
            arrive(pool, "logit", NT - 1)
            pool.dma_start(xrow[:], slots[0:P, :]).then_inc(xrow_in, 16)
            with pool.Fori(0, total) as i:
                pool.wait_ge(x_turned, i + 1)
                pool.dma_start(xrow[:], slots[bass.ds((i + 1) * P, P), :]).then_inc(xrow_in, 16)
                pool.wait_ge(y_evac, i + 2)
                pool.dma_start(slots[bass.ds(i * P, P), :], yrow[:]).then_inc(y_sent, 16)
                pool.wait_ge(y_sent, i * 16 + 16)
                pool.sem_inc(yrow_free, 1)
            for t in range(NT):
                for k in range(2):
                    pool.indirect_dma_start(
                        out=yg[:, t, k, :], out_offset=None,
                        in_=slots, in_offset=bass.IndirectOffsetOnAxis(ap=slot_u[:, k, t:t + 1], axis=0)
                    ).then_inc(g_in[t], 16)

        @block.scalar
        def _(act):
            def copy(dst, src):
                return act.activation(dst, src, ACT.Copy)

            def q_half(half):
                for c in range(PAIRS):
                    arrive(act, "q1", half, c)
                    n = copy(qT1[:, c, half * 512:(half + 1) * 512], bank("q1", half, c))
                    empty(n, "q1", half, c)

            for t in range(NT):
                arrive(act, "T1", t)
                n = copy(xnT[:, :, t * P:(t + 1) * P], bank("T1", t).rearrange("p (k n) -> p k n", k=KD))
                empty(n, "T1", t)
            q_half(0)
            q_half(1)

            def evac_k(b, c):
                act.wait_ge(k_proj, PAIRS * b + c + 1)
                copy(KT[:, c, :], ps[:, 4 + c % 2, :]).then_inc(k_evac, 1)

            def exps(b, c):
                act.wait_ge(neg_max, PAIRS * b + c + 1)
                wait(act, pt_done, PAIRS * (b - 1) + c + 1)
                act.activation(prob[:, c, :], ps[:, c, :], ACT.Exp, bias=negmax[:, c:c + 1], scale=SCALE,
                               accum_out=rowsum[:, c:c + 1]).then_inc(exp_done, 1)

            def batch(b, more=True):
                for c in range(PAIRS):
                    exps(b, c)
                    if more and c >= 1:
                        evac_k(b + 1, c - 1)
                if more:
                    evac_k(b + 1, PAIRS - 1)

            for c in range(PAIRS):
                evac_k(0, c)
            batch(0)
            batch(1)
            with act.Fori(1, NB // 2 - 1) as p:
                for u in range(2):
                    batch(2 * p + u)
            batch(NB - 2)
            batch(NB - 1, more=False)

            for t in range(NT):
                arrive(act, "T2", t)
                n = copy(xnT[:, :, t * P:(t + 1) * P], bank("T2", t).rearrange("p (k n) -> p k n", k=KD))
                empty(n, "T2", t)
            for half in range(2):
                arrive(act, "t1", half)
                n = copy(t1T[:, half * 512:(half + 1) * 512], bank("t1", half)[0:32, :])
                empty(n, "t1", half)
            for t in range(NT):
                for what, dst, ready in (("k", ksil[:, t, :], k_ready), ("v", vt[:, t, :], v_ready),
                                         ("q", qT2[:, :, t * P:(t + 1) * P], q_ready)):
                    arrive(act, what, t)
                    src = bank(what, t)
                    if what == "q":
                        src = src.rearrange("p (k n) -> p k n", k=KD)
                    n = act.activation(dst, src, ACT.Silu)
                    empty(n, what, t)
            for t in range(NT):
                arrive(act, "gate", t)
                n = act.activation(xn[:, t, :], bank("gate", t), ACT.Sigmoid)
                empty(n, "gate", t)
            act.wait_ge(f_in, 1)
            act.activation(fa[:], fa[:], ACT.Exp).then_inc(f_exp, 1)
            act.wait_ge(f_exp, 1)
            act.activation(fa[:], fa[:], ACT.Ln, bias=1.0).then_inc(f_ln, 1)
            for t in range(NT + LAG_R):
                if t < NT:
                    for r in range(HR):
                        arrive(act, "seg", t, r)
                        if t >= 2:
                            taken(act, "A", t - 2, r)
                        n = act.activation(dec[t % 2][:, r], bank("seg", t, r).rearrange("p (c s) -> p c s", s=P),
                                           ACT.Exp)
                        empty(n, "seg", t, r)
                u = t - LAG_T4
                if 0 <= u < NT:
                    arrive(act, "T4", u)
                    n = copy(xnT[:, :, u * P:(u + 1) * P], bank("T4", u).rearrange("p (k n) -> p k n", k=KD))
                    empty(n, "T4", u)
                u = t - LAG_T5
                if 0 <= u < NT:
                    arrive(act, "T5", u)
                    n = copy(xnT[:, :, u * P:(u + 1) * P], bank("T5", u).rearrange("p (k n) -> p k n", k=KD))
                    empty(n, "T5", u)

            act.wait_ge(p01, 1)
            act.activation(wgt[:, 1, :], lv[:, 0, :], ACT.Exp).then_inc(e01, 1)
            act.wait_ge(bounds_ready, 1)
            act.wait_ge(w2_in, 11 * 16)
            with act.Fori(0, E) as e:
                first = act.value_load(bounds[0:1, bass.ds(e, 1)], min_val=0, max_val=MAX_TILES - 1)
                end = act.value_load(bounds[0:1, bass.ds(e + 1, 1)], min_val=1, max_val=MAX_TILES)
                with act.Fori(first, end) as i:
                    for g in range(KF // 4):
                        act.wait_ge(up_done, i * (KF // 4) + (g + 1))
                        for j in range(4):
                            f = 4 * g + j
                            last = act.activation(hT[:, f, :], ps[:, 4 + g, j * P:(j + 1) * P], ACT.Gelu,
                                                  bias=b1_sb[:, bass.ds(e, 1), f])
                        last.then_inc(gelu_done, 1)

        @block.vector
        def _(dve):
            own = [0]

            def link(ins):
                own[0] += 1
                ins.then_inc(dve_own, 1)
                dve.wait_ge(dve_own, own[0])

            def spread(kind, t, src):
                link(dve.bn_stats(stats[:, 0, :], src))
                link(dve.bn_aggr(mv[:, kind, t, :], stats[:, 0, :]))
                dve.tensor_scalar(vare[:, kind, t:t + 1], mv[:, kind, t, 1:2], EPS, None, ALU.add
                                  ).then_inc(var_ready[kind], 1)

            def centre(kind, t, src):
                dve.wait_ge(rstd_ready[kind], t + 1)
                return dve.tensor_scalar(xn[:, t, :], src, mv[:, kind, t, 0:1], rstd[:, kind, t:t + 1],
                                         ALU.subtract, ALU.mult)

            dve.wait_ge(consts_ready, 1)
            for t in range(NT + 1):
                if t < NT:
                    dve.wait_ge(x_in, 16 * NT)
                    spread(0, t, xs[:, t, :])
                if t:
                    centre(0, t - 1, xs[:, t - 1, :]).then_inc(xn_ready[0], 1)

            def maxes(b):
                for c in range(PAIRS):
                    dve.wait_ge(scores, PAIRS * b + c + 1)
                    dve.reduce_max(rowmax[:, c:c + 1], ps[:, c, :], AX.X).then_inc(raw_max, 1)
                    dve.wait_ge(raw_max, PAIRS * b + c + 1)
                    dve.tensor_scalar(negmax[:, c:c + 1], rowmax[:, c:c + 1], -SCALE, None, ALU.mult
                                      ).then_inc(neg_max, 1)

            def inverses(b):
                for c in range(PAIRS):
                    dve.wait_ge(exp_done, PAIRS * b + c + 1)
                    wait(dve, norm_done, PAIRS * (b - 1) + c + 1)
                    dve.reciprocal(rowinv[:, c:c + 1], rowsum[:, c:c + 1]).then_inc(inv_done, 1)

            def evac_v(b, u, c):
                dve.wait_ge(v_proj, LC * b + c + 1)
                dve.tensor_copy(V[u][:, c, :], ps[:, 4 + c % 2, :]).then_inc(v_evac, 1)

            def evac_pt(b, c):
                dve.wait_ge(pt_done, PAIRS * b + c + 1)
                wait(dve, pv_done, PAIRS * b + c - 1)
                dve.tensor_copy(PT[c % 2][:], ps[:, 6, :].rearrange("p (l n) -> p l n", l=LC)
                                ).then_inc(pt_evac, 1)

            def evac_o(b):
                dve.wait_ge(pv_done, PAIRS * (b + 1))
                for g in range(2):
                    h = slice(g * DH, (g + 1) * DH)
                    o = ps[h, 7, :].rearrange("p (c n) -> p c n", c=PAIRS)
                    last = dve.tensor_copy(OT[h, :, bass.ds(b * S, S)], o[:, :, h])
                last.then_inc(o_evac, 1)

            def block_q(b, u):
                wait(dve, scores, PAIRS * (b - 1))
                for g in range(2):
                    h = slice(g * DH, (g + 1) * DH)
                    last = dve.tensor_copy(qbd[u][h, :, h], qT1[h, :, bass.ds(b * S, S)])
                last.then_inc(qbd_ready, 1)

            def batch(b, u, more=True):
                maxes(b)
                inverses(b)
                if more:
                    block_q(b + 1, 1 - u)
                for c in range(LC):
                    if more:
                        evac_v(b + 1, 1 - u, c)
                    evac_pt(b, c)
                evac_o(b)

            for half in range(2):
                for c in range(PAIRS):
                    taken(dve, "q1", half, c)
            block_q(0, 0)
            for c in range(LC):
                evac_v(0, 0, c)
            batch(0, 0)
            batch(1, 1)
            with dve.Fori(1, NB // 2 - 1) as p:
                for u in range(2):
                    batch(2 * p + u, u)
            batch(NB - 2, 0)
            batch(NB - 1, 1, more=False)

            for t in range(NT + 1):
                if t < NT:
                    arrive(dve, "wo1", t)
                    dve.wait_ge(bo_added, t + 1)
                    n = dve.tensor_tensor(xs[:, t, :], xs[:, t, :], bank("wo1", t), ALU.add)
                    empty(n, "wo1", t)
                    taken(dve, "wo1", t)
                    spread(1, t, xs[:, t, :])
                if t:
                    centre(1, t - 1, xs[:, t - 1, :]).then_inc(xn_ready[1], 1)
            for t in range(NT):
                arrive(dve, "z", t)
                n = dve.tensor_copy(zf[:, t, :], bank("z", t)[:, 0:H])
                empty(n, "z", t)
            for t in range(NT):
                taken(dve, "z", t)
            link(dve.tensor_scalar(fb[:], zf[:], -1.0, None, ALU.mult))
            dve.tensor_tensor(fa[:], zf[:], fb[:], ALU.min).then_inc(f_in, 1)
            for t in range(NT):
                taken(dve, "k", t)
                link(dve.tensor_tensor(ksq[:], ksil[:, t, :], ksil[:, t, :], ALU.mult))
                if t >= 2:
                    dve.wait_ge(v_scaled, t - 1)
                link(dve.tensor_reduce(ksum[:, t % 2, :], ksq[:].rearrange("p (h d) -> p h d", d=HD), AX.X, ALU.add))
                dve.tensor_scalar(ksum[:, t % 2, :], ksum[:, t % 2, :], 1e-24, None, ALU.max
                                  ).then_inc(knorm_in, 1)
            for t in range(NT):
                arrive(dve, "kT", t)
                n = dve.tensor_copy(kT2[:, :, t * P:(t + 1) * P], bank("kT", t).rearrange("p (k n) -> p k n", k=KD))
                empty(n, "kT", t)
            dve.wait_ge(f_ln, 1)
            link(dve.tensor_scalar(fb[:], zf[:], 0.0, None, ALU.min))
            dve.tensor_tensor(fa[:], fb[:], fa[:], ALU.subtract).then_inc(f_ready, 1)

            for t in range(NT + LAG_R):
                if t < NT:
                    for r in range(HR):
                        arrive(dve, "A", t, r)
                        dve.wait_ge(dec_ready, HR * t + r + 1)
                        if t:
                            arrive(dve, "o", t - 1)
                        n = dve.tensor_tensor(Wt[:, r], bank("A", t, r).rearrange("p (c s) -> p c s", s=P),
                                              dec[t % 2][:, r], ALU.mult)
                        empty(n, "A", t, r)
                u = t - LAG_O
                if 0 <= u < NT:
                    arrive(dve, "o", u)
                    taken(dve, "gate", u)
                    n = dve.tensor_tensor(xn[:, u, :], bank("o", u), xn[:, u, :], ALU.mult)
                    empty(n, "o", u)
                    taken(dve, "o", u)
                    spread(2, u, xn[:, u, :])
                    link(centre(2, u, xn[:, u, :]))
                    dve.wait_ge(w2_in, 11 * 16)
                    dve.tensor_tensor(xn[:, u, :], xn[:, u, :], lnw_rows[:], ALU.mult).then_inc(xn_ready[2], 1)
                u = t - 2
                if 0 <= u < NT:
                    arrive(dve, "wo2", u)
                    n = dve.tensor_tensor(xs[:, u, :], xs[:, u, :], bank("wo2", u), ALU.add)
                    empty(n, "wo2", u)
                    taken(dve, "wo2", u)
                    spread(3, u, xs[:, u, :])
                u = t - 3
                if 0 <= u < NT:
                    centre(3, u, xs[:, u, :]).then_inc(xn_ready[3], 1)
                u = t - LAG_R
                if 0 <= u < NT:
                    arrive(dve, "logit", u)
                    n = dve.tensor_copy(logit[:, u, :], bank("logit", u)[:, 0:E])
                    empty(n, "logit", u)
                    taken(dve, "logit", u)

            bc = [P, NT, E, E]
            Lj, Le = logit[:].unsqueeze(2).to_broadcast(bc), logit[:].unsqueeze(3).to_broadcast(bc)
            dve.tensor_tensor(cmp[:], Lj, Le, ALU.is_gt)
            link(dve.tensor_tensor(tie[:], Lj, Le, ALU.is_equal))
            link(dve.tensor_tensor(tie[:], tie[:], lower[:].unsqueeze(1).to_broadcast(bc), ALU.mult))
            link(dve.tensor_tensor(cmp[:], cmp[:], tie[:], ALU.add))
            link(dve.tensor_reduce(rank[:], cmp[:], AX.X, ALU.add))
            dve.tensor_scalar(selm[:], rank[:], 1.5, None, ALU.is_lt).then_inc(sel_ready, 1)
            dve.tensor_scalar(m0[:], rank[:], 0.0, None, ALU.is_equal)
            link(dve.tensor_scalar(m1[:], rank[:], 1.0, None, ALU.is_equal))
            for k, m in ((0, m0), (1, m1)):
                link(dve.tensor_tensor(comb[:], m[:], logit[:], ALU.mult))
                link(dve.tensor_reduce(lv[:, k, :], comb[:], AX.X, ALU.add))
            dve.tensor_tensor(lv[:, 0, :], lv[:, 1, :], lv[:, 0, :], ALU.subtract).then_inc(p01, 1)
            arrive(dve, "total")
            n = dve.tensor_copy(tsum[:], bank("total")[:, 0:NT * E].rearrange("p (t e) -> p t e", e=E))
            empty(n, "total")
            taken(dve, "total")
            for t in range(1, NT):
                link(dve.tensor_tensor(tsum[:, t, :], tsum[:, t, :], tsum[:, t - 1, :], ALU.add))
            link(dve.tensor_tensor(ge[:], tsum[:, NT - 1, :].unsqueeze(2).to_broadcast([P, E, NT]),
                                   steps[:].unsqueeze(1).to_broadcast([P, E, NT]), ALU.is_ge))
            link(dve.tensor_reduce(tcount[:], ge[:], AX.X, ALU.add))
            link(dve.tensor_scalar(tcount[:], tcount[:], 1.0, None, ALU.max))
            link(dve.memset(tstart[:, 0:1], 0.0))
            for e in range(E):
                link(dve.tensor_tensor(tstart[:, e + 1:e + 2], tstart[:, e:e + 1], tcount[:, e:e + 1], ALU.add))
            dve.tensor_copy(bounds[:, 0:E + 1], tstart[:]).then_inc(bounds_ready, 1)
            arrive(dve, "prefix")
            n = dve.tensor_copy(posn[:], bank("prefix")[:, 0:NT * E].rearrange("p (t e) -> p t e", e=E))
            empty(n, "prefix")
            taken(dve, "prefix")
            link(dve.tensor_tensor(posn[:, 1:NT, :], posn[:, 1:NT, :], tsum[:, 0:NT - 1, :], ALU.add))
            link(dve.scalar_tensor_tensor(posn[:], tstart[:, 0:E].unsqueeze(1).to_broadcast([P, NT, E]), float(P),
                                          posn[:], ALU.mult, ALU.add))
            for k, m in ((0, m0), (1, m1)):
                link(dve.tensor_tensor(comb[:], m[:], posn[:], ALU.mult))
                link(dve.tensor_reduce(slotf[:, k, :], comb[:], AX.X, ALU.add))
            dve.tensor_copy(slot_u[:], slotf[:]).then_inc(slots_ready, 1)
            dve.wait_ge(e01, 1)
            link(dve.tensor_scalar(lv[:, 0, :], wgt[:, 1, :], 1.0, None, ALU.add))
            link(dve.reciprocal(wgt[:, 0, :], lv[:, 0, :]))
            link(dve.tensor_tensor(wgt[:, 1, :], wgt[:, 1, :], wgt[:, 0, :], ALU.mult))
            link(dve.tensor_tensor(comb[:], m0[:], wgt[:, 0, :].unsqueeze(2).to_broadcast([P, NT, E]), ALU.mult))
            link(dve.tensor_tensor(posn[:], m1[:], wgt[:, 1, :].unsqueeze(2).to_broadcast([P, NT, E]), ALU.mult))
            dve.tensor_tensor(comb[:], comb[:], posn[:], ALU.add).then_inc(comb_ready, 1)
            for half in range(2):
                arrive(dve, "combT", half)
                n = dve.tensor_copy(combT[:, half * 512:(half + 1) * 512], bank("combT", half)[0:E, :])
                empty(n, "combT", half)
            for t in range(NT):
                arrive(dve, "b2", t)
                n = dve.tensor_tensor(xs[:, t, :], xs[:, t, :], bank("b2", t), ALU.add)
                empty(n, "b2", t)

            total = dve.value_load(bounds[0:1, E:E + 1], min_val=E, max_val=MAX_TILES)
            dve.sem_inc(y_evac, 1)
            dve.sem_inc(yrow_free, 1)

            def evac_x(n):
                dve.wait_ge(x_turned, n)
                dve.tensor_copy(xT[:], ps[:, 1, :].rearrange("p (k n) -> p k n", k=KD)).then_inc(xT_ready, 1)

            evac_x(1)
            with dve.Fori(0, total) as i:
                evac_x(i + 2)
                dve.wait_ge(down_done, i + 1)
                dve.wait_ge(yrow_free, i + 1)
                dve.tensor_copy(yrow[:], ps[:, 0, :]).then_inc(y_evac, 1)
            for t in range(NT):
                dve.wait_ge(g_in[t], 2 * 16)
                for k in range(2):
                    n = dve.scalar_tensor_tensor(xs[:, t, :], yg[:, t, k, :], wgt[:, k, t:t + 1], xs[:, t, :],
                                                 ALU.mult, ALU.add)
                    if k == 0:
                        link(n)
                n.then_inc(out_ready, 1)

        @block.tensor
        def _(pe):
            def product(dst, pairs):
                n = len(pairs)
                for i, (lhsT, rhs) in enumerate(pairs):
                    last = pe.matmul(dst, lhsT, rhs, start=(i == 0), stop=(i == n - 1))
                return last

            def transposes(key, t, src):
                claim(pe, key, t)
                for k in range(KD):
                    last = pe.transpose(bank(key, t)[:, k * P:(k + 1) * P], src[:, k * P:(k + 1) * P], ident[:])
                fill(last, key, t)

            pe.wait_ge(consts_ready, 2)
            for t in range(NT):
                pe.wait_ge(xn_ready[0], t + 1)
                transposes("T1", t, xn[:, t, :])
            pe.wait_ge(w_in, 4 * 16)
            for half in range(2):
                for t in range(half * NT // 2, (half + 1) * NT // 2):
                    taken(pe, "T1", t)
                for c in range(PAIRS):
                    claim(pe, "q1", half, c)
                    fill(product(bank("q1", half, c),
                                 [(wq1[:, k, c * P:(c + 1) * P], xnT[:, k, half * 512:(half + 1) * 512])
                                  for k in range(KD)]), "q1", half, c)

            def proj_k(b, u, c):
                if c >= 2:
                    wait(pe, k_evac, PAIRS * b + c - 1)
                else:
                    wait(pe, v_evac, LC * (b - 1) + c + 3)
                product(ps[:, 4 + c % 2, :], [(wk1[:, k, c * P:(c + 1) * P], cT[u][:, k, :]) for k in range(KC)]
                        ).then_inc(k_proj, 1)

            def proj_v(b, u, c):
                if c >= 2:
                    wait(pe, v_evac, LC * b + c - 1)
                else:
                    wait(pe, k_evac, PAIRS * b + c + 3)
                product(ps[:, 4 + c % 2, :], [(cT[u][:, k, c * P:(c + 1) * P], wv1[:, k, :]) for k in range(KC)]
                        ).then_inc(v_proj, 1)

            def score(b, u, c):
                pe.wait_ge(k_evac, PAIRS * b + c + 1)
                wait(pe, exp_done, PAIRS * (b - 1) + c + 1)
                pe.matmul(ps[:, c, :], qbd[u][:, c, :], KT[:, c, :], start=True, stop=True).then_inc(scores, 1)

            def turn(b, c):
                pe.wait_ge(norm_done, PAIRS * b + c + 1)
                wait(pe, pt_evac, PAIRS * b + c)
                for j in range(LC):
                    last = pe.transpose(ps[:, 6, j * P:(j + 1) * P], prob[:, c, j * P:(j + 1) * P], ident[:])
                last.then_inc(pt_done, 1)

            def attend(b, u, c):
                pe.wait_ge(pt_evac, PAIRS * b + c + 1)
                if c == 0:
                    pe.wait_ge(v_evac, LC * (b + 1))
                    wait(pe, o_evac, b)
                product(ps[:, 7, c * P:(c + 1) * P],
                        [(V[u][:, j, c * P:(c + 1) * P], PT[c % 2][:, j, :]) for j in range(LC)]
                        ).then_inc(pv_done, 1)

            def batch(b, u, nth, more=True):
                pe.wait_ge(qbd_ready, b + 1)
                for c in range(PAIRS):
                    score(b, u, c)
                if more:
                    pe.wait_ge(ctx_in[1 - u], 16 * nth)
                    for c in range(PAIRS):
                        proj_k(b + 1, 1 - u, c)
                for c in range(LC):
                    if more:
                        proj_v(b + 1, 1 - u, c)
                    turn(b, c)
                    if c >= 1:
                        attend(b, u, c - 1)
                attend(b, u, PAIRS - 1)

            for b in range(8):
                pe.wait_ge(emptied[b], RING1 // 8)
            pe.wait_ge(ctx_in[0], 16)
            for c in range(PAIRS):
                proj_k(0, 0, c)
            for c in range(LC):
                proj_v(0, 0, c)
            batch(0, 0, 1)
            batch(1, 1, 2)
            with pe.Fori(1, NB // 2 - 1) as p:
                for u in range(2):
                    batch(2 * p + u, u, p + 1 + u)
            batch(NB - 2, 0, NB // 2)
            batch(NB - 1, 1, None, more=False)

            pe.wait_ge(w2_in, 11 * 16)
            pe.wait_ge(o_evac, NB)
            for t in range(NT + 2):
                if t < NT:
                    claim(pe, "wo1", t)
                    fill(product(bank("wo1", t), [(OT[:, k, t * P:(t + 1) * P], wo1[:, k, :]) for k in range(KD)]),
                         "wo1", t)
                if t >= 2:
                    pe.wait_ge(xn_ready[1], t - 1)
                    transposes("T2", t - 2, xn[:, t - 2, :])
            for t in range(NT):
                claim(pe, "z", t)
                taken(pe, "T2", t)
                fill(product(bank("z", t)[:, 0:H], [(xnT[:, k, t * P:(t + 1) * P], wf[:, k, :]) for k in range(KD)]),
                     "z", t)
            for half in range(2):
                claim(pe, "t1", half)
                fill(product(bank("t1", half)[0:32, :],
                             [(wg1[:, k, :], xnT[:, k, half * 512:(half + 1) * 512]) for k in range(KD)]),
                     "t1", half)
            for t in range(NT):
                for what, w in (("k", wkT2), ("v", wvT2)):
                    claim(pe, what, t)
                    fill(product(bank(what, t), [(xnT[:, k, t * P:(t + 1) * P], w[:, k, :]) for k in range(KD)]),
                         what, t)
                claim(pe, "q", t)
                for c in range(KD):
                    last = product(bank("q", t)[:, c * P:(c + 1) * P],
                                   [(wqT2[:, k, c * P:(c + 1) * P], xnT[:, k, t * P:(t + 1) * P])
                                    for k in range(KD)])
                fill(last, "q", t)
            for half in range(2):
                taken(pe, "t1", half)
            for t in range(NT):
                claim(pe, "gate", t)
                fill(product(bank("gate", t), [(t1T[:, t * P:(t + 1) * P], wg2[:])]), "gate", t)
                taken(pe, "k", t)
                transposes("kT", t, ksil[:, t, :])
            for t in range(NT + LAG_R):
                if t < NT:
                    tok = slice(t * P, (t + 1) * P)
                    taken(pe, "q", t)
                    taken(pe, "kT", t)
                    for r in range(HR):
                        claim(pe, "seg", t, r)
                        pe.wait_ge(Mf_ready, HR * t + r + 1)
                        for c in range(HR):
                            last = pe.matmul(bank("seg", t, r)[:, c * P:(c + 1) * P], Mf[:, r, c, :], causal[:],
                                             start=True, stop=True)
                        fill(last, "seg", t, r)
                        claim(pe, "A", t, r)
                        h = slice(r * HD, (r + 1) * HD)
                        for c in range(HR):
                            last = pe.matmul(bank("A", t, r)[:, c * P:(c + 1) * P], kT2[h, c, tok], qT2[h, c, tok],
                                             start=True, stop=True)
                        fill(last, "A", t, r)
                u = t - LAG_O
                if 0 <= u < NT:
                    claim(pe, "o", u)
                    for r in range(HR):
                        taken(pe, "A", u, r)
                    pe.wait_ge(v_scaled, u + 1)
                    for c in range(HR):
                        for r in range(HR):
                            h = HR * c + r
                            last = pe.matmul(bank("o", u)[:, h * HD:(h + 1) * HD], Wt[:, r, c, :],
                                             vt[:, u, h * HD:(h + 1) * HD], start=True, stop=True)
                    fill(last, "o", u)
                u = t - LAG_T4
                if 0 <= u < NT:
                    pe.wait_ge(xn_ready[2], u + 1)
                    transposes("T4", u, xn[:, u, :])
                    claim(pe, "wo2", u)
                    taken(pe, "T4", u)
                    pe.wait_ge(woT_in, 16)
                    fill(product(bank("wo2", u), [(xnT[:, k, u * P:(u + 1) * P], woT2[:, k, :]) for k in range(KD)]),
                         "wo2", u)
                u = t - LAG_T5
                if 0 <= u < NT:
                    pe.wait_ge(xn_ready[3], u + 1)
                    transposes("T5", u, xn[:, u, :])
                    claim(pe, "logit", u)
                    taken(pe, "T5", u)
                    fill(product(bank("logit", u)[:, 0:E],
                                 [(xnT[:, k, u * P:(u + 1) * P], gw[:, k, :]) for k in range(KD)]), "logit", u)

            pe.wait_ge(sel_ready, 1)
            rows = selm[:].rearrange("p t e -> p (t e)")
            for key, m in (("prefix", before), ("total", ones)):
                claim(pe, key)
                fill(product(bank(key)[:, 0:NT * E], [(m[:], rows)]), key)
            pe.wait_ge(comb_ready, 1)
            for half in range(2):
                claim(pe, "combT", half)
                for j in range(4):
                    last = pe.transpose(bank("combT", half)[0:E, j * P:(j + 1) * P], comb[:, 4 * half + j, :],
                                        ident[:])
                fill(last, "combT", half)
            for t in range(NT):
                claim(pe, "b2", t)
                taken(pe, "combT", t // 4)
                fill(product(bank("b2", t), [(combT[:, t * P:(t + 1) * P], b2_sb[:])]), "b2", t)

            for t in range(NT):
                taken(pe, "b2", t)

            def turn_x():
                for k in range(KD):
                    last = pe.transpose(ps[:, 1, k * P:(k + 1) * P], xrow[:, k * P:(k + 1) * P], ident[:])
                last.then_inc(x_turned, 1)

            def expert_tile(u, i, loads):
                pe.wait_ge(w1_in[u], loads)
                pe.wait_ge(xT_ready, i + 1)
                for g in range(KF // 4):
                    for j in range(4):
                        f = 4 * g + j
                        last = product(ps[:, 4 + g, j * P:(j + 1) * P],
                                       [(W1[u][:, k, f * P:(f + 1) * P], xT[:, k, :]) for k in range(KD)])
                    last.then_inc(up_done, 1)
                pe.wait_ge(xrow_in, i * 16 + 32)
                turn_x()
                pe.wait_ge(w2e_in[u], loads)
                pe.wait_ge(y_evac, i + 1)
                for f in range(KF):
                    if f % 4 == 0:
                        pe.wait_ge(gelu_done, i * (KF // 4) + (f // 4 + 1))
                    last = pe.matmul(ps[:, 0, :], hT[:, f, :], W2[u][:, f, :], start=(f == 0), stop=(f == KF - 1))
                last.then_inc(down_done, 1)

            pe.wait_ge(bounds_ready, 1)
            pe.wait_ge(xrow_in, 16)
            turn_x()
            with pe.Fori(0, E // 2) as p:
                for u in range(2):
                    first = pe.value_load(bounds[0:1, bass.ds(2 * p + u, 1)], min_val=0, max_val=MAX_TILES - 1)
                    end = pe.value_load(bounds[0:1, bass.ds(2 * p + u + 1, 1)], min_val=1, max_val=MAX_TILES)
                    with pe.Fori(first, end) as i:
                        expert_tile(u, i, p * 16 + 16)


_INS = ["x", "ctxT", "xWq", "xWk", "xWv", "xWo", "xbo", "aWqT", "aWkT", "aWvT", "aWfT", "aWg1T", "aWg2T",
        "a_ln_w", "aWoT", "gate_w", "w1", "b1T", "w2", "b2"]


def kernel(**inputs):
    import numpy as np
    import concourse.bacc as bacc
    from concourse.bass_utils import run_bass_kernel_spmd

    g = {k: np.asarray(v) for k, v in inputs.items()}
    B, S, D = g["x"].shape
    E, _, F = g["L0_ffn_w1"].shape
    host = {
        "x": g["x"].reshape(B * S, D),
        "ctxT": g["ctx_768"].transpose(0, 2, 1),
        "xWq": g["L0_xattn_Wq"], "xWk": g["L0_xattn_Wk"], "xWv": g["L0_xattn_Wv"], "xWo": g["L0_xattn_Wo"],
        "xbo": g["L0_xattn_bo"].reshape(1, D),
        "aWqT": g["L0_attn_Wq"].T, "aWkT": g["L0_attn_Wk"].T, "aWvT": g["L0_attn_Wv"].T,
        "aWfT": g["L0_attn_Wf"].T, "aWg1T": g["L0_attn_Wg1"].T, "aWg2T": g["L0_attn_Wg2"].T,
        "a_ln_w": g["L0_attn_ln_w"].reshape(1, D), "aWoT": g["L0_attn_Wo"].T,
        "gate_w": g["L0_ffn_gate_w"], "w1": g["L0_ffn_w1"],
        "b1T": g["L0_ffn_b1"].reshape(E, F // 128, 128).transpose(2, 0, 1),
        "w2": g["L0_ffn_w2"], "b2": g["L0_ffn_b2"],
    }
    nc = bacc.Bacc("TRN2", target_bir_lowering=False, num_devices=1)
    arrays, args = {}, []
    for name in _INS:
        a = np.ascontiguousarray(host[name])
        arrays[f"in_{name}"] = a
        args.append(nc.dram_tensor(f"in_{name}", a.shape, mybir.dt.from_np(a.dtype), kind="ExternalInput").ap())
    fp32 = mybir.dt.float32
    args.append(nc.dram_tensor("out_rows", (B * S, D), fp32, kind="ExternalOutput").ap())
    rows = (2 * B * S // 128 + E) * 128
    args.append(nc.dram_tensor("slots", (rows, D), fp32, kind="Internal").ap())
    perceiver_layer(nc, *args)
    r = run_bass_kernel_spmd(nc, [arrays], core_ids=[0])
    return r.results[0]["out_rows"].reshape(B, S, D)
```

```python
import concourse.bass as bass
from concourse import mybir
from contextlib import ExitStack


def perceiver_layer(
    nc: bass.Bass,
    x: bass.AP,
    ctxT: bass.AP,
    xWq: bass.AP,
    xWk: bass.AP,
    xWv: bass.AP,
    xWo: bass.AP,
    xbo: bass.AP,
    aWqT: bass.AP,
    aWkT: bass.AP,
    aWvT: bass.AP,
    aWfT: bass.AP,
    aWg1T: bass.AP,
    aWg2T: bass.AP,
    a_ln_w: bass.AP,
    aWoT: bass.AP,
    gate_w: bass.AP,
    w1: bass.AP,
    b1T: bass.AP,
    w2: bass.AP,
    b2: bass.AP,
    out: bass.AP,
    slots: bass.AP,
):
    fp32 = mybir.dt.float32
    fp32r = mybir.dt.float32r
    i32 = mybir.dt.int32
    u32 = mybir.dt.uint32
    ALU = mybir.AluOpType
    ACT = mybir.ActivationFunctionType
    AX = mybir.AxisListType

    P = 128
    D = x.shape[1]
    NT = x.shape[0] // P
    KD = D // P
    NB, C, L = ctxT.shape
    S = x.shape[0] // NB
    KC = C // P
    LC = L // P
    XH = 8
    DH = D // XH
    PAIRS = XH // 2
    SCALE = DH ** -0.5
    H = 16
    HD = D // H
    HR = P // HD
    E, _, F = w1.shape
    KF = F // P
    MAX_TILES = 2 * NT + E - 1
    EPS = 1e-5
    KB = 1024
    BASE = 16512

    ctx = ExitStack()
    with ctx:
        used = [0]
        ctx.enter_context(nc.sbuf_tensor("arena", [P, 52000], fp32))

        def at(name, shape, offset, dt=fp32):
            return nc.alloc_sbuf_tensor_at(name, shape, dt, offset=BASE + offset)

        def const(name, shape, dt=fp32):
            n = 4
            for s in shape[1:]:
                n *= s
            n = (n + 31) // 32 * 32
            h = at(name, shape, 192 * KB + used[0], dt)
            used[0] += n
            return h

        def sem(name):
            return ctx.enter_context(nc.semaphore(name))

        xs = at("xs", [P, NT, D], 144 * KB)
        xn = at("xn", [P, NT, D], 160 * KB)
        xnT = at("xnT", [P, KD, NT * P], 176 * KB)
        ident = const("ident", [P, P])
        causal = const("causal", [P, P])
        after = const("after", [P, P])
        before = const("before", [P, P])
        ones = const("ones", [P, P])
        bo_rows = const("bo_rows", [P, D])
        lnw_rows = const("lnw_rows", [P, D])
        gw = const("gw", [P, KD, E])
        wf = const("wf", [P, KD, H])
        stats = const("stats", [P, 2, 6])
        mv = const("mv", [P, 4, NT, 2])
        vare = const("vare", [P, 4, NT])
        rstd = const("rstd", [P, 4, NT])
        mhalf = const("mhalf", [P, H])
        rowmax = const("rowmax", [P, PAIRS])
        negmax = const("negmax", [P, PAIRS])
        rowsum = const("rowsum", [P, PAIRS])
        rowinv = const("rowinv", [P, PAIRS])
        zf = const("zf", [P, NT, H])
        fa = const("fa", [P, NT, H])
        fb = const("fb", [P, NT, H])
        ksum = const("ksum", [P, 2, H])
        knorm = const("knorm", [P, 2, H])
        logit = const("logit", [P, NT, E])
        tcount = const("tcount", [P, E])
        tstart = const("tstart", [P, E + 1])
        bounds = const("bounds", [P, 16], i32)
        wgt = const("wgt", [P, 2, NT])
        slot_u = const("slot_u", [P, 2, NT], u32)
        b1_sb = const("b1_sb", [P, E, KF])
        b2_sb = const("b2_sb", [E, D])
        zeros = const("zeros", [P, D])
        lower = const("lower", [P, E, E])
        steps = const("steps", [P, NT])
        assert used[0] <= 15 * KB + 800, used[0]

        OT = at("OT", [P, PAIRS, NT * P], 0)
        qbd = [[at(f"qbd{u}{part}", [P, PAIRS, P], (16 + 4 * u + 2 * n) * KB, fp32r)
                for n, part in enumerate("hl")] for u in range(2)]
        wk1 = [at(f"wk1{part}", [P, KC, D], (24 + 6 * n) * KB, fp32r) for n, part in enumerate("hl")]
        wv1 = [at(f"wv1{part}", [P, KC, D], (36 + 6 * n) * KB, fp32r) for n, part in enumerate("hl")]
        craw = at("craw", [P, KC, L], 48 * KB)
        cT = [[at(f"cT{u}{part}", [P, KC, L], (54 + 12 * u + 6 * n) * KB, fp32r)
               for n, part in enumerate("hl")] for u in range(2)]
        KT = [at(f"KT{part}", [P, PAIRS, L], (78 + 8 * n) * KB, fp32r) for n, part in enumerate("hl")]
        V = [at(f"V{u}", [P, LC, D], (94 + 8 * u) * KB) for u in range(2)]
        prob = at("prob", [P, PAIRS, L], 126 * KB)
        PT = [at(f"PT{u}", [P, LC, P], (134 + 2 * u) * KB) for u in range(2)]
        qT1 = at("qT1", [P, PAIRS, NT * P], 160 * KB)
        wq1 = at("wq1", [P, KD, D], 78 * KB)
        wkr = at("wkr", [P, KC, D], 110 * KB)
        wvr = at("wvr", [P, KC, D], 116 * KB)
        wo1 = at("wo1", [P, KD, D], 54 * KB)
        wqT2 = at("wqT2", [P, KD, D], 24 * KB)
        wkT2 = at("wkT2", [P, KD, D], 32 * KB)
        wvT2 = at("wvT2", [P, KD, D], 40 * KB)
        wg1 = at("wg1", [P, KD, 32], 48 * KB)
        wg2 = at("wg2", [32, D], 49 * KB)
        ksil = at("ksil", [P, NT, D], 0)
        t1T = at("t1T", [32, NT * P], 51 * KB)
        Mf = at("Mf", [P, HR, HR, P], 55 * KB)
        ksq = at("ksq", [P, D], 128 * KB)
        qT2 = at("qT2", [P, KD, NT * P], 64 * KB)
        kT2 = at("kT2", [P, KD, NT * P], 80 * KB)
        vt = at("vt", [P, NT, D], 96 * KB)
        dec = [at(f"dec{u}", [P, HR, HR, P], (112 + 8 * u) * KB) for u in range(2)]
        Wt = at("Wt", [P, HR, HR, P], 128 * KB)
        woT2 = at("woT2", [P, KD, D], 136 * KB)
        W1 = [at(f"W1_{u}", [P, KD, F], 64 * u * KB) for u in range(2)]
        W2 = [at(f"W2_{u}", [P, KF, D], (64 * u + 32) * KB) for u in range(2)]
        hT = at("hT", [P, KF, P], 176 * KB)
        xT = at("xT", [P, KD, P], 184 * KB)
        combT = at("combT", [E, NT * P], 128 * KB)
        yg = at("yg", [P, NT, 2, D], 0)
        xin = at("xin", [P, 2, D], 188 * KB)
        xrow = at("xrow", [P, D], 142 * KB)
        yrow = at("yrow", [P, 2, D], 132 * KB)
        cmp = at("cmp", [P, NT, E, E], 134 * KB)
        tie = at("tie", [P, NT, E, E], 136 * KB)
        rank = at("rank", [P, NT, E], 138 * KB + 512)
        m0 = at("m0", [P, NT, E], 138 * KB + 768)
        m1 = at("m1", [P, NT, E], 139 * KB)
        selm = at("selm", [P, NT, E], 139 * KB + 256)
        posn = at("posn", [P, NT, E], 139 * KB + 512)
        tsum = at("tsum", [P, NT, E], 139 * KB + 768)
        comb = at("comb", [P, NT, E], 140 * KB)
        lv = at("lv", [P, 2, NT], 140 * KB + 256)
        slotf = at("slotf", [P, 2, NT], 140 * KB + 384)
        ge = at("ge", [P, E, NT], 140 * KB + 576)

        ps = ctx.enter_context(nc.psum_tensor("ps", [P, 8, 512], fp32))

        filled = [sem(f"bank{b}_filled") for b in range(8)]
        emptied = [sem(f"bank{b}_emptied") for b in range(8)]
        plan = {}

        def place(*key):
            plan[key] = (len(plan) % 8, len(plan) // 8)

        def bank(*key):
            return ps[:, plan[key][0], :]

        def claim(pe, *key):
            b, n = plan[key]
            if n:
                pe.wait_ge(emptied[b], n)

        def fill(ins, *key):
            ins.then_inc(filled[plan[key][0]], 1)

        def arrive(eng, *key):
            b, n = plan[key]
            eng.wait_ge(filled[b], n + 1)

        def empty(ins, *key):
            ins.then_inc(emptied[plan[key][0]], 1)

        def taken(eng, *key):
            b, n = plan[key]
            eng.wait_ge(emptied[b], n + 1)

        for t in range(NT):
            place("T1", t)
        for half in range(2):
            for c in range(PAIRS):
                place("q1", half, c)
        RING1 = len(plan)
        for t in range(NT + 2):
            if t < NT:
                place("wo1", t)
            if t >= 2:
                place("T2", t - 2)
        for t in range(NT):
            place("z", t)
        for half in range(2):
            place("t1", half)
        for t in range(NT):
            for what in ("k", "v", "q"):
                place(what, t)
        for t in range(NT):
            place("gate", t)
            place("kT", t)
        LAG_O, LAG_T4, LAG_W, LAG_T5, LAG_R = 1, 2, 2, 4, 4
        for t in range(NT + LAG_R):
            if t < NT:
                for r in range(HR):
                    place("seg", t, r)
                    place("A", t, r)
            if 0 <= t - LAG_O < NT:
                place("o", t - LAG_O)
            if 0 <= t - LAG_T4 < NT:
                place("T4", t - LAG_T4)
                place("wo2", t - LAG_W)
            if 0 <= t - LAG_T5 < NT:
                place("T5", t - LAG_T5)
                place("logit", t - LAG_R)
        place("prefix")
        place("total")
        place("combT", 0)
        place("combT", 1)
        for t in range(NT):
            place("b2", t)
        RING_ALL = len(plan)

        x_in = sem("x_in")
        w_in = sem("w_in")
        w2_in = sem("w2_in")
        woT_in = sem("woT_in")
        consts_ready = sem("consts_ready")
        pool_own = sem("pool_own")
        dve_own = sem("dve_own")
        var_ready = [sem(f"var_ready{k}") for k in range(4)]
        rstd_ready = [sem(f"rstd_ready{k}") for k in range(4)]
        xn_ready = [sem(f"xn_ready{k}") for k in range(4)]
        xnT_ready = [sem(f"xnT_ready{k}") for k in range(4)]
        ctx_in = sem("ctx_in")
        wo_in = sem("wo_in")
        w_hi = sem("w_hi")
        w_split = sem("w_split")
        c_hi = sem("c_hi")
        c_split = sem("c_split")
        k_hi = sem("k_hi")
        q_hi = sem("q_hi")
        v_proj = sem("v_proj")
        k_proj = sem("k_proj")
        k_split = sem("k_split")
        v_evac = sem("v_evac")
        qbd_ready = sem("qbd_ready")
        scores = sem("scores")
        raw_max = sem("raw_max")
        neg_max = sem("neg_max")
        exp_done = sem("exp_done")
        inv_done = sem("inv_done")
        norm_done = sem("norm_done")
        pt_done = sem("pt_done")
        pt_evac = sem("pt_evac")
        pv_done = sem("pv_done")
        o_evac = sem("o_evac")
        bo_added = sem("bo_added")
        k_ready = sem("k_ready")
        knorm_in = sem("knorm_in")
        v_ready = sem("v_ready")
        v_scaled = sem("v_scaled")
        q_ready = sem("q_ready")
        f_ready = sem("f_ready")
        f_exp = sem("f_exp")
        f_in = sem("f_in")
        f_ln = sem("f_ln")
        Mf_ready = sem("Mf_ready")
        dec_ready = sem("dec_ready")
        sel_ready = sem("sel_ready")
        p01 = sem("p01")
        e01 = sem("e01")
        comb_ready = sem("comb_ready")
        bounds_ready = sem("bounds_ready")
        slots_ready = sem("slots_ready")
        zero_sent = sem("zero_sent")
        scattered = sem("scattered")
        xin_in = sem("xin_in")
        x_copied = sem("x_copied")
        xT_ready = sem("xT_ready")
        up_done = sem("up_done")
        gelu_done = sem("gelu_done")
        down_done = sem("down_done")
        y_sent = sem("y_sent")
        g_in = [sem(f"g_in{t}") for t in range(NT)]
        x_turned = sem("x_turned")
        y_evac = sem("y_evac")
        yrow_free = sem("yrow_free")
        w1_in = [sem(f"w1_in{u}") for u in range(2)]
        w2e_in = [sem(f"w2e_in{u}") for u in range(2)]
        out_ready = sem("out_ready")
        out_sent = sem("out_sent")

        def wait(eng, s, v):
            if not (isinstance(v, int) and v <= 0):
                eng.wait_ge(s, v)

        block = ctx.enter_context(nc.Block())
        blk = lambda w, k: w.rearrange("(k p) n -> p k n", p=P)

        @block.sync
        def _(sp):
            for t in range(NT):
                sp.dma_start(xs[:, t, :], x[t * P:(t + 1) * P, :]).then_inc(x_in, 16)
            sp.dma_start(wq1[:], blk(xWq, KD)).then_inc(w_in, 16)
            sp.dma_start(wkr[:], blk(xWk, KC)).then_inc(w_in, 16)
            sp.dma_start(wvr[:], blk(xWv, KC)).then_inc(w_in, 16)
            sp.dma_start(bo_rows[:], xbo.to_broadcast([P, D])).then_inc(w_in, 16)
            sp.dma_start(craw[:], ctxT[0].rearrange("(k p) l -> p k l", p=P)).then_inc(ctx_in, 16)
            for dst, src in ((wf, aWfT), (gw, gate_w)):
                sp.dma_start(dst[:], src.rearrange("(k p) n -> p k n", p=P)).then_inc(w2_in, 16)
            sp.dma_start(lnw_rows[:], a_ln_w.to_broadcast([P, D])).then_inc(w2_in, 16)
            sp.dma_start(b1_sb[:], b1T).then_inc(w2_in, 16)
            sp.dma_start(b2_sb[:], b2).then_inc(w2_in, 16)
            sp.wait_ge(consts_ready, 2)
            sp.dma_start(slots.rearrange("(t p) n -> p t n", p=P),
                         zeros[:].unsqueeze(1).to_broadcast([P, slots.shape[0] // P, D])).then_inc(zero_sent, 16)
            with sp.Fori(1, NB) as b:
                sp.wait_ge(c_split, b)
                sp.dma_start(craw[:], ctxT[bass.ds(b, 1)].rearrange("b (k p) l -> p (b k) l", p=P)
                             ).then_inc(ctx_in, 16)
            sp.wait_ge(v_proj, (NB - 1) * LC)
            sp.dma_start(wo1[:], blk(xWo, KD)).then_inc(wo_in, 16)
            sp.wait_ge(v_proj, NB * LC)
            for dst, src in ((wqT2, aWqT), (wkT2, aWkT), (wvT2, aWvT), (wg1, aWg1T)):
                sp.dma_start(dst[:], src.rearrange("(k p) n -> p k n", p=P)).then_inc(w2_in, 16)
            sp.dma_start(wg2[:], aWg2T).then_inc(w2_in, 16)
            sp.wait_ge(o_evac, NB)
            sp.dma_start(woT2[:], blk(aWoT, KD)).then_inc(woT_in, 16)
            w1e = w1.rearrange("e (k p) f -> e p k f", p=P)
            w2e = w2.rearrange("e (k p) d -> e p k d", p=P)
            arrive(sp, "kT", NT - 1)
            sp.dma_start(W1[0][:], w1e[0]).then_inc(w1_in[0], 16)
            arrive(sp, "seg", NT - 1, HR - 1)
            sp.dma_start(W2[0][:], w2e[0]).then_inc(w2e_in[0], 16)
            arrive(sp, "A", NT - 1, HR - 1)
            sp.dma_start(W1[1][:], w1e[1]).then_inc(w1_in[1], 16)
            arrive(sp, "o", NT - 1)
            sp.dma_start(W2[1][:], w2e[1]).then_inc(w2e_in[1], 16)
            sp.wait_ge(bounds_ready, 1)
            with sp.Fori(1, E // 2) as p:
                for u in range(2):
                    end = sp.value_load(bounds[0:1, bass.ds(2 * p + u - 1, 1)], min_val=1, max_val=MAX_TILES)
                    sp.wait_ge(down_done, end)
                    sp.dma_start(W1[u][:], w1e[bass.ds(2 * p + u, 1)].rearrange("e p k f -> p (e k) f")
                                 ).then_inc(w1_in[u], 16)
                    sp.dma_start(W2[u][:], w2e[bass.ds(2 * p + u, 1)].rearrange("e p k f -> p (e k) f")
                                 ).then_inc(w2e_in[u], 16)
            for t in range(NT):
                sp.wait_ge(out_ready, t + 1)
                sp.dma_start(out[t * P:(t + 1) * P, :], xs[:, t, :]).then_inc(out_sent, 16)
            sp.wait_ge(out_sent, 16 * NT)

        @block.gpsimd
        def _(pool):
            own = [0]

            def link(ins):
                own[0] += 1
                ins.then_inc(pool_own, 1)
                pool.wait_ge(pool_own, own[0])

            def select(m, pattern, cm, op, base=0, fill=0.0):
                return pool.affine_select(out=m, in_=m, compare_op=op, fill=fill, base=base,
                                          pattern=pattern, channel_multiplier=cm)

            pool.memset(mhalf[:], -0.5).then_inc(consts_ready, 1)
            link(pool.memset(ident[:], 0.0))
            link(select(ident[:], [[-1, P]], 1, ALU.not_equal, fill=1.0))
            for m in (causal, after, before):
                link(pool.memset(m[:], 1.0))
            link(select(causal[:], [[1, P]], -1, ALU.is_ge))
            link(select(after[:], [[-1, P]], 1, ALU.is_gt))
            link(select(before[:], [[1, P]], -1, ALU.is_gt))
            link(pool.memset(causal[0:S, S:P], 0.0))
            link(pool.memset(after[S:P, 0:S], 0.0))
            for u in range(2):
                for part in range(2):
                    link(pool.memset(qbd[u][part][:].bitcast(fp32), 0.0))
            link(pool.memset(zeros[:], 0.0))
            link(pool.memset(lower[:], 1.0))
            link(select(lower[:], [[1, E], [-1, E]], 0, ALU.is_gt))
            for m in range(NT):
                link(pool.memset(steps[:, m:m + 1], float(P * m + 1)))
            pool.memset(ones[:], 1.0).then_inc(consts_ready, 1)
            pool.wait_ge(consts_ready, 2)

            def powers(kind, t, n=1):
                pool.wait_ge(var_ready[kind], t + n)
                pool.tensor_tensor(rstd[:, kind, t:t + n], vare[:, kind, t:t + n], mhalf[:, 0:n], ALU.pow
                                   ).then_inc(rstd_ready[kind], n)

            for t in range(NT):
                powers(0, t)

            pool.wait_ge(w_in, 4 * 16)
            for raw, (hi, lo) in ((wkr, wk1), (wvr, wv1)):
                pool.tensor_copy(hi[:], raw[:]).then_inc(w_hi, 1)
                pool.wait_ge(w_hi, 1 if raw is wkr else 2)
                pool.tensor_tensor(lo[:], raw[:], hi[:].bitcast(fp32), ALU.subtract).then_inc(w_split, 1)

            def split_context(b, u):
                pool.wait_ge(ctx_in, 16 * (b + 1))
                wait(pool, v_proj, LC * (b - 1))
                pool.tensor_tensor(cT[u][0][:], craw[:], ones[:, 0:1].unsqueeze(2).to_broadcast([P, KC, L]), ALU.mult
                                   ).then_inc(c_hi, 1)
                pool.wait_ge(c_hi, b + 1)
                pool.tensor_tensor(cT[u][1][:], craw[:], cT[u][0][:].bitcast(fp32), ALU.subtract
                                   ).then_inc(c_split, 1)

            split_context(0, 0)
            split_context(1, 1)
            pool.wait_ge(w_in, 4 * 16)
            for t in range(NT):
                pool.wait_ge(xn_ready[0], t + 1)
                pool.tensor_tensor(xs[:, t, :], xs[:, t, :], bo_rows[:], ALU.add).then_inc(bo_added, 1)

            def normalise(b):
                for c in range(PAIRS):
                    pool.wait_ge(inv_done, PAIRS * b + c + 1)
                    pool.tensor_tensor(prob[:, c, :], prob[:, c, :], rowinv[:, c:c + 1].to_broadcast([P, L]), ALU.mult
                                       ).then_inc(norm_done, 1)

            for b in range(2):
                normalise(b)
                split_context(b + 2, b)
            with pool.Fori(1, NB // 2 - 1) as p:
                for u in range(2):
                    normalise(2 * p + u)
                    split_context(2 * p + u + 2, u)
            normalise(NB - 2)
            normalise(NB - 1)

            for t in range(NT):
                powers(1, t)
            for t in range(NT):
                pool.wait_ge(knorm_in, t + 1)
                if t:
                    pool.wait_ge(v_scaled, t)
                link(pool.tensor_tensor(knorm[:, t % 2, :], ksum[:, t % 2, :], mhalf[:], ALU.pow))
                taken(pool, "v", t)
                v3 = vt[:, t, :].rearrange("p (h d) -> p h d", d=HD)
                pool.tensor_tensor(v3, v3, knorm[:, t % 2, :].unsqueeze(2).to_broadcast([P, H, HD]), ALU.mult
                                   ).then_inc(v_scaled, 1)

            def masked_f(t):
                fv = fa[:, t, :].rearrange("p (c r) -> p r c", r=HR)
                for r in range(HR):
                    if t:
                        arrive(pool, "seg", t - 1, r)
                    pool.tensor_tensor(Mf[:, r], after[:].unsqueeze(1).to_broadcast([P, HR, P]),
                                       fv[:, r, :].unsqueeze(2).to_broadcast([P, HR, P]), ALU.mult
                                       ).then_inc(Mf_ready, 1)

            def mask_decay(t):
                for r in range(HR):
                    taken(pool, "seg", t, r)
                    pool.tensor_tensor(dec[t % 2][:, r], dec[t % 2][:, r],
                                       causal[:].unsqueeze(1).to_broadcast([P, HR, P]), ALU.mult
                                       ).then_inc(dec_ready, 1)

            pool.wait_ge(f_ready, 1)
            masked_f(0)
            for t in range(NT + LAG_R):
                if t < NT:
                    mask_decay(t)
                if t + 1 < NT:
                    masked_f(t + 1)
                if 0 <= t - 1 < NT:
                    powers(2, t - 1)
                if 0 <= t - 2 < NT:
                    powers(3, t - 2)

            pool.wait_ge(slots_ready, 1)
            pool.wait_ge(zero_sent, 16)
            for t in range(NT):
                for k in range(2):
                    pool.indirect_dma_start(
                        out=slots, out_offset=bass.IndirectOffsetOnAxis(ap=slot_u[:, k, t:t + 1], axis=0),
                        in_=xn[:, t, :], in_offset=None).then_inc(scattered, 16)
            pool.wait_ge(scattered, 16 * 2 * NT)
            total = pool.value_load(bounds[0:1, E:E + 1], min_val=E, max_val=MAX_TILES)
            taken(pool, "T5", NT - 1)
            arrive(pool, "logit", NT - 1)
            for n in range(2):
                pool.dma_start(xin[:, n, :], slots[n * P:(n + 1) * P, :]).then_inc(xin_in, 16)
                pool.wait_ge(xin_in, 16 * (n + 1))
            with pool.Fori(0, total) as i:
                pool.wait_ge(x_copied, i + 1)
                pool.dma_start(xin[:, bass.ds(i % 2, 1), :], slots[bass.ds((i + 2) * P, P), :]
                               ).then_inc(xin_in, 16)
                pool.wait_ge(y_evac, i + 2)
                pool.dma_start(slots[bass.ds(i * P, P), :], yrow[:, bass.ds(i % 2, 1), :]).then_inc(y_sent, 16)
                pool.wait_ge(xin_in, i * 16 + 48)
                pool.wait_ge(y_sent, i * 16 + 16)
                pool.sem_inc(yrow_free, 1)
            for t in range(NT):
                for k in range(2):
                    pool.indirect_dma_start(
                        out=yg[:, t, k, :], out_offset=None,
                        in_=slots, in_offset=bass.IndirectOffsetOnAxis(ap=slot_u[:, k, t:t + 1], axis=0)
                    ).then_inc(g_in[t], 16)

        @block.scalar
        def _(act):
            def copy(dst, src):
                return act.activation(dst, src, ACT.Copy)

            def q_half(half):
                for c in range(PAIRS):
                    arrive(act, "q1", half, c)
                    n = copy(qT1[:, c, half * 512:(half + 1) * 512], bank("q1", half, c))
                    empty(n, "q1", half, c)

            for t in range(NT):
                arrive(act, "T1", t)
                n = copy(xnT[:, :, t * P:(t + 1) * P], bank("T1", t).rearrange("p (k n) -> p k n", k=KD))
                empty(n, "T1", t)
            q_half(0)
            q_half(1)

            def high_k(b, c):
                act.wait_ge(k_proj, PAIRS * b + c + 1)
                copy(KT[0][:, c, :], ps[:, 4 + c % 2, :]).then_inc(k_hi, 1)

            def evac_v(b, u, c):
                act.wait_ge(v_proj, LC * b + c + 1)
                copy(V[u][:, c, :], ps[:, 4 + c % 2, :]).then_inc(v_evac, 1)

            def exps(b, c):
                act.wait_ge(neg_max, PAIRS * b + c + 1)
                wait(act, pt_done, PAIRS * (b - 1) + c + 1)
                act.activation(prob[:, c, :], ps[:, c, :], ACT.Exp, bias=negmax[:, c:c + 1], scale=SCALE,
                               accum_out=rowsum[:, c:c + 1]).then_inc(exp_done, 1)

            def batch(b, u, more=True):
                for c in range(PAIRS):
                    exps(b, c)
                    if more and c >= 1:
                        high_k(b + 1, c - 1)
                if more:
                    high_k(b + 1, PAIRS - 1)
                for c in range(LC):
                    if more:
                        evac_v(b + 1, 1 - u, c)

            for c in range(PAIRS):
                high_k(0, c)
            for c in range(LC):
                evac_v(0, 0, c)
            batch(0, 0)
            batch(1, 1)
            with act.Fori(1, NB // 2 - 1) as p:
                for u in range(2):
                    batch(2 * p + u, u)
            batch(NB - 2, 0)
            batch(NB - 1, 1, more=False)

            for t in range(NT):
                arrive(act, "T2", t)
                n = copy(xnT[:, :, t * P:(t + 1) * P], bank("T2", t).rearrange("p (k n) -> p k n", k=KD))
                empty(n, "T2", t)
            for half in range(2):
                arrive(act, "t1", half)
                n = copy(t1T[:, half * 512:(half + 1) * 512], bank("t1", half)[0:32, :])
                empty(n, "t1", half)
            for t in range(NT):
                for what, dst, ready in (("k", ksil[:, t, :], k_ready), ("v", vt[:, t, :], v_ready),
                                         ("q", qT2[:, :, t * P:(t + 1) * P], q_ready)):
                    arrive(act, what, t)
                    src = bank(what, t)
                    if what == "q":
                        src = src.rearrange("p (k n) -> p k n", k=KD)
                    n = act.activation(dst, src, ACT.Silu)
                    empty(n, what, t)
            for t in range(NT):
                arrive(act, "gate", t)
                n = act.activation(xn[:, t, :], bank("gate", t), ACT.Sigmoid)
                empty(n, "gate", t)
            act.wait_ge(f_in, 1)
            act.activation(fa[:], fa[:], ACT.Exp).then_inc(f_exp, 1)
            act.wait_ge(f_exp, 1)
            act.activation(fa[:], fa[:], ACT.Ln, bias=1.0).then_inc(f_ln, 1)
            for t in range(NT + LAG_R):
                if t < NT:
                    for r in range(HR):
                        arrive(act, "seg", t, r)
                        if t >= 2:
                            taken(act, "A", t - 2, r)
                        n = act.activation(dec[t % 2][:, r], bank("seg", t, r).rearrange("p (c s) -> p c s", s=P),
                                           ACT.Exp)
                        empty(n, "seg", t, r)
                u = t - LAG_T4
                if 0 <= u < NT:
                    arrive(act, "T4", u)
                    n = copy(xnT[:, :, u * P:(u + 1) * P], bank("T4", u).rearrange("p (k n) -> p k n", k=KD))
                    empty(n, "T4", u)
                u = t - LAG_T5
                if 0 <= u < NT:
                    arrive(act, "T5", u)
                    n = copy(xnT[:, :, u * P:(u + 1) * P], bank("T5", u).rearrange("p (k n) -> p k n", k=KD))
                    empty(n, "T5", u)

            act.wait_ge(p01, 1)
            act.activation(wgt[:, 1, :], lv[:, 0, :], ACT.Exp).then_inc(e01, 1)
            act.wait_ge(bounds_ready, 1)
            act.wait_ge(w2_in, 10 * 16)
            with act.Fori(0, E) as e:
                first = act.value_load(bounds[0:1, bass.ds(e, 1)], min_val=0, max_val=MAX_TILES - 1)
                end = act.value_load(bounds[0:1, bass.ds(e + 1, 1)], min_val=1, max_val=MAX_TILES)
                with act.Fori(first, end) as i:
                    for g in range(KF // 4):
                        act.wait_ge(up_done, i * (KF // 4) + (g + 1))
                        for j in range(4):
                            f = 4 * g + j
                            last = act.activation(hT[:, f, :], ps[:, 4 + g, j * P:(j + 1) * P], ACT.Gelu,
                                                  bias=b1_sb[:, bass.ds(e, 1), f])
                        last.then_inc(gelu_done, 1)

        @block.vector
        def _(dve):
            own = [0]

            def link(ins):
                own[0] += 1
                ins.then_inc(dve_own, 1)
                dve.wait_ge(dve_own, own[0])

            def spread(kind, t, src):
                link(dve.bn_stats(stats[:, 0, :], src))
                link(dve.bn_aggr(mv[:, kind, t, :], stats[:, 0, :]))
                dve.tensor_scalar(vare[:, kind, t:t + 1], mv[:, kind, t, 1:2], EPS, None, ALU.add
                                  ).then_inc(var_ready[kind], 1)

            def centre(kind, t, src):
                dve.wait_ge(rstd_ready[kind], t + 1)
                return dve.tensor_scalar(xn[:, t, :], src, mv[:, kind, t, 0:1], rstd[:, kind, t:t + 1],
                                         ALU.subtract, ALU.mult)

            dve.wait_ge(consts_ready, 1)
            for t in range(NT + 1):
                if t < NT:
                    dve.wait_ge(x_in, 16 * NT)
                    spread(0, t, xs[:, t, :])
                if t:
                    centre(0, t - 1, xs[:, t - 1, :]).then_inc(xn_ready[0], 1)

            def maxes(b):
                for c in range(PAIRS):
                    dve.wait_ge(scores, PAIRS * b + c + 1)
                    dve.reduce_max(rowmax[:, c:c + 1], ps[:, c, :], AX.X).then_inc(raw_max, 1)
                    dve.wait_ge(raw_max, PAIRS * b + c + 1)
                    dve.tensor_scalar(negmax[:, c:c + 1], rowmax[:, c:c + 1], -SCALE, None, ALU.mult
                                      ).then_inc(neg_max, 1)

            def inverse(b, c):
                dve.wait_ge(exp_done, PAIRS * b + c + 1)
                wait(dve, norm_done, PAIRS * (b - 1) + c + 1)
                dve.reciprocal(rowinv[:, c:c + 1], rowsum[:, c:c + 1]).then_inc(inv_done, 1)

            def low(lo, held, hi):
                return dve.tensor_tensor(lo, held, hi.bitcast(fp32), ALU.subtract)

            def low_k(b, c):
                dve.wait_ge(k_hi, PAIRS * b + c + 1)
                low(KT[1][:, c, :], ps[:, 4 + c % 2, :], KT[0][:, c, :]).then_inc(k_split, 1)

            def evac_pt(b, c):
                dve.wait_ge(pt_done, PAIRS * b + c + 1)
                wait(dve, pv_done, PAIRS * b + c - 1)
                dve.tensor_copy(PT[c % 2][:], ps[:, 6, :].rearrange("p (l n) -> p l n", l=LC)
                                ).then_inc(pt_evac, 1)

            def evac_o(b):
                dve.wait_ge(pv_done, PAIRS * (b + 1))
                for g in range(2):
                    h = slice(g * DH, (g + 1) * DH)
                    o = ps[h, 7, :].rearrange("p (c n) -> p c n", c=PAIRS)
                    last = dve.tensor_copy(OT[h, :, bass.ds(b * S, S)], o[:, :, h])
                last.then_inc(o_evac, 1)

            def block_q(b, u):
                wait(dve, scores, PAIRS * (b - 1))
                hi, lo = qbd[u]
                heads = [slice(g * DH, (g + 1) * DH) for g in range(2)]
                for h in heads:
                    last = dve.tensor_copy(hi[h, :, h], qT1[h, :, bass.ds(b * S, S)])
                last.then_inc(q_hi, 1)
                dve.wait_ge(q_hi, b + 1)
                for h in heads:
                    last = low(lo[h, :, h], qT1[h, :, bass.ds(b * S, S)], hi[h, :, h])
                last.then_inc(qbd_ready, 1)

            def batch(b, u, more=True):
                maxes(b)
                for c in range(PAIRS):
                    inverse(b, c)
                    if more:
                        low_k(b + 1, c)
                if more:
                    block_q(b + 1, 1 - u)
                for c in range(LC):
                    evac_pt(b, c)
                evac_o(b)

            for half in range(2):
                for c in range(PAIRS):
                    taken(dve, "q1", half, c)
            block_q(0, 0)
            for c in range(PAIRS):
                low_k(0, c)
            batch(0, 0)
            batch(1, 1)
            with dve.Fori(1, NB // 2 - 1) as p:
                for u in range(2):
                    batch(2 * p + u, u)
            batch(NB - 2, 0)
            batch(NB - 1, 1, more=False)

            for t in range(NT + 1):
                if t < NT:
                    arrive(dve, "wo1", t)
                    dve.wait_ge(bo_added, t + 1)
                    n = dve.tensor_tensor(xs[:, t, :], xs[:, t, :], bank("wo1", t), ALU.add)
                    empty(n, "wo1", t)
                    taken(dve, "wo1", t)
                    spread(1, t, xs[:, t, :])
                if t:
                    centre(1, t - 1, xs[:, t - 1, :]).then_inc(xn_ready[1], 1)
            for t in range(NT):
                arrive(dve, "z", t)
                n = dve.tensor_copy(zf[:, t, :], bank("z", t)[:, 0:H])
                empty(n, "z", t)
            for t in range(NT):
                taken(dve, "z", t)
            link(dve.tensor_scalar(fb[:], zf[:], -1.0, None, ALU.mult))
            dve.tensor_tensor(fa[:], zf[:], fb[:], ALU.min).then_inc(f_in, 1)
            for t in range(NT):
                taken(dve, "k", t)
                link(dve.tensor_tensor(ksq[:], ksil[:, t, :], ksil[:, t, :], ALU.mult))
                if t >= 2:
                    dve.wait_ge(v_scaled, t - 1)
                link(dve.tensor_reduce(ksum[:, t % 2, :], ksq[:].rearrange("p (h d) -> p h d", d=HD), AX.X, ALU.add))
                dve.tensor_scalar(ksum[:, t % 2, :], ksum[:, t % 2, :], 1e-24, None, ALU.max
                                  ).then_inc(knorm_in, 1)
            for t in range(NT):
                arrive(dve, "kT", t)
                n = dve.tensor_copy(kT2[:, :, t * P:(t + 1) * P], bank("kT", t).rearrange("p (k n) -> p k n", k=KD))
                empty(n, "kT", t)
            dve.wait_ge(f_ln, 1)
            link(dve.tensor_scalar(fb[:], zf[:], 0.0, None, ALU.min))
            dve.tensor_tensor(fa[:], fb[:], fa[:], ALU.subtract).then_inc(f_ready, 1)

            for t in range(NT + LAG_R):
                if t < NT:
                    for r in range(HR):
                        arrive(dve, "A", t, r)
                        dve.wait_ge(dec_ready, HR * t + r + 1)
                        if t:
                            arrive(dve, "o", t - 1)
                        n = dve.tensor_tensor(Wt[:, r], bank("A", t, r).rearrange("p (c s) -> p c s", s=P),
                                              dec[t % 2][:, r], ALU.mult)
                        empty(n, "A", t, r)
                u = t - LAG_O
                if 0 <= u < NT:
                    arrive(dve, "o", u)
                    taken(dve, "gate", u)
                    n = dve.tensor_tensor(xn[:, u, :], bank("o", u), xn[:, u, :], ALU.mult)
                    empty(n, "o", u)
                    taken(dve, "o", u)
                    spread(2, u, xn[:, u, :])
                    link(centre(2, u, xn[:, u, :]))
                    dve.wait_ge(w2_in, 10 * 16)
                    dve.tensor_tensor(xn[:, u, :], xn[:, u, :], lnw_rows[:], ALU.mult).then_inc(xn_ready[2], 1)
                u = t - 2
                if 0 <= u < NT:
                    arrive(dve, "wo2", u)
                    n = dve.tensor_tensor(xs[:, u, :], xs[:, u, :], bank("wo2", u), ALU.add)
                    empty(n, "wo2", u)
                    taken(dve, "wo2", u)
                    spread(3, u, xs[:, u, :])
                u = t - 3
                if 0 <= u < NT:
                    centre(3, u, xs[:, u, :]).then_inc(xn_ready[3], 1)
                u = t - LAG_R
                if 0 <= u < NT:
                    arrive(dve, "logit", u)
                    n = dve.tensor_copy(logit[:, u, :], bank("logit", u)[:, 0:E])
                    empty(n, "logit", u)
                    taken(dve, "logit", u)

            bc = [P, NT, E, E]
            Lj, Le = logit[:].unsqueeze(2).to_broadcast(bc), logit[:].unsqueeze(3).to_broadcast(bc)
            dve.tensor_tensor(cmp[:], Lj, Le, ALU.is_gt)
            link(dve.tensor_tensor(tie[:], Lj, Le, ALU.is_equal))
            link(dve.tensor_tensor(tie[:], tie[:], lower[:].unsqueeze(1).to_broadcast(bc), ALU.mult))
            link(dve.tensor_tensor(cmp[:], cmp[:], tie[:], ALU.add))
            link(dve.tensor_reduce(rank[:], cmp[:], AX.X, ALU.add))
            dve.tensor_scalar(selm[:], rank[:], 1.5, None, ALU.is_lt).then_inc(sel_ready, 1)
            dve.tensor_scalar(m0[:], rank[:], 0.0, None, ALU.is_equal)
            link(dve.tensor_scalar(m1[:], rank[:], 1.0, None, ALU.is_equal))
            for k, m in ((0, m0), (1, m1)):
                link(dve.tensor_tensor(comb[:], m[:], logit[:], ALU.mult))
                link(dve.tensor_reduce(lv[:, k, :], comb[:], AX.X, ALU.add))
            dve.tensor_tensor(lv[:, 0, :], lv[:, 1, :], lv[:, 0, :], ALU.subtract).then_inc(p01, 1)
            arrive(dve, "total")
            n = dve.tensor_copy(tsum[:], bank("total")[:, 0:NT * E].rearrange("p (t e) -> p t e", e=E))
            empty(n, "total")
            taken(dve, "total")
            for t in range(1, NT):
                link(dve.tensor_tensor(tsum[:, t, :], tsum[:, t, :], tsum[:, t - 1, :], ALU.add))
            link(dve.tensor_tensor(ge[:], tsum[:, NT - 1, :].unsqueeze(2).to_broadcast([P, E, NT]),
                                   steps[:].unsqueeze(1).to_broadcast([P, E, NT]), ALU.is_ge))
            link(dve.tensor_reduce(tcount[:], ge[:], AX.X, ALU.add))
            link(dve.tensor_scalar(tcount[:], tcount[:], 1.0, None, ALU.max))
            link(dve.memset(tstart[:, 0:1], 0.0))
            for e in range(E):
                link(dve.tensor_tensor(tstart[:, e + 1:e + 2], tstart[:, e:e + 1], tcount[:, e:e + 1], ALU.add))
            dve.tensor_copy(bounds[:, 0:E + 1], tstart[:]).then_inc(bounds_ready, 1)
            arrive(dve, "prefix")
            n = dve.tensor_copy(posn[:], bank("prefix")[:, 0:NT * E].rearrange("p (t e) -> p t e", e=E))
            empty(n, "prefix")
            taken(dve, "prefix")
            link(dve.tensor_tensor(posn[:, 1:NT, :], posn[:, 1:NT, :], tsum[:, 0:NT - 1, :], ALU.add))
            link(dve.scalar_tensor_tensor(posn[:], tstart[:, 0:E].unsqueeze(1).to_broadcast([P, NT, E]), float(P),
                                          posn[:], ALU.mult, ALU.add))
            for k, m in ((0, m0), (1, m1)):
                link(dve.tensor_tensor(comb[:], m[:], posn[:], ALU.mult))
                link(dve.tensor_reduce(slotf[:, k, :], comb[:], AX.X, ALU.add))
            dve.tensor_copy(slot_u[:], slotf[:]).then_inc(slots_ready, 1)
            dve.wait_ge(e01, 1)
            link(dve.tensor_scalar(lv[:, 0, :], wgt[:, 1, :], 1.0, None, ALU.add))
            link(dve.reciprocal(wgt[:, 0, :], lv[:, 0, :]))
            link(dve.tensor_tensor(wgt[:, 1, :], wgt[:, 1, :], wgt[:, 0, :], ALU.mult))
            link(dve.tensor_tensor(comb[:], m0[:], wgt[:, 0, :].unsqueeze(2).to_broadcast([P, NT, E]), ALU.mult))
            link(dve.tensor_tensor(posn[:], m1[:], wgt[:, 1, :].unsqueeze(2).to_broadcast([P, NT, E]), ALU.mult))
            dve.tensor_tensor(comb[:], comb[:], posn[:], ALU.add).then_inc(comb_ready, 1)
            for half in range(2):
                arrive(dve, "combT", half)
                n = dve.tensor_copy(combT[:, half * 512:(half + 1) * 512], bank("combT", half)[0:E, :])
                empty(n, "combT", half)
            for t in range(NT):
                arrive(dve, "b2", t)
                n = dve.tensor_tensor(xs[:, t, :], xs[:, t, :], bank("b2", t), ALU.add)
                empty(n, "b2", t)

            total = dve.value_load(bounds[0:1, E:E + 1], min_val=E, max_val=MAX_TILES)
            dve.sem_inc(y_evac, 1)
            dve.sem_inc(yrow_free, 2)

            def evac_x(n):
                dve.wait_ge(x_turned, n)
                dve.tensor_copy(xT[:], ps[:, 1, :].rearrange("p (k n) -> p k n", k=KD)).then_inc(xT_ready, 1)

            def copy_x(n, par):
                dve.wait_ge(xin_in, n * 16 + 16)
                dve.tensor_copy(xrow[:], xin[:, par, :]).then_inc(x_copied, 1)

            copy_x(0, 0)
            evac_x(1)
            copy_x(1, 1)
            with dve.Fori(0, total) as i:
                evac_x(i + 2)
                copy_x(i + 2, bass.ds(i % 2, 1))
                dve.wait_ge(down_done, i + 1)
                dve.wait_ge(yrow_free, i + 1)
                dve.tensor_copy(yrow[:, bass.ds(i % 2, 1), :], ps[:, 0, :]).then_inc(y_evac, 1)
            for t in range(NT):
                dve.wait_ge(g_in[t], 2 * 16)
                for k in range(2):
                    n = dve.scalar_tensor_tensor(xs[:, t, :], yg[:, t, k, :], wgt[:, k, t:t + 1], xs[:, t, :],
                                                 ALU.mult, ALU.add)
                    if k == 0:
                        link(n)
                n.then_inc(out_ready, 1)

        @block.tensor
        def _(pe):
            def product(dst, pairs):
                n = len(pairs)
                for i, (lhsT, rhs) in enumerate(pairs):
                    last = pe.matmul(dst, lhsT, rhs, start=(i == 0), stop=(i == n - 1))
                return last

            def product3(dst, pairs):
                return product(dst, [p for (ah, al), (bh, bl) in pairs for p in ((ah, bh), (al, bh), (ah, bl))])

            def transposes(key, t, src):
                claim(pe, key, t)
                for k in range(KD):
                    last = pe.transpose(bank(key, t)[:, k * P:(k + 1) * P], src[:, k * P:(k + 1) * P], ident[:])
                fill(last, key, t)

            pe.wait_ge(consts_ready, 2)
            for t in range(NT):
                pe.wait_ge(xn_ready[0], t + 1)
                transposes("T1", t, xn[:, t, :])
            pe.wait_ge(w_in, 4 * 16)
            for half in range(2):
                for t in range(half * NT // 2, (half + 1) * NT // 2):
                    taken(pe, "T1", t)
                for c in range(PAIRS):
                    claim(pe, "q1", half, c)
                    fill(product(bank("q1", half, c),
                                 [(wq1[:, k, c * P:(c + 1) * P], xnT[:, k, half * 512:(half + 1) * 512])
                                  for k in range(KD)]), "q1", half, c)

            def proj_k(b, u, c):
                if c >= 2:
                    wait(pe, k_split, PAIRS * b + c - 1)
                else:
                    wait(pe, v_evac, LC * (b - 1) + c + 3)
                product3(ps[:, 4 + c % 2, :],
                         [([w[:, k, c * P:(c + 1) * P] for w in wk1], [x_[:, k, :] for x_ in cT[u]])
                          for k in range(KC)]
                        ).then_inc(k_proj, 1)

            def proj_v(b, u, c):
                if c >= 2:
                    wait(pe, v_evac, LC * b + c - 1)
                else:
                    wait(pe, k_split, PAIRS * b + c + 3)
                product3(ps[:, 4 + c % 2, :],
                         [([x_[:, k, c * P:(c + 1) * P] for x_ in cT[u]], [w[:, k, :] for w in wv1])
                          for k in range(KC)]
                        ).then_inc(v_proj, 1)

            def score(b, u, c):
                pe.wait_ge(k_split, PAIRS * b + c + 1)
                wait(pe, exp_done, PAIRS * (b - 1) + c + 1)
                product3(ps[:, c, :], [([q[:, c, :] for q in qbd[u]], [k[:, c, :] for k in KT])]
                         ).then_inc(scores, 1)

            def turn(b, c):
                pe.wait_ge(norm_done, PAIRS * b + c + 1)
                wait(pe, pt_evac, PAIRS * b + c)
                for j in range(LC):
                    last = pe.transpose(ps[:, 6, j * P:(j + 1) * P], prob[:, c, j * P:(j + 1) * P], ident[:])
                last.then_inc(pt_done, 1)

            def attend(b, u, c):
                pe.wait_ge(pt_evac, PAIRS * b + c + 1)
                if c == 0:
                    pe.wait_ge(v_evac, LC * (b + 1))
                    wait(pe, o_evac, b)
                product(ps[:, 7, c * P:(c + 1) * P],
                        [(V[u][:, j, c * P:(c + 1) * P], PT[c % 2][:, j, :]) for j in range(LC)]
                        ).then_inc(pv_done, 1)

            def batch(b, u, more=True):
                pe.wait_ge(qbd_ready, b + 1)
                for c in range(PAIRS):
                    score(b, u, c)
                if more:
                    pe.wait_ge(c_split, b + 2)
                    for c in range(PAIRS):
                        proj_k(b + 1, 1 - u, c)
                for c in range(LC):
                    if more:
                        proj_v(b + 1, 1 - u, c)
                    turn(b, c)
                    if c >= 1:
                        attend(b, u, c - 1)
                attend(b, u, PAIRS - 1)

            for b in range(8):
                pe.wait_ge(emptied[b], RING1 // 8)
            pe.wait_ge(w_split, 2)
            pe.wait_ge(c_split, 1)
            for c in range(PAIRS):
                proj_k(0, 0, c)
            for c in range(LC):
                proj_v(0, 0, c)
            batch(0, 0)
            batch(1, 1)
            with pe.Fori(1, NB // 2 - 1) as p:
                for u in range(2):
                    batch(2 * p + u, u)
            batch(NB - 2, 0)
            batch(NB - 1, 1, more=False)

            pe.wait_ge(wo_in, 16)
            pe.wait_ge(o_evac, NB)
            for t in range(NT + 2):
                if t < NT:
                    claim(pe, "wo1", t)
                    fill(product(bank("wo1", t), [(OT[:, k, t * P:(t + 1) * P], wo1[:, k, :]) for k in range(KD)]),
                         "wo1", t)
                if t >= 2:
                    pe.wait_ge(xn_ready[1], t - 1)
                    transposes("T2", t - 2, xn[:, t - 2, :])
            pe.wait_ge(w2_in, 10 * 16)
            for t in range(NT):
                claim(pe, "z", t)
                taken(pe, "T2", t)
                fill(product(bank("z", t)[:, 0:H], [(xnT[:, k, t * P:(t + 1) * P], wf[:, k, :]) for k in range(KD)]),
                     "z", t)
            for half in range(2):
                claim(pe, "t1", half)
                fill(product(bank("t1", half)[0:32, :],
                             [(wg1[:, k, :], xnT[:, k, half * 512:(half + 1) * 512]) for k in range(KD)]),
                     "t1", half)
            for t in range(NT):
                for what, w in (("k", wkT2), ("v", wvT2)):
                    claim(pe, what, t)
                    fill(product(bank(what, t), [(xnT[:, k, t * P:(t + 1) * P], w[:, k, :]) for k in range(KD)]),
                         what, t)
                claim(pe, "q", t)
                for c in range(KD):
                    last = product(bank("q", t)[:, c * P:(c + 1) * P],
                                   [(wqT2[:, k, c * P:(c + 1) * P], xnT[:, k, t * P:(t + 1) * P])
                                    for k in range(KD)])
                fill(last, "q", t)
            for half in range(2):
                taken(pe, "t1", half)
            for t in range(NT):
                claim(pe, "gate", t)
                fill(product(bank("gate", t), [(t1T[:, t * P:(t + 1) * P], wg2[:])]), "gate", t)
                taken(pe, "k", t)
                transposes("kT", t, ksil[:, t, :])
            for t in range(NT + LAG_R):
                if t < NT:
                    tok = slice(t * P, (t + 1) * P)
                    taken(pe, "q", t)
                    taken(pe, "kT", t)
                    for r in range(HR):
                        claim(pe, "seg", t, r)
                        pe.wait_ge(Mf_ready, HR * t + r + 1)
                        for c in range(HR):
                            last = pe.matmul(bank("seg", t, r)[:, c * P:(c + 1) * P], Mf[:, r, c, :], causal[:],
                                             start=True, stop=True)
                        fill(last, "seg", t, r)
                        claim(pe, "A", t, r)
                        h = slice(r * HD, (r + 1) * HD)
                        for c in range(HR):
                            last = pe.matmul(bank("A", t, r)[:, c * P:(c + 1) * P], kT2[h, c, tok], qT2[h, c, tok],
                                             start=True, stop=True)
                        fill(last, "A", t, r)
                u = t - LAG_O
                if 0 <= u < NT:
                    claim(pe, "o", u)
                    for r in range(HR):
                        taken(pe, "A", u, r)
                    pe.wait_ge(v_scaled, u + 1)
                    for c in range(HR):
                        for r in range(HR):
                            h = HR * c + r
                            last = pe.matmul(bank("o", u)[:, h * HD:(h + 1) * HD], Wt[:, r, c, :],
                                             vt[:, u, h * HD:(h + 1) * HD], start=True, stop=True)
                    fill(last, "o", u)
                u = t - LAG_T4
                if 0 <= u < NT:
                    pe.wait_ge(xn_ready[2], u + 1)
                    transposes("T4", u, xn[:, u, :])
                    claim(pe, "wo2", u)
                    taken(pe, "T4", u)
                    pe.wait_ge(woT_in, 16)
                    fill(product(bank("wo2", u), [(xnT[:, k, u * P:(u + 1) * P], woT2[:, k, :]) for k in range(KD)]),
                         "wo2", u)
                u = t - LAG_T5
                if 0 <= u < NT:
                    pe.wait_ge(xn_ready[3], u + 1)
                    transposes("T5", u, xn[:, u, :])
                    claim(pe, "logit", u)
                    taken(pe, "T5", u)
                    fill(product(bank("logit", u)[:, 0:E],
                                 [(xnT[:, k, u * P:(u + 1) * P], gw[:, k, :]) for k in range(KD)]), "logit", u)

            pe.wait_ge(sel_ready, 1)
            rows = selm[:].rearrange("p t e -> p (t e)")
            for key, m in (("prefix", before), ("total", ones)):
                claim(pe, key)
                fill(product(bank(key)[:, 0:NT * E], [(m[:], rows)]), key)
            pe.wait_ge(comb_ready, 1)
            for half in range(2):
                claim(pe, "combT", half)
                for j in range(4):
                    last = pe.transpose(bank("combT", half)[0:E, j * P:(j + 1) * P], comb[:, 4 * half + j, :],
                                        ident[:])
                fill(last, "combT", half)
            for t in range(NT):
                claim(pe, "b2", t)
                taken(pe, "combT", t // 4)
                fill(product(bank("b2", t), [(combT[:, t * P:(t + 1) * P], b2_sb[:])]), "b2", t)

            for t in range(NT):
                taken(pe, "b2", t)

            def turn_x():
                for k in range(KD):
                    last = pe.transpose(ps[:, 1, k * P:(k + 1) * P], xrow[:, k * P:(k + 1) * P], ident[:])
                last.then_inc(x_turned, 1)

            def expert_tile(u, i, loads):
                pe.wait_ge(w1_in[u], loads)
                pe.wait_ge(xT_ready, i + 1)
                for g in range(KF // 4):
                    for j in range(4):
                        f = 4 * g + j
                        last = product(ps[:, 4 + g, j * P:(j + 1) * P],
                                       [(W1[u][:, k, f * P:(f + 1) * P], xT[:, k, :]) for k in range(KD)])
                    last.then_inc(up_done, 1)
                pe.wait_ge(x_copied, i + 2)
                turn_x()
                pe.wait_ge(w2e_in[u], loads)
                pe.wait_ge(y_evac, i + 1)
                for f in range(KF):
                    if f % 4 == 0:
                        pe.wait_ge(gelu_done, i * (KF // 4) + (f // 4 + 1))
                    last = pe.matmul(ps[:, 0, :], hT[:, f, :], W2[u][:, f, :], start=(f == 0), stop=(f == KF - 1))
                last.then_inc(down_done, 1)

            pe.wait_ge(bounds_ready, 1)
            pe.wait_ge(x_copied, 1)
            turn_x()
            with pe.Fori(0, E // 2) as p:
                for u in range(2):
                    first = pe.value_load(bounds[0:1, bass.ds(2 * p + u, 1)], min_val=0, max_val=MAX_TILES - 1)
                    end = pe.value_load(bounds[0:1, bass.ds(2 * p + u + 1, 1)], min_val=1, max_val=MAX_TILES)
                    with pe.Fori(first, end) as i:
                        expert_tile(u, i, p * 16 + 16)


_INS = ["x", "ctxT", "xWq", "xWk", "xWv", "xWo", "xbo", "aWqT", "aWkT", "aWvT", "aWfT", "aWg1T", "aWg2T",
        "a_ln_w", "aWoT", "gate_w", "w1", "b1T", "w2", "b2"]


def kernel(**inputs):
    import numpy as np
    import concourse.bacc as bacc
    from concourse.bass_utils import run_bass_kernel_spmd

    g = {k: np.asarray(v) for k, v in inputs.items()}
    B, S, D = g["x"].shape
    E, _, F = g["L0_ffn_w1"].shape
    host = {
        "x": g["x"].reshape(B * S, D),
        "ctxT": g["ctx_768"].transpose(0, 2, 1),
        "xWq": g["L0_xattn_Wq"], "xWk": g["L0_xattn_Wk"], "xWv": g["L0_xattn_Wv"], "xWo": g["L0_xattn_Wo"],
        "xbo": g["L0_xattn_bo"].reshape(1, D),
        "aWqT": g["L0_attn_Wq"].T, "aWkT": g["L0_attn_Wk"].T, "aWvT": g["L0_attn_Wv"].T,
        "aWfT": g["L0_attn_Wf"].T, "aWg1T": g["L0_attn_Wg1"].T, "aWg2T": g["L0_attn_Wg2"].T,
        "a_ln_w": g["L0_attn_ln_w"].reshape(1, D), "aWoT": g["L0_attn_Wo"].T,
        "gate_w": g["L0_ffn_gate_w"], "w1": g["L0_ffn_w1"],
        "b1T": g["L0_ffn_b1"].reshape(E, F // 128, 128).transpose(2, 0, 1),
        "w2": g["L0_ffn_w2"], "b2": g["L0_ffn_b2"],
    }
    nc = bacc.Bacc("TRN2", target_bir_lowering=False, num_devices=1)
    arrays, args = {}, []
    for name in _INS:
        a = np.ascontiguousarray(host[name])
        arrays[f"in_{name}"] = a
        args.append(nc.dram_tensor(f"in_{name}", a.shape, mybir.dt.from_np(a.dtype), kind="ExternalInput").ap())
    fp32 = mybir.dt.float32
    args.append(nc.dram_tensor("out_rows", (B * S, D), fp32, kind="ExternalOutput").ap())
    rows = (2 * B * S // 128 + E + 1) * 128
    args.append(nc.dram_tensor("slots", (rows, D), fp32, kind="Internal").ap())
    perceiver_layer(nc, *args)
    r = run_bass_kernel_spmd(nc, [arrays], core_ids=[0])
    return r.results[0]["out_rows"].reshape(B, S, D)
```

```python
import concourse.bass as bass
from concourse import mybir
from contextlib import ExitStack


def perceiver_layer(
    nc: bass.Bass,
    x: bass.AP,
    ctxT: bass.AP,
    xWq: bass.AP,
    xWk: bass.AP,
    xWv: bass.AP,
    xWo: bass.AP,
    xbo: bass.AP,
    aWqT: bass.AP,
    aWkT: bass.AP,
    aWvT: bass.AP,
    aWfT: bass.AP,
    aWg1T: bass.AP,
    aWg2T: bass.AP,
    a_ln_w: bass.AP,
    aWoT: bass.AP,
    gate_w: bass.AP,
    w1: bass.AP,
    b1T: bass.AP,
    w2: bass.AP,
    b2: bass.AP,
    out: bass.AP,
    slots: bass.AP,
):
    fp32 = mybir.dt.float32
    fp32r = mybir.dt.float32r
    i32 = mybir.dt.int32
    u32 = mybir.dt.uint32
    ALU = mybir.AluOpType
    ACT = mybir.ActivationFunctionType
    AX = mybir.AxisListType

    P = 128
    D = x.shape[1]
    NT = x.shape[0] // P
    KD = D // P
    NB, C, L = ctxT.shape
    S = x.shape[0] // NB
    KC = C // P
    LC = L // P
    XH = 8
    DH = D // XH
    PAIRS = XH // 2
    SCALE = DH ** -0.5
    H = 16
    HD = D // H
    GF = 3 * 32 + H
    HR = P // HD
    E, _, F = w1.shape
    KF = F // P
    FG = 4
    NG = KF // FG
    MAX_TILES = 2 * NT + E - 1
    TILES_AHEAD = MAX_TILES + 2
    CAP = NT * P
    SENT = ((0, NT - 3), (NT - 3, NT - 1), (NT - 1, NT))
    EPS = 1e-5
    KB = 1024
    BASE = 16512

    ctx = ExitStack()
    with ctx:
        used = [0]
        ctx.enter_context(nc.sbuf_tensor("arena", [P, 52000], fp32))

        def at(name, shape, offset, dt=fp32):
            return nc.alloc_sbuf_tensor_at(name, shape, dt, offset=BASE + offset)

        def const(name, shape, dt=fp32):
            n = 4
            for s in shape[1:]:
                n *= s
            n = (n + 31) // 32 * 32
            h = at(name, shape, 192 * KB + used[0], dt)
            used[0] += n
            return h

        def sem(name):
            return ctx.enter_context(nc.semaphore(name))

        xs = at("xs", [P, NT, D], 144 * KB)
        xn = at("xn", [P, NT, D], 160 * KB)
        xnT = at("xnT", [P, KD, NT * P], 176 * KB)
        ident = const("ident", [P, P])
        causal = const("causal", [P, P])
        after = const("after", [P, P])
        before = const("before", [P, P])
        ones = const("ones", [P, P])
        unseen = const("unseen", [P, P], fp32r)
        ident_r = const("ident_r", [P, P], fp32r)
        after_r = const("after_r", [P, P], fp32r)
        lnw_rows = const("lnw_rows", [P, D])
        gw = const("gw", [P, KD, E])
        stats = const("stats", [P, 2, 6])
        mv = const("mv", [P, 4, NT, 2])
        vare = const("vare", [P, 4, NT])
        rstd = const("rstd", [P, 4, NT])
        mhalf = const("mhalf", [P, H])
        rowmax = const("rowmax", [P, PAIRS])
        negmax = const("negmax", [P, PAIRS])
        rowsum = const("rowsum", [P, PAIRS])
        rowinv = const("rowinv", [P, PAIRS])
        zf = const("zf", [P, NT, H])
        fa = const("fa", [P, NT, H])
        fb = const("fb", [P, NT, H])
        fh = const("fh", [P, NT, H], fp32r)
        fl = const("fl", [P, NT, H])
        ksum = const("ksum", [P, 2, H])
        knorm = const("knorm", [P, 2, H])
        logit = const("logit", [P, NT, E])
        comb = const("comb", [P, NT, E])
        tcount = const("tcount", [P, E])
        tstart = const("tstart", [P, E + 1])
        bounds = const("bounds", [P, 16], i32)
        wgt = const("wgt", [P, 2, NT])
        slot_u = const("slot_u", [P, 2, NT], u32)
        b1_sb = const("b1_sb", [P, E, KF])
        b2_sb = const("b2_sb", [E, D])
        zeros = const("zeros", [P, D])
        lower = const("lower", [P, E + 1, E])
        cap_row = const("cap_row", [P, E])
        tile_no = const("tile_no", [P, TILES_AHEAD])
        tile_row = const("tile_row", [P, TILES_AHEAD], i32)
        steps = const("steps", [P, NT])
        assert used[0] <= 15 * KB + 800, used[0]

        OT = [at(f"OT{part}", [P, PAIRS, NT * P], 110 * n * KB, fp32r) for n, part in enumerate("hl")]
        qbd = [[at(f"qbd{u}{part}", [P, PAIRS, P], (16 + 4 * u + 2 * n) * KB, fp32r)
                for n, part in enumerate("hl")] for u in range(2)]
        wk1 = [at(f"wk1{part}", [P, KC, D], (24 + 6 * n) * KB, fp32r) for n, part in enumerate("hl")]
        wv1 = [at(f"wv1{part}", [P, KC, D], (36 + 6 * n) * KB, fp32r) for n, part in enumerate("hl")]
        craw = at("craw", [P, KC, L], 48 * KB)
        cT = [[at(f"cT{u}{part}", [P, KC, L], (66 - 12 * u + 6 * n) * KB, fp32r)
               for n, part in enumerate("hl")] for u in range(2)]
        KT = [at(f"KT{part}", [P, PAIRS, L], (78 + 8 * n) * KB, fp32r) for n, part in enumerate("hl")]
        V = [at(f"V{u}", [P, LC, D], (94 + 8 * u) * KB) for u in range(2)]
        prob = at("prob", [P, PAIRS, L], 126 * KB)
        PT = [at(f"PT{u}", [P, LC, P], (134 + 2 * u) * KB) for u in range(2)]
        bo_rows = at("bo_rows", [P, D], 138 * KB)
        qT1 = at("qT1", [P, PAIRS, NT * P], 160 * KB)
        xnT1 = [at(f"xnT1{part}", [P, KD, NT * P], (176, 0)[n] * KB, fp32r) for n, part in enumerate("hl")]
        wkr = at("wkr", [P, KC, D], 110 * KB)
        wvr = at("wvr", [P, KC, D], 116 * KB)

        def parts(name, shape, raw, hi):
            return at(name, shape, raw), (at(f"{name}h", shape, hi, fp32r), at(f"{name}l", shape, raw, fp32r))

        wq1_raw, wq1 = parts("wq1", [P, KD, D], 78 * KB, 86 * KB)
        wo1_raw, wo1 = parts("wo1", [P, KD, D], 70 * KB, 62 * KB)
        wq2_raw, wq2 = parts("wq2", [P, KD, D], 24 * KB, 112 * KB)
        wk2_raw, wk2 = parts("wk2", [P, KD, D], 32 * KB, 48 * KB)
        wv2_raw, wv2 = parts("wv2", [P, KD, D], 40 * KB, 126 * KB)
        wgf_raw, wgf = parts("wgf", [P, KD, GF], 16 * KB, 18 * KB)
        wg2 = at("wg2", [96, D], 20 * KB, fp32r)
        wg2_raw = at("wg2_raw", [96, D], 22 * KB)
        xnT2 = [at(f"xnT2{part}", [P, KD, NT * P], (176, 80)[n] * KB, fp32r) for n, part in enumerate("hl")]
        ksil = at("ksil", [P, NT, D], 0)
        t1T = at("t1T", [96, NT * P], 122 * KB, fp32r)
        zT = at("zT", [P, NT * P], 56 * KB)
        wo2 = (at("wo2h", [P, KD, D], 32 * KB, fp32r), at("wo2l", [P, KD, D], 136 * KB, fp32r))
        gatedT = [at(f"gatedT{u}", [P, KD, P], (40 + 2 * u) * KB, fp32r) for u in range(2)]
        gates = [at(f"gates{part}", [P, HR, HR, P], (48 + 8 * n) * KB, fp32r) for n, part in enumerate("hl")]
        ksq = at("ksq", [P, D], 120 * KB)
        qT2 = at("qT2", [P, KD, NT * P], 64 * KB)
        kT2 = at("kT2", [P, KD, NT * P], 80 * KB)
        vt = at("vt", [P, NT, D], 96 * KB)
        dec = [at(f"dec{u}", [P, HR, HR, P], (112 + 8 * u) * KB) for u in range(2)]
        Wt = at("Wt", [P, HR, HR, P], 128 * KB)
        woT2 = at("woT2", [P, KD, D], 136 * KB)
        W1 = [at(f"W1_{u}", [P, KD, F], 64 * u * KB) for u in range(2)]
        W2 = [at(f"W2{part}", [P, KF, D], (64 * n + 32) * KB, fp32r) for n, part in enumerate("hl")]
        W2first = at("W2first", [P, KF, D], 96 * KB)
        W2raw = [at(f"W2raw{n}", [P, FG, D], (160 + 8 * n) * KB) for n in range(2)]
        hraw = [at(f"hraw{n}", [P, FG, P], (130, 186)[n] * KB) for n in range(2)]
        hT = [at(f"hT{part}", [P, KF, P], (176, 136)[n] * KB, fp32r) for n, part in enumerate("hl")]
        xT = at("xT", [P, KD, P], 184 * KB)
        combT = at("combT", [E, NT * P], 40 * KB)
        yg = [at(f"yg{k}", [P, NT, D], 16 * k * KB) for k in range(2)]
        xin = at("xin", [P, 2, D], 188 * KB)
        xrow = at("xrow", [P, D], 128 * KB)
        yrow = at("yrow", [P, 2, D], 132 * KB)
        cmp = at("cmp", [P, NT, E, E], 48 * KB)
        tie = at("tie", [P, NT, E, E], 50 * KB)
        rank = at("rank", [P, NT, E], 52 * KB + 512)
        m0 = at("m0", [P, NT, E], 52 * KB + 768)
        m1 = at("m1", [P, NT, E], 53 * KB)
        selm = at("selm", [P, NT, E], 53 * KB + 256)
        second = at("second", [P, NT, E], 54 * KB)
        posn = at("posn", [P, NT, E], 53 * KB + 512)
        tsum = at("tsum", [P, NT, E], 53 * KB + 768)
        lv = at("lv", [P, 2, NT], 54 * KB + 256)
        slotf = at("slotf", [P, 2, NT], 54 * KB + 384)
        swap = at("swap", [P, NT], 54 * KB + 512)
        ge = at("ge", [P, E, NT], 54 * KB + 576)
        tpart = at("tpart", [P, E + 1, E], 55 * KB)
        rowgap = at("rowgap", [P, E], 55 * KB + 512)
        tile_at = at("tile_at", [P, TILES_AHEAD], 55 * KB + 544)
        rowsum_f = at("rowsum_f", [P, TILES_AHEAD], 55 * KB + 672)
        passed = at("passed", [P, TILES_AHEAD, E], 40 * KB)

        ps = ctx.enter_context(nc.psum_tensor("ps", [P, 8, 512], fp32))

        filled = [sem(f"bank{b}_filled") for b in range(8)]
        emptied = [sem(f"bank{b}_emptied") for b in range(8)]
        plan = {}

        def place(*key):
            plan[key] = (len(plan) % 8, len(plan) // 8)

        def bank(*key):
            return ps[:, plan[key][0], :]

        def claim(pe, *key):
            b, n = plan[key]
            if n:
                pe.wait_ge(emptied[b], n)

        def fill(ins, *key):
            ins.then_inc(filled[plan[key][0]], 1)

        def arrive(eng, *key):
            b, n = plan[key]
            eng.wait_ge(filled[b], n + 1)

        def empty(ins, *key):
            ins.then_inc(emptied[plan[key][0]], 1)

        def taken(eng, *key):
            b, n = plan[key]
            eng.wait_ge(emptied[b], n + 1)

        for t in range(NT):
            place("T1", t)
        for half in range(2):
            for c in range(PAIRS):
                place("q1", half, c)
        RING1 = len(plan)
        for t in range(NT):
            place("wo1", t)
            if t >= 2:
                place("T2", t - 2)
        place("k", 0)
        place("T2", NT - 2)
        place("v", 0)
        place("T2", NT - 1)
        for t in range(NT):
            if t:
                place("k", t)
                place("v", t)
            else:
                place("t1", 0)
                place("t1", 1)
            if t == 1:
                place("z")
            if t % 4 == 3:
                for c in range(KD):
                    place("q", t // 4, c)
        for t in range(NT):
            place("gate", t)
            place("kT", t)
        for t in range(NT):
            for r in range(HR):
                place("seg", t, r)
            for what, lag in (("T4", 2), ("T5", 3), ("o", 1), ("wo2", 2)):
                if t - lag >= 0:
                    place(what, t - lag)
            for r in range(HR):
                place("A", t, r)
            if t >= 3:
                place("logit", t - 3)
        for key in (("T4", NT - 2), ("T5", NT - 3), ("o", NT - 1), ("logit", NT - 3), ("prefix", 0), ("total", 0),
                    ("wo2", NT - 2),
                    ("T4", NT - 1), ("wo2", NT - 1), ("T5", NT - 2), ("logit", NT - 2), ("prefix", 1), ("total", 1),
                    ("T5", NT - 1), ("logit", NT - 1), ("prefix", 2), ("total", 2)):
            place(*key)
        RING2 = [sum(1 for at_bank, _ in plan.values() if at_bank == b) for b in range(8)]
        place("combT", 0)
        place("combT", 1)
        for t in range(NT):
            place("b2", t)

        x_in = [sem(f"x_in{t}") for t in range(NT)]
        wq_in = sem("wq_in")
        wq_hi = sem("wq_hi")
        wq_split = sem("wq_split")
        x1_hi = sem("x1_hi")
        w_in = sem("w_in")
        w2_in = sem("w2_in")
        woT_in = sem("woT_in")
        consts_ready = sem("consts_ready")
        pool_own = sem("pool_own")
        dve_own = sem("dve_own")
        var_ready = [sem(f"var_ready{k}") for k in range(4)]
        rstd_ready = [sem(f"rstd_ready{k}") for k in range(4)]
        xn_ready = [sem(f"xn_ready{k}") for k in range(4)]
        ctx_in = sem("ctx_in")
        wo_in = sem("wo_in")
        wq2_in, wk2_in, wv2_in = sem("wq2_in"), sem("wk2_in"), sem("wv2_in")
        wo_hi, wk2_hi, wv2_hi, wq2_hi = sem("wo_hi"), sem("wk2_hi"), sem("wv2_hi"), sem("wq2_hi")
        wo_split, wk2_split, wv2_split, wq2_split = (sem("wo_split"), sem("wk2_split"), sem("wv2_split"),
                                                     sem("wq2_split"))
        small_hi = sem("small_hi")
        small_split = sem("small_split")
        x2_hi = sem("x2_hi")
        t1_hi = sem("t1_hi")
        wo2_hi = sem("wo2_hi")
        wo2_split = sem("wo2_split")
        x4_hi = sem("x4_hi")
        o_hi = sem("o_hi")
        w_hi = sem("w_hi")
        w_split = sem("w_split")
        c_hi = sem("c_hi")
        c_split = sem("c_split")
        k_hi = sem("k_hi")
        q_hi = sem("q_hi")
        v_proj = sem("v_proj")
        k_proj = sem("k_proj")
        k_split = sem("k_split")
        v_evac = sem("v_evac")
        qbd_ready = sem("qbd_ready")
        scores = sem("scores")
        raw_max = sem("raw_max")
        neg_max = sem("neg_max")
        exp_done = sem("exp_done")
        inv_done = sem("inv_done")
        norm_done = sem("norm_done")
        pt_done = sem("pt_done")
        pt_evac = sem("pt_evac")
        pv_done = sem("pv_done")
        o_evac = sem("o_evac")
        bo_added = sem("bo_added")
        knorm_in = sem("knorm_in")
        v_scaled = sem("v_scaled")
        f_ready = sem("f_ready")
        f_exp = sem("f_exp")
        f_in = sem("f_in")
        f_ln = sem("f_ln")
        fh_ready = sem("fh_ready")
        gates_ready = sem("gates_ready")
        masks_r = sem("masks_r")
        sel_ready = sem("sel_ready")
        p01 = sem("p01")
        e01 = sem("e01")
        comb_ready = sem("comb_ready")
        bounds_ready = sem("bounds_ready")
        slots_ready = sem("slots_ready")
        zero_sent = sem("zero_sent")
        tables_ready = sem("tables_ready")
        scattered = sem("scattered")
        xin_in = sem("xin_in")
        x_copied = sem("x_copied")
        xT_ready = sem("xT_ready")
        up_done = sem("up_done")
        gelu_done = sem("gelu_done")
        h_hi = sem("h_hi")
        h_split = sem("h_split")
        w2_hi = sem("w2_hi")
        w2_split = sem("w2_split")
        down_done = sem("down_done")
        y_sent = sem("y_sent")
        g_in = [[sem(f"g_in{k}_{t}") for t in range(NT)] for k in range(2)]
        x_turned = sem("x_turned")
        y_evac = sem("y_evac")
        yrow_free = sem("yrow_free")
        w1_in = [sem(f"w1_in{u}") for u in range(2)]
        w2first_in = sem("w2first_in")
        w2raw_in = [sem(f"w2raw_in{n}") for n in range(2)]
        first_added = sem("first_added")
        out_ready = sem("out_ready")
        out_sent = sem("out_sent")

        def wait(eng, s, v):
            if not (isinstance(v, int) and v <= 0):
                eng.wait_ge(s, v)

        block = ctx.enter_context(nc.Block())
        blk = lambda w, k: w.rearrange("(k p) n -> p k n", p=P)

        @block.sync
        def _(sp):
            for t in range(NT):
                sp.dma_start(xs[:, t, :], x[t * P:(t + 1) * P, :]).then_inc(x_in[t], 16)
            sp.dma_start(wq1_raw[:], blk(xWq, KD)).then_inc(wq_in, 16)
            sp.dma_start(wkr[:], blk(xWk, KC)).then_inc(w_in, 16)
            sp.dma_start(wvr[:], blk(xWv, KC)).then_inc(w_in, 16)
            sp.dma_start(bo_rows[:], xbo.to_broadcast([P, D])).then_inc(w_in, 16)
            sp.dma_start(craw[:], ctxT[0].rearrange("(k p) l -> p k l", p=P)).then_inc(ctx_in, 16)
            sp.dma_start(gw[:], blk(gate_w, KD)).then_inc(w2_in, 16)
            sp.dma_start(lnw_rows[:], a_ln_w.to_broadcast([P, D])).then_inc(w2_in, 16)
            sp.dma_start(b1_sb[:], b1T).then_inc(w2_in, 16)
            sp.dma_start(b2_sb[:], b2).then_inc(w2_in, 16)

            def load_context(b):
                sp.wait_ge(c_split, b)
                sp.dma_start(craw[:], ctxT[bass.ds(b, 1)].rearrange("b (k p) l -> p (b k) l", p=P)
                             ).then_inc(ctx_in, 16)

            sp.wait_ge(consts_ready, 2)
            with sp.Fori(1, E + 1) as b:
                load_context(b)
                sp.dma_start(slots[bass.ds((b - 1) * CAP, CAP), :].rearrange("(t p) n -> p t n", p=P),
                             zeros[:].unsqueeze(1).to_broadcast([P, NT, D])).then_inc(zero_sent, 16)
            with sp.Fori(E + 1, NB) as b:
                load_context(b)
            sp.wait_ge(v_proj, (NB - 1) * LC)
            sp.dma_start(wo1_raw[:], blk(xWo, KD)).then_inc(wo_in, 16)
            sp.wait_ge(v_proj, NB * LC)
            for dst, src, there in ((wk2_raw, aWkT, wk2_in), (wv2_raw, aWvT, wv2_in), (wq2_raw, aWqT, wq2_in)):
                sp.dma_start(dst[:], blk(src, KD)).then_inc(there, 16)
            sp.wait_ge(scores, NB * PAIRS)
            for n in range(3):
                sp.dma_start(wgf_raw[:, :, 32 * n:32 * (n + 1)], blk(aWg1T, KD)).then_inc(w2_in, 16)
                sp.dma_start(wg2_raw[32 * n:32 * (n + 1), :], aWg2T).then_inc(w2_in, 16)
            sp.dma_start(wgf_raw[:, :, 96:GF], blk(aWfT, KD)).then_inc(w2_in, 16)
            sp.wait_ge(o_evac, NB)
            sp.dma_start(woT2[:], blk(aWoT, KD)).then_inc(woT_in, 16)
            w1e = w1.rearrange("e (k p) f -> e p k f", p=P)
            w2e = w2.rearrange("e (g k p) d -> e g p k d", g=NG, p=P)
            arrive(sp, "kT", NT - 1)
            sp.dma_start(W1[0][:], w1e[0]).then_inc(w1_in[0], 16)
            arrive(sp, "A", NT - 1, HR - 1)
            sp.dma_start(W1[1][:], w1e[1]).then_inc(w1_in[1], 16)

            arrive(sp, "o", NT - 1)
            for g in range(NG):
                sp.dma_start(W2first[:, FG * g:FG * (g + 1), :], w2e[0, g]).then_inc(w2first_in, 16)

            def load_w2(e, g, split):
                if split is not None:
                    sp.wait_ge(w2_split, split)
                src = w2e[e, g] if isinstance(e, int) else w2e[bass.ds(e, 1), g].rearrange("e p k d -> p (e k) d")
                sp.dma_start(W2raw[g % 2][:], src).then_inc(w2raw_in[g % 2], 16)

            sp.wait_ge(scattered, 16 * 2 * NT)
            sp.wait_ge(xin_in, 2 * 16)
            for g in range(2):
                load_w2(1, g, None)
            with sp.Fori(0, E // 2 - 1) as p:
                for u in range(2):
                    for g in range(2, NG):
                        load_w2(2 * p + (u + 1), g, (2 * p + u) * NG + (NG + g - 1))
                    end = sp.value_load(bounds[0:1, bass.ds(2 * p + u + 1, 1)], min_val=1, max_val=MAX_TILES)
                    sp.wait_ge(up_done, end * NG)
                    sp.dma_start(W1[u][:], w1e[bass.ds(2 * p + (u + 2), 1)].rearrange("e p k f -> p (e k) f")
                                 ).then_inc(w1_in[u], 16)
                    for g in range(2):
                        load_w2(2 * p + (u + 2), g, (2 * p + u) * NG + (2 * NG + g - 1))
            for g in range(2, NG):
                load_w2(E - 1, g, (E - 1) * NG + g - 1)
            for t in range(NT):
                sp.wait_ge(out_ready, t + 1)
                sp.dma_start(out[t * P:(t + 1) * P, :], xs[:, t, :]).then_inc(out_sent, 16)
            sp.wait_ge(out_sent, 16 * NT)

        @block.gpsimd
        def _(pool):
            own = [0]

            def link(ins):
                own[0] += 1
                ins.then_inc(pool_own, 1)
                pool.wait_ge(pool_own, own[0])

            def select(m, pattern, cm, op, base=0, fill=0.0):
                return pool.affine_select(out=m, in_=m, compare_op=op, fill=fill, base=base,
                                          pattern=pattern, channel_multiplier=cm)

            link(pool.memset(mhalf[:], -0.5))
            link(pool.memset(ident[:], 0.0))
            select(ident[:], [[-1, P]], 1, ALU.not_equal, fill=1.0).then_inc(consts_ready, 1)

            def powers(kind, t, n=1):
                pool.wait_ge(var_ready[kind], t + n)
                pool.tensor_tensor(rstd[:, kind, t:t + n], vare[:, kind, t:t + n], mhalf[:, 0:n], ALU.pow
                                   ).then_inc(rstd_ready[kind], n)

            for m in (causal, after, before, lower, ones):
                link(pool.memset(m[:], 1.0))
            link(select(causal[:], [[1, P]], -1, ALU.is_ge))
            link(select(after[:], [[-1, P]], 1, ALU.is_gt))
            link(select(before[:], [[1, P]], -1, ALU.is_gt))
            link(pool.memset(causal[0:S, S:P], 0.0))
            link(pool.memset(after[S:P, 0:S], 0.0))
            link(select(lower[:], [[1, E + 1], [-1, E]], 0, ALU.is_gt))
            for t in range(3):
                powers(0, t)
            for t in range(3, 7):
                powers(0, t)
                pool.wait_ge(rstd_ready[0], t + 1)
                link(pool.memset(qbd[(t - 3) // 2][(t - 3) % 2][:].bitcast(fp32), 0.0))
            powers(0, 7)
            pool.wait_ge(rstd_ready[0], NT)
            for m in range(NT):
                link(pool.memset(steps[:, m:m + 1], float(P * m + 1)))
            for e in range(E):
                link(pool.memset(cap_row[:, e:e + 1], float(CAP * e)))
            for i in range(TILES_AHEAD):
                link(pool.memset(tile_no[:, i:i + 1], float(i)))
            pool.memset(zeros[:], 0.0).then_inc(consts_ready, 1)

            pool.wait_ge(w_in, 3 * 16)
            for raw, (hi, lo) in ((wkr, wk1), (wvr, wv1)):
                pool.wait_ge(w_hi, 1 if raw is wkr else 2)
                pool.tensor_tensor(lo[:], raw[:], hi[:].bitcast(fp32), ALU.subtract).then_inc(w_split, 1)

            def split_context(b, u):
                pool.wait_ge(ctx_in, 16 * (b + 1))
                wait(pool, v_proj, LC * (b - 1))
                pool.tensor_tensor(cT[u][0][:], craw[:], ones[:, 0:1].unsqueeze(2).to_broadcast([P, KC, L]), ALU.mult
                                   ).then_inc(c_hi, 1)
                pool.wait_ge(c_hi, b + 1)
                pool.tensor_tensor(cT[u][1][:], craw[:], cT[u][0][:].bitcast(fp32), ALU.subtract
                                   ).then_inc(c_split, 1)

            split_context(0, 0)
            split_context(1, 1)
            for t in range(NT):
                pool.wait_ge(xn_ready[0], t + 1)
                pool.tensor_tensor(xs[:, t, :], xs[:, t, :], bo_rows[:], ALU.add).then_inc(bo_added, 1)

            def normalise(b):
                for c in range(PAIRS):
                    pool.wait_ge(inv_done, PAIRS * b + c + 1)
                    pool.tensor_tensor(prob[:, c, :], prob[:, c, :], rowinv[:, c:c + 1].to_broadcast([P, L]), ALU.mult
                                       ).then_inc(norm_done, 1)

            for b in range(2):
                normalise(b)
                split_context(b + 2, b)
            with pool.Fori(1, NB // 2 - 1) as p:
                for u in range(2):
                    normalise(2 * p + u)
                    split_context(2 * p + u + 2, u)
            normalise(NB - 2)
            normalise(NB - 1)

            def low_w(raw, split, hi_done, done, k):
                pool.wait_ge(hi_done, 1)
                pool.tensor_tensor(split[1][:, k, :], raw[:, k, :], split[0][:, k, :].bitcast(fp32), ALU.subtract
                                   ).then_inc(done, 1)

            for k in range(KD):
                low_w(wo1_raw, wo1, wo_hi, wo_split, k)
            for t in range(NT):
                powers(1, t)
                for k in range(2 * t, 2 * t + 2):
                    if k < KD:
                        low_w(wk2_raw, wk2, wk2_hi, wk2_split, k)
                    elif k < 2 * KD:
                        low_w(wv2_raw, wv2, wv2_hi, wv2_split, k - KD)
            for k in range(KD):
                low_w(wq2_raw, wq2, wq2_hi, wq2_split, k)

            def masked_gates(t):
                for r in range(HR):
                    if t:
                        arrive(pool, "seg", t - 1, r)
                    for f, part in ((fh, gates[0]), (fl, gates[1])):
                        fv = f[:, t, :].rearrange("p (c r) -> p r c", r=HR)
                        if f is fh:
                            fv = fv.bitcast(fp32)
                        pool.tensor_tensor(part[:, r], causal[:].unsqueeze(1).to_broadcast([P, HR, P]),
                                           fv[:, r, :].unsqueeze(2).to_broadcast([P, HR, P]), ALU.mult
                                           ).then_inc(gates_ready, 1)

            for t in range(NT):
                if t == NT - 1:
                    pool.wait_ge(f_ready, 1)
                    arrive(pool, "k", NT - 1)
                    masked_gates(0)
                pool.wait_ge(knorm_in, t + 1)
                if t:
                    pool.wait_ge(v_scaled, t)
                link(pool.tensor_tensor(knorm[:, t % 2, :], ksum[:, t % 2, :], mhalf[:], ALU.pow))
                taken(pool, "v", t)
                v3 = vt[:, t, :].rearrange("p (h d) -> p h d", d=HD)
                pool.tensor_tensor(v3, v3, knorm[:, t % 2, :].unsqueeze(2).to_broadcast([P, H, HD]), ALU.mult
                                   ).then_inc(v_scaled, 1)

            def send_rows(t):
                pool.wait_ge(slots_ready, [t < b for a, b in SENT].index(True) + 1)
                if t == 0:
                    pool.wait_ge(zero_sent, 16 * E)
                for k in range(2):
                    pool.indirect_dma_start(
                        out=slots, out_offset=bass.IndirectOffsetOnAxis(ap=slot_u[:, k, t:t + 1], axis=0),
                        in_=xn[:, t, :], in_offset=None).then_inc(scattered, 16)

            for t in range(NT + 2):
                if t + 1 < NT:
                    masked_gates(t + 1)
                if 0 <= t - 1 < NT:
                    powers(2, t - 1)
                if t == NT + 1:
                    for u in range(3):
                        send_rows(u)
                if 0 <= t - 2 < NT:
                    powers(3, t - 2)

            for t in range(3, NT):
                send_rows(t)
            pool.wait_ge(scattered, 16 * 2 * NT)

            def tile_rows(i):
                row = pool.value_load(tile_row[0:1, i], min_val=0, max_val=E * CAP - P)
                return slots[bass.ds(row, P), :]

            pool.wait_ge(tables_ready, 1)
            total = pool.value_load(bounds[0:1, E:E + 1], min_val=E, max_val=MAX_TILES)
            taken(pool, "T5", NT - 1)
            arrive(pool, "logit", NT - 1)
            for n in range(2):
                pool.dma_start(xin[:, n, :], tile_rows(slice(n, n + 1))).then_inc(xin_in, 16)
                pool.wait_ge(xin_in, 16 * (n + 1))
            pool.sem_inc(h_split, 2)

            def low_h(i):
                for g in range(NG):
                    f = slice(FG * g, FG * (g + 1))
                    pool.wait_ge(h_hi, i * NG + (g + 1))
                    pool.tensor_tensor(hT[1][:, f, :], hraw[g % 2][:], hT[0][:, f, :].bitcast(fp32), ALU.subtract
                                       ).then_inc(h_split, 1)

            pool.wait_ge(x_copied, 1)
            pool.dma_start(xin[:, 0, :], tile_rows(slice(2, 3))).then_inc(xin_in, 16)
            low_h(0)
            pool.wait_ge(xin_in, 3 * 16)

            def load_rows(i):
                pool.wait_ge(x_copied, i + 1)
                pool.dma_start(xin[:, bass.ds(i % 2, 1), :], tile_rows(bass.ds(i + 2, 1))).then_inc(xin_in, 16)

            def store_rows(i):
                pool.wait_ge(y_evac, i + 2)
                pool.dma_start(tile_rows(bass.ds(i, 1)), yrow[:, bass.ds(i % 2, 1), :]).then_inc(y_sent, 16)

            def fetch(t, k):
                pool.indirect_dma_start(
                    out=yg[k][:, t, :], out_offset=None,
                    in_=slots, in_offset=bass.IndirectOffsetOnAxis(ap=slot_u[:, k, t:t + 1], axis=0)
                ).then_inc(g_in[k][t], 16)

            last_first = pool.value_load(bounds[0:1, E - 1:E], min_val=E - 1, max_val=MAX_TILES - 1)
            with pool.Fori(1, last_first) as i:
                load_rows(i)
                store_rows(i - 1)
                low_h(i)
                pool.wait_ge(xin_in, i * 16 + 48)
                pool.wait_ge(y_sent, i * 16)
                pool.sem_inc(yrow_free, 1)
            store_rows(last_first - 1)
            pool.wait_ge(y_sent, last_first * 16)
            pool.sem_inc(yrow_free, 1)
            for t in range(NT):
                fetch(t, 0)
            with pool.Fori(last_first, total) as i:
                load_rows(i)
                low_h(i)
                for t in range(NT):
                    pool.wait_ge(g_in[0][t], 16)
                store_rows(i)
                pool.wait_ge(xin_in, i * 16 + 48)
                pool.wait_ge(y_sent, i * 16 + 16)
                pool.sem_inc(yrow_free, 1)
            for t in range(NT):
                fetch(t, 1)

        @block.scalar
        def _(act):
            def copy(dst, src):
                return act.activation(dst, src, ACT.Copy)

            def q_half(half):
                for c in range(PAIRS):
                    arrive(act, "q1", half, c)
                    n = copy(qT1[:, c, half * 512:(half + 1) * 512], bank("q1", half, c))
                    empty(n, "q1", half, c)

            for t in range(NT):
                arrive(act, "T1", t)
                copy(xnT1[0][:, :, t * P:(t + 1) * P], bank("T1", t).rearrange("p (k n) -> p k n", k=KD)
                     ).then_inc(x1_hi, 1)
                if t >= NT - KD:
                    k = t - (NT - KD)
                    act.wait_ge(wq_in, 16)
                    copy(wq1[0][:, k, :], wq1_raw[:, k, :]).then_inc(wq_hi, 1)
            act.wait_ge(w_in, 3 * 16)
            for raw, split in ((wkr, wk1), (wvr, wv1)):
                copy(split[0][:], raw[:]).then_inc(w_hi, 1)
            q_half(0)
            q_half(1)

            def high_k(b, c):
                act.wait_ge(k_proj, PAIRS * b + c + 1)
                copy(KT[0][:, c, :], ps[:, 4 + c % 2, :]).then_inc(k_hi, 1)

            def evac_v(b, u, c):
                act.wait_ge(v_proj, LC * b + c + 1)
                copy(V[u][:, c, :], ps[:, 4 + c % 2, :]).then_inc(v_evac, 1)

            def exps(b, c):
                act.wait_ge(neg_max, PAIRS * b + c + 1)
                wait(act, pt_done, PAIRS * (b - 1) + c + 1)
                act.activation(prob[:, c, :], ps[:, c, :], ACT.Exp, bias=negmax[:, c:c + 1], scale=SCALE,
                               accum_out=rowsum[:, c:c + 1]).then_inc(exp_done, 1)

            def batch(b, u, more=True):
                for c in range(PAIRS):
                    exps(b, c)
                    if more and c >= 1:
                        high_k(b + 1, c - 1)
                if more:
                    high_k(b + 1, PAIRS - 1)
                for c in range(LC):
                    if more:
                        evac_v(b + 1, 1 - u, c)

            for c in range(PAIRS):
                high_k(0, c)
            for c in range(LC):
                evac_v(0, 0, c)
            batch(0, 0)
            batch(1, 1)
            with act.Fori(1, NB // 2 - 1) as p:
                for u in range(2):
                    batch(2 * p + u, u)
            batch(NB - 2, 0)
            batch(NB - 1, 1, more=False)

            act.wait_ge(wo_in, 16)
            act.wait_ge(v_proj, NB * LC)
            copy(wo1[0][:], wo1_raw[:]).then_inc(wo_hi, 1)
            act.wait_ge(wk2_in, 16)
            copy(wk2[0][:], wk2_raw[:]).then_inc(wk2_hi, 1)
            act.wait_ge(pt_done, NB * PAIRS)
            act.wait_ge(wv2_in, 16)
            copy(wv2[0][:], wv2_raw[:]).then_inc(wv2_hi, 1)
            for t in range(NT):
                arrive(act, "T2", t)
                copy(xnT2[0][:, :, t * P:(t + 1) * P], bank("T2", t).rearrange("p (k n) -> p k n", k=KD)
                     ).then_inc(x2_hi, 1)
                if t == NT - 2:
                    arrive(act, "wo1", NT - 1)
                    act.wait_ge(wq2_in, 16)
                    copy(wq2[0][:], wq2_raw[:]).then_inc(wq2_hi, 1)
            for t in range(NT):
                for what, dst in (("k", ksil[:, t, :]), ("v", vt[:, t, :])):
                    arrive(act, what, t)
                    n = act.activation(dst, bank(what, t), ACT.Silu)
                    empty(n, what, t)
                if t == 0:
                    for half in range(2):
                        toks = slice(half * 512, (half + 1) * 512)
                        arrive(act, "t1", half)
                        copy(zT[96:GF, toks], bank("t1", half)[96:GF, :])
                        copy(t1T[:, toks], bank("t1", half)[0:96, :]).then_inc(t1_hi, 1)
                if t == 2:
                    act.wait_ge(f_in, 1)
                    act.activation(fa[:], fa[:], ACT.Exp).then_inc(f_exp, 1)
                    act.wait_ge(f_exp, 1)
                    act.activation(fa[:], fa[:], ACT.Ln, bias=1.0).then_inc(f_ln, 1)
                if t % 4 == 3:
                    for c in range(KD):
                        arrive(act, "q", t // 4, c)
                        n = act.activation(qT2[:, c, (t - 3) * P:(t + 1) * P], bank("q", t // 4, c), ACT.Silu)
                        empty(n, "q", t // 4, c)
            for t in range(NT):
                arrive(act, "gate", t)
                n = act.activation(xn[:, t, :], bank("gate", t), ACT.Sigmoid)
                empty(n, "gate", t)
            for t in range(NT + 3):
                if t < NT:
                    for r in range(HR):
                        arrive(act, "seg", t, r)
                        if t >= 2:
                            taken(act, "A", t - 2, r)
                        n = act.activation(dec[t % 2][:, r], bank("seg", t, r).rearrange("p (c s) -> p c s", s=P),
                                           ACT.Exp)
                        empty(n, "seg", t, r)
                u = t - 2
                if 0 <= u < NT:
                    arrive(act, "T4", u)
                    copy(xnT2[0][:, :, u * P:(u + 1) * P], bank("T4", u).rearrange("p (k n) -> p k n", k=KD)
                         ).then_inc(x4_hi, 1)
                u = t - 3
                if 0 <= u < NT:
                    arrive(act, "T5", u)
                    n = copy(xnT[:, :, u * P:(u + 1) * P], bank("T5", u).rearrange("p (k n) -> p k n", k=KD))
                    empty(n, "T5", u)

            act.wait_ge(p01, 1)
            act.activation(wgt[:, 1, :], lv[:, 0, :], ACT.Exp).then_inc(e01, 1)
            act.wait_ge(bounds_ready, 1)
            act.wait_ge(w2_in, 11 * 16)
            with act.Fori(0, E) as e:
                first = act.value_load(bounds[0:1, bass.ds(e, 1)], min_val=0, max_val=MAX_TILES - 1)
                end = act.value_load(bounds[0:1, bass.ds(e + 1, 1)], min_val=1, max_val=MAX_TILES)
                with act.Fori(first, end) as i:
                    for g in range(NG):
                        act.wait_ge(up_done, i * NG + (g + 1))
                        act.wait_ge(h_split, i * NG + (g + 1))
                        for j in range(FG):
                            last = act.activation(hraw[g % 2][:, j, :], ps[:, 4 + g, j * P:(j + 1) * P], ACT.Gelu,
                                                  bias=b1_sb[:, bass.ds(e, 1), FG * g + j])
                        last.then_inc(gelu_done, 1)
                        act.wait_ge(gelu_done, i * NG + (g + 1))
                        copy(hT[0][:, FG * g:FG * (g + 1), :], hraw[g % 2][:]).then_inc(h_hi, 1)

        @block.vector
        def _(dve):
            own = [0]

            def link(ins):
                own[0] += 1
                ins.then_inc(dve_own, 1)
                dve.wait_ge(dve_own, own[0])

            def spread(kind, t, src):
                link(dve.bn_stats(stats[:, 0, :], src))
                link(dve.bn_aggr(mv[:, kind, t, :], stats[:, 0, :]))
                dve.tensor_scalar(vare[:, kind, t:t + 1], mv[:, kind, t, 1:2], EPS, None, ALU.add
                                  ).then_inc(var_ready[kind], 1)

            def low(lo, held, hi):
                return dve.tensor_tensor(lo, held, hi.bitcast(fp32), ALU.subtract)

            def centre(kind, t, src):
                dve.wait_ge(rstd_ready[kind], t + 1)
                return dve.tensor_scalar(xn[:, t, :], src, mv[:, kind, t, 0:1], rstd[:, kind, t:t + 1],
                                         ALU.subtract, ALU.mult)

            for t in range(NT + 1):
                if t < NT:
                    dve.wait_ge(x_in[t], 16)
                    spread(0, t, xs[:, t, :])
                if t:
                    centre(0, t - 1, xs[:, t - 1, :]).then_inc(xn_ready[0], 1)

            for k in range(KD):
                dve.wait_ge(wq_hi, k + 1)
                low(wq1[1][:, k, :], wq1_raw[:, k, :], wq1[0][:, k, :]).then_inc(wq_split, 1)
            for t in range(NT):
                dve.wait_ge(x1_hi, t + 1)
                tok = slice(t * P, (t + 1) * P)
                n = low(xnT1[1][:, :, tok], bank("T1", t).rearrange("p (k n) -> p k n", k=KD), xnT1[0][:, :, tok])
                empty(n, "T1", t)
            dve.wait_ge(consts_ready, 2)
            dve.tensor_copy(ident_r[:], ident[:])
            dve.tensor_copy(after_r[:], after[:])
            dve.tensor_scalar(unseen[:], causal[:], -1.0, 32768.0, ALU.add, ALU.mult).then_inc(masks_r, 1)

            def maxes(b):
                for c in range(PAIRS):
                    dve.wait_ge(scores, PAIRS * b + c + 1)
                    dve.reduce_max(rowmax[:, c:c + 1], ps[:, c, :], AX.X).then_inc(raw_max, 1)
                    dve.wait_ge(raw_max, PAIRS * b + c + 1)
                    dve.tensor_scalar(negmax[:, c:c + 1], rowmax[:, c:c + 1], -SCALE, None, ALU.mult
                                      ).then_inc(neg_max, 1)

            def inverse(b, c):
                dve.wait_ge(exp_done, PAIRS * b + c + 1)
                wait(dve, norm_done, PAIRS * (b - 1) + c + 1)
                dve.reciprocal(rowinv[:, c:c + 1], rowsum[:, c:c + 1]).then_inc(inv_done, 1)

            def low_k(b, c):
                dve.wait_ge(k_hi, PAIRS * b + c + 1)
                low(KT[1][:, c, :], ps[:, 4 + c % 2, :], KT[0][:, c, :]).then_inc(k_split, 1)

            def evac_pt(b, c):
                dve.wait_ge(pt_done, PAIRS * b + c + 1)
                wait(dve, pv_done, PAIRS * b + c - 1)
                dve.tensor_copy(PT[c % 2][:], ps[:, 6, :].rearrange("p (l n) -> p l n", l=LC)
                                ).then_inc(pt_evac, 1)

            def evac_o(b):
                dve.wait_ge(pv_done, PAIRS * (b + 1))
                for g in range(2):
                    h = slice(g * DH, (g + 1) * DH)
                    o = ps[h, 7, :].rearrange("p (c n) -> p c n", c=PAIRS)
                    last = dve.tensor_copy(OT[0][h, :, bass.ds(b * S, S)], o[:, :, h])
                last.then_inc(o_hi, 1)
                dve.wait_ge(o_hi, b + 1)
                for g in range(2):
                    h = slice(g * DH, (g + 1) * DH)
                    o = ps[h, 7, :].rearrange("p (c n) -> p c n", c=PAIRS)
                    last = low(OT[1][h, :, bass.ds(b * S, S)], o[:, :, h], OT[0][h, :, bass.ds(b * S, S)])
                last.then_inc(o_evac, 1)

            def block_q(b, u):
                wait(dve, scores, PAIRS * (b - 1))
                hi, lo = qbd[u]
                heads = [slice(g * DH, (g + 1) * DH) for g in range(2)]
                for h in heads:
                    last = dve.tensor_copy(hi[h, :, h], qT1[h, :, bass.ds(b * S, S)])
                last.then_inc(q_hi, 1)
                dve.wait_ge(q_hi, b + 1)
                for h in heads:
                    last = low(lo[h, :, h], qT1[h, :, bass.ds(b * S, S)], hi[h, :, h])
                last.then_inc(qbd_ready, 1)

            def batch(b, u, more=True):
                maxes(b)
                for c in range(PAIRS):
                    inverse(b, c)
                    if more:
                        low_k(b + 1, c)
                if more:
                    block_q(b + 1, 1 - u)
                for c in range(LC):
                    evac_pt(b, c)
                evac_o(b)

            for half in range(2):
                for c in range(PAIRS):
                    taken(dve, "q1", half, c)
            block_q(0, 0)
            for c in range(PAIRS):
                low_k(0, c)
            batch(0, 0)
            batch(1, 1)
            with dve.Fori(1, NB // 2 - 1) as p:
                for u in range(2):
                    batch(2 * p + u, u)
            batch(NB - 2, 0)
            batch(NB - 1, 1, more=False)

            for t in range(NT + 1):
                if t < NT:
                    arrive(dve, "wo1", t)
                    dve.wait_ge(bo_added, t + 1)
                    n = dve.tensor_tensor(xs[:, t, :], xs[:, t, :], bank("wo1", t), ALU.add)
                    empty(n, "wo1", t)
                    taken(dve, "wo1", t)
                    spread(1, t, xs[:, t, :])
                if t:
                    centre(1, t - 1, xs[:, t - 1, :]).then_inc(xn_ready[1], 1)
                if t == NT - 1:
                    dve.wait_ge(w2_in, 11 * 16)
                    dve.tensor_copy(wgf[0][:], wgf_raw[:])
                    dve.tensor_copy(wg2[:], wg2_raw[:]).then_inc(small_hi, 1)
                    dve.wait_ge(small_hi, 1)
                    low(wgf[1][:], wgf_raw[:], wgf[0][:])
                    low(wg2[64:96], wg2_raw[64:96], wg2[64:96]).then_inc(small_split, 1)
                for u in ([t - 2] if t < NT else [NT - 2, NT - 1]):
                    if u >= 0:
                        dve.wait_ge(x2_hi, u + 1)
                        tok = slice(u * P, (u + 1) * P)
                        n = low(xnT2[1][:, :, tok], bank("T2", u).rearrange("p (k n) -> p k n", k=KD),
                                xnT2[0][:, :, tok])
                        empty(n, "T2", u)
            for t in range(NT):
                taken(dve, "k", t)
                link(dve.tensor_tensor(ksq[:], ksil[:, t, :], ksil[:, t, :], ALU.mult))
                if t >= 2:
                    dve.wait_ge(v_scaled, t - 1)
                link(dve.tensor_reduce(ksum[:, t % 2, :], ksq[:].rearrange("p (h d) -> p h d", d=HD), AX.X, ALU.add))
                dve.tensor_scalar(ksum[:, t % 2, :], ksum[:, t % 2, :], 1e-24, None, ALU.max
                                  ).then_inc(knorm_in, 1)
                if t == 0:
                    for half in range(2):
                        toks = slice(half * 512, (half + 1) * 512)
                        dve.wait_ge(t1_hi, half + 1)
                        n = low(t1T[32:64, toks], bank("t1", half)[32:64, :], t1T[32:64, toks])
                        empty(n, "t1", half)
                if t == 1:
                    arrive(dve, "z")
                    n = dve.tensor_copy(zf[:], bank("z")[:, 0:NT * H].rearrange("p (t h) -> p t h", h=H))
                    empty(n, "z")
                    taken(dve, "z")
                    link(dve.tensor_scalar(fb[:], zf[:], -1.0, None, ALU.mult))
                    dve.tensor_tensor(fa[:], zf[:], fb[:], ALU.min).then_inc(f_in, 1)
                if t == 4:
                    dve.wait_ge(f_ln, 1)
                    link(dve.tensor_scalar(fb[:], zf[:], 0.0, None, ALU.min))
                    link(dve.tensor_tensor(fa[:], fb[:], fa[:], ALU.subtract))
                    dve.tensor_copy(fh[:], fa[:]).then_inc(fh_ready, 1)
                    dve.wait_ge(fh_ready, 1)
                    low(fl[:], fa[:], fh[:]).then_inc(f_ready, 1)
            dve.wait_ge(woT_in, 16)
            arrive(dve, "k", NT - 1)
            dve.tensor_copy(wo2[0][:], woT2[:]).then_inc(wo2_hi, 1)
            dve.wait_ge(wo2_hi, 1)
            low(wo2[1][:], woT2[:], wo2[0][:]).then_inc(wo2_split, 1)
            for t in range(NT):
                arrive(dve, "kT", t)
                n = dve.tensor_copy(kT2[:, :, t * P:(t + 1) * P], bank("kT", t).rearrange("p (k n) -> p k n", k=KD))
                empty(n, "kT", t)

            def low_gated(u):
                dve.wait_ge(x4_hi, u + 1)
                if u >= 2:
                    arrive(dve, "wo2", u - 2)
                n = low(gatedT[u % 2][:], bank("T4", u).rearrange("p (k n) -> p k n", k=KD),
                        xnT2[0][:, :, u * P:(u + 1) * P])
                empty(n, "T4", u)

            def gated(u):
                arrive(dve, "o", u)
                taken(dve, "gate", u)
                n = dve.tensor_tensor(xn[:, u, :], bank("o", u), xn[:, u, :], ALU.mult)
                empty(n, "o", u)
                taken(dve, "o", u)
                spread(2, u, xn[:, u, :])

            def gated_norm(u):
                link(centre(2, u, xn[:, u, :]))
                dve.wait_ge(w2_in, 11 * 16)
                dve.tensor_tensor(xn[:, u, :], xn[:, u, :], lnw_rows[:], ALU.mult).then_inc(xn_ready[2], 1)

            def add_projected(u):
                arrive(dve, "wo2", u)
                n = dve.tensor_tensor(xs[:, u, :], xs[:, u, :], bank("wo2", u), ALU.add)
                empty(n, "wo2", u)
                taken(dve, "wo2", u)
                spread(3, u, xs[:, u, :])

            def last_norm(u):
                centre(3, u, xs[:, u, :]).then_inc(xn_ready[3], 1)

            def weights(t):
                for r in range(HR):
                    arrive(dve, "A", t, r)
                    taken(dve, "seg", t, r)
                    n = dve.tensor_tensor(Wt[:, r], bank("A", t, r).rearrange("p (c s) -> p c s", s=P),
                                          dec[t % 2][:, r], ALU.mult)
                    empty(n, "A", t, r)

            def evac_logit(u):
                arrive(dve, "logit", u)
                n = dve.tensor_copy(logit[:, u, :], bank("logit", u)[:, 0:E])
                empty(n, "logit", u)
                taken(dve, "logit", u)

            def choose(a, b):
                ts, bc = slice(a, b), [P, b - a, E, E]
                Lj, Le = logit[:, ts].unsqueeze(2).to_broadcast(bc), logit[:, ts].unsqueeze(3).to_broadcast(bc)
                dve.tensor_tensor(cmp[:, ts], Lj, Le, ALU.is_gt)
                link(dve.tensor_tensor(tie[:, ts], Lj, Le, ALU.is_equal))
                link(dve.tensor_tensor(tie[:, ts], tie[:, ts], lower[:, 0:E].unsqueeze(1).to_broadcast(bc), ALU.mult))
                link(dve.tensor_tensor(cmp[:, ts], cmp[:, ts], tie[:, ts], ALU.add))
                link(dve.tensor_reduce(rank[:, ts], cmp[:, ts], AX.X, ALU.add))
                dve.tensor_scalar(selm[:, ts], rank[:, ts], 1.5, None, ALU.is_lt).then_inc(sel_ready, 1)
                dve.tensor_scalar(m0[:, ts], rank[:, ts], 0.0, None, ALU.is_equal)
                link(dve.tensor_scalar(m1[:, ts], rank[:, ts], 1.0, None, ALU.is_equal))

            def last_second(pair, a, b):
                one, two, gap = pair[:, 0, a:b], pair[:, 1, a:b], swap[:, a:b]
                link(dve.tensor_tensor(gap, two, one, ALU.subtract))
                link(dve.tensor_tensor(gap, gap, m0[:, a:b, E - 1], ALU.mult))
                dve.tensor_tensor(one, one, gap, ALU.add)
                link(dve.tensor_tensor(two, two, gap, ALU.subtract))

            def find_slots(n):
                a, b = SENT[n]
                arrive(dve, "total", n)
                counts = bank("total", n)[:, 0:(b - a) * E].rearrange("p (t e) -> p t e", e=E)
                empty(dve.tensor_copy(tsum[:, a:b], counts), "total", n)
                taken(dve, "total", n)
                for t in range(max(a, 1), b):
                    link(dve.tensor_tensor(tsum[:, t, :], tsum[:, t, :], tsum[:, t - 1, :], ALU.add))
                arrive(dve, "prefix", n)
                places = bank("prefix", n)[:, 0:(b - a) * E].rearrange("p (t e) -> p t e", e=E)
                empty(dve.tensor_copy(posn[:, a:b], places), "prefix", n)
                taken(dve, "prefix", n)
                c = max(a, 1)
                link(dve.tensor_tensor(posn[:, c:b, :], posn[:, c:b, :], tsum[:, c - 1:b - 1, :], ALU.add))
                link(dve.tensor_tensor(posn[:, a:b], posn[:, a:b],
                                       cap_row[:].unsqueeze(1).to_broadcast([P, b - a, E]), ALU.add))
                for k, m in ((0, m0), (1, m1)):
                    link(dve.tensor_tensor(comb[:, a:b], m[:, a:b], posn[:, a:b], ALU.mult))
                    link(dve.tensor_reduce(slotf[:, k, a:b], comb[:, a:b], AX.X, ALU.add))
                last_second(slotf, a, b)
                dve.tensor_copy(slot_u[:, :, a:b], slotf[:, :, a:b]).then_inc(slots_ready, 1)

            for t in range(NT):
                if t >= 3:
                    last_norm(t - 3)
                if t >= 2:
                    low_gated(t - 2)
                if t >= 1:
                    gated(t - 1)
                if t >= 2:
                    add_projected(t - 2)
                if t >= 1:
                    gated_norm(t - 1)
                weights(t)
                if t >= 3:
                    evac_logit(t - 3)
            last_norm(NT - 3)
            low_gated(NT - 2)
            choose(*SENT[0])
            gated(NT - 1)
            gated_norm(NT - 1)
            evac_logit(NT - 3)
            find_slots(0)
            add_projected(NT - 2)
            low_gated(NT - 1)
            last_norm(NT - 2)
            add_projected(NT - 1)
            last_norm(NT - 1)
            evac_logit(NT - 2)
            choose(*SENT[1])
            find_slots(1)
            evac_logit(NT - 1)
            choose(*SENT[2])
            find_slots(2)
            link(dve.tensor_tensor(ge[:], tsum[:, NT - 1, :].unsqueeze(2).to_broadcast([P, E, NT]),
                                   steps[:].unsqueeze(1).to_broadcast([P, E, NT]), ALU.is_ge))
            link(dve.tensor_reduce(tcount[:], ge[:], AX.X, ALU.add))
            link(dve.tensor_scalar(tcount[:], tcount[:], 1.0, None, ALU.max))
            link(dve.tensor_tensor(tpart[:], lower[:], tcount[:].unsqueeze(1).to_broadcast([P, E + 1, E]), ALU.mult))
            link(dve.tensor_reduce(tstart[:], tpart[:], AX.X, ALU.add))
            dve.tensor_copy(bounds[:, 0:E + 1], tstart[:]).then_inc(bounds_ready, 1)
            link(dve.tensor_scalar(rowgap[:], tcount[:], -float(P), float(CAP), ALU.mult, ALU.add))
            link(dve.tensor_scalar(rowsum_f[:, 0:1], tstart[:, E:E + 1], -1.0, None, ALU.add))
            link(dve.tensor_tensor(tile_at[:], tile_no[:], rowsum_f[:, 0:1].to_broadcast([P, TILES_AHEAD]), ALU.min))
            ie = [P, TILES_AHEAD, E]
            link(dve.tensor_tensor(passed[:], tile_at[:].unsqueeze(2).to_broadcast(ie),
                                   tstart[:, 1:E + 1].unsqueeze(1).to_broadcast(ie), ALU.is_ge))
            link(dve.tensor_tensor(passed[:], passed[:], rowgap[:].unsqueeze(1).to_broadcast(ie), ALU.mult))
            link(dve.tensor_reduce(rowsum_f[:], passed[:], AX.X, ALU.add))
            link(dve.scalar_tensor_tensor(rowsum_f[:], tile_at[:], float(P), rowsum_f[:], ALU.mult, ALU.add))
            dve.tensor_copy(tile_row[:], rowsum_f[:]).then_inc(tables_ready, 1)
            for k, m in ((0, m0), (1, m1)):
                link(dve.tensor_tensor(comb[:], m[:], logit[:], ALU.mult))
                link(dve.tensor_reduce(lv[:, k, :], comb[:], AX.X, ALU.add))
            dve.tensor_tensor(lv[:, 0, :], lv[:, 1, :], lv[:, 0, :], ALU.subtract).then_inc(p01, 1)
            dve.wait_ge(e01, 1)
            link(dve.tensor_scalar(lv[:, 0, :], wgt[:, 1, :], 1.0, None, ALU.add))
            link(dve.reciprocal(wgt[:, 0, :], lv[:, 0, :]))
            link(dve.tensor_tensor(wgt[:, 1, :], wgt[:, 1, :], wgt[:, 0, :], ALU.mult))
            link(dve.tensor_tensor(comb[:], m0[:], wgt[:, 0, :].unsqueeze(2).to_broadcast([P, NT, E]), ALU.mult))
            link(dve.tensor_tensor(second[:], m1[:], wgt[:, 1, :].unsqueeze(2).to_broadcast([P, NT, E]), ALU.mult))
            dve.tensor_tensor(comb[:], comb[:], second[:], ALU.add).then_inc(comb_ready, 1)
            last_second(wgt, 0, NT)

            dve.sem_inc(y_evac, 1)
            dve.sem_inc(yrow_free, 2)

            def evac_x(n):
                dve.wait_ge(x_turned, n)
                dve.tensor_copy(xT[:], ps[:, 1, :].rearrange("p (k n) -> p k n", k=KD)).then_inc(xT_ready, 1)

            def copy_x(n, par):
                dve.wait_ge(xin_in, n * 16 + 16)
                dve.tensor_copy(xrow[:], xin[:, par, :]).then_inc(x_copied, 1)

            def split_first(g):
                f = slice(FG * g, FG * (g + 1))
                dve.tensor_copy(W2[0][:, f, :], W2first[:, f, :]).then_inc(w2_hi, 1)
                dve.wait_ge(w2_hi, g + 1)
                low(W2[1][:, f, :], W2first[:, f, :], W2[0][:, f, :]).then_inc(w2_split, 1)

            dve.wait_ge(w2first_in, 16 * NG)
            split_first(0)
            copy_x(0, 0)
            evac_x(1)
            copy_x(1, 1)
            for g in range(1, NG):
                split_first(g)

            def split_w2(e):
                for g in range(NG):
                    f = slice(FG * g, FG * (g + 1))
                    raw = W2raw[g % 2]
                    dve.wait_ge(w2raw_in[g % 2], (e - 1) * (16 * NG // 2) + 16 * (g // 2 + 1))
                    dve.tensor_copy(W2[0][:, f, :], raw[:]).then_inc(w2_hi, 1)
                    dve.wait_ge(w2_hi, e * NG + (g + 1))
                    low(W2[1][:, f, :], raw[:], W2[0][:, f, :]).then_inc(w2_split, 1)

            def expert_rows(e):
                first = dve.value_load(bounds[0:1, bass.ds(e, 1)], min_val=0, max_val=MAX_TILES - 1)
                end = dve.value_load(bounds[0:1, bass.ds(e + 1, 1)], min_val=1, max_val=MAX_TILES)
                with dve.Fori(first, end) as i:
                    evac_x(i + 2)
                    copy_x(i + 2, bass.ds(i % 2, 1))
                    dve.wait_ge(down_done, i + 1)
                    dve.wait_ge(yrow_free, i + 1)
                    dve.tensor_copy(yrow[:, bass.ds(i % 2, 1), :], ps[:, 0, :]).then_inc(y_evac, 1)

            with dve.Fori(0, E - 1) as e:
                expert_rows(e)
                split_w2(e + 1)
            expert_rows(E - 1)
            for half in range(2):
                arrive(dve, "combT", half)
                n = dve.tensor_copy(combT[:, half * 512:(half + 1) * 512], bank("combT", half)[0:E, :])
                empty(n, "combT", half)
            def add_expert(k, t, added):
                dve.wait_ge(g_in[k][t], 16)
                dve.scalar_tensor_tensor(xs[:, t, :], yg[k][:, t, :], wgt[:, k, t:t + 1], xs[:, t, :],
                                         ALU.mult, ALU.add).then_inc(added, 1)

            for t in range(NT + 2):
                if t < NT:
                    arrive(dve, "b2", t)
                    n = dve.tensor_tensor(xs[:, t, :], xs[:, t, :], bank("b2", t), ALU.add)
                    empty(n, "b2", t)
                    taken(dve, "b2", t)
                    add_expert(0, t, first_added)
                if t >= 2:
                    dve.wait_ge(first_added, t - 1)
                    add_expert(1, t - 2, out_ready)

        @block.tensor
        def _(pe):
            def product(dst, pairs):
                n = len(pairs)
                for i, (lhsT, rhs) in enumerate(pairs):
                    last = pe.matmul(dst, lhsT, rhs, start=(i == 0), stop=(i == n - 1))
                return last

            def product3(dst, pairs):
                return product(dst, [p for (ah, al), (bh, bl) in pairs for p in ((ah, bh), (al, bh), (ah, bl))])

            both = lambda split, *where: [part[where] for part in split]
            all_p = slice(None)

            def transposes(key, t, src):
                claim(pe, key, t)
                for k in range(KD):
                    last = pe.transpose(bank(key, t)[:, k * P:(k + 1) * P], src[:, k * P:(k + 1) * P], ident[:])
                fill(last, key, t)

            pe.wait_ge(consts_ready, 1)
            for t in range(NT):
                pe.wait_ge(xn_ready[0], t + 1)
                transposes("T1", t, xn[:, t, :])
            pe.wait_ge(wq_hi, KD)
            for half in range(2):
                toks = slice(half * 512, (half + 1) * 512)
                pe.wait_ge(x1_hi, (half + 1) * NT // 2)
                for low_parts in (False, True):
                    if low_parts:
                        pe.wait_ge(wq_split, KD)
                        for t in range(half * NT // 2, (half + 1) * NT // 2):
                            taken(pe, "T1", t)
                    for c in range(PAIRS):
                        if not low_parts:
                            claim(pe, "q1", half, c)
                        wh, wl = both(wq1, all_p, all_p, slice(c * P, (c + 1) * P))
                        xh, xl = both(xnT1, all_p, all_p, toks)
                        passes = ((wl, xh), (wh, xl)) if low_parts else ((wh, xh),)
                        for k in range(KD):
                            for n, (a, b) in enumerate(passes):
                                last = pe.matmul(bank("q1", half, c), a[:, k, :], b[:, k, :],
                                                 start=(not low_parts and k == 0),
                                                 stop=(low_parts and k == KD - 1 and n == 1))
                        if low_parts:
                            fill(last, "q1", half, c)

            def proj_k(b, u, c):
                if c >= 2:
                    wait(pe, k_split, PAIRS * b + c - 1)
                else:
                    wait(pe, v_evac, LC * (b - 1) + c + 3)
                product3(ps[:, 4 + c % 2, :],
                         [([w[:, k, c * P:(c + 1) * P] for w in wk1], [x_[:, k, :] for x_ in cT[u]])
                          for k in range(KC)]
                        ).then_inc(k_proj, 1)

            def proj_v(b, u, c):
                if c >= 2:
                    wait(pe, v_evac, LC * b + c - 1)
                else:
                    wait(pe, k_split, PAIRS * b + c + 3)
                product3(ps[:, 4 + c % 2, :],
                         [([x_[:, k, c * P:(c + 1) * P] for x_ in cT[u]], [w[:, k, :] for w in wv1])
                          for k in range(KC)]
                        ).then_inc(v_proj, 1)

            def score(b, u, c):
                pe.wait_ge(k_split, PAIRS * b + c + 1)
                wait(pe, exp_done, PAIRS * (b - 1) + c + 1)
                product3(ps[:, c, :], [([q[:, c, :] for q in qbd[u]], [k[:, c, :] for k in KT])]
                         ).then_inc(scores, 1)

            def turn(b, c):
                pe.wait_ge(norm_done, PAIRS * b + c + 1)
                wait(pe, pt_evac, PAIRS * b + c)
                for j in range(LC):
                    last = pe.transpose(ps[:, 6, j * P:(j + 1) * P], prob[:, c, j * P:(j + 1) * P], ident[:])
                last.then_inc(pt_done, 1)

            def attend(b, u, c):
                pe.wait_ge(pt_evac, PAIRS * b + c + 1)
                if c == 0:
                    pe.wait_ge(v_evac, LC * (b + 1))
                    wait(pe, o_evac, b)
                product(ps[:, 7, c * P:(c + 1) * P],
                        [(V[u][:, j, c * P:(c + 1) * P], PT[c % 2][:, j, :]) for j in range(LC)]
                        ).then_inc(pv_done, 1)

            def batch(b, u, more=True):
                pe.wait_ge(qbd_ready, b + 1)
                for c in range(PAIRS):
                    score(b, u, c)
                if more:
                    pe.wait_ge(c_split, b + 2)
                    for c in range(PAIRS):
                        proj_k(b + 1, 1 - u, c)
                for c in range(LC):
                    if more:
                        proj_v(b + 1, 1 - u, c)
                    turn(b, c)
                    if c >= 1:
                        attend(b, u, c - 1)
                attend(b, u, PAIRS - 1)

            for b in range(8):
                pe.wait_ge(emptied[b], RING1 // 8)
            pe.wait_ge(w_split, 2)
            pe.wait_ge(c_split, 1)
            for c in range(PAIRS):
                proj_k(0, 0, c)
            for c in range(LC):
                proj_v(0, 0, c)
            batch(0, 0)
            batch(1, 1)
            with pe.Fori(1, NB // 2 - 1) as p:
                for u in range(2):
                    batch(2 * p + u, u)
            batch(NB - 2, 0)
            batch(NB - 1, 1, more=False)

            pe.wait_ge(wo_split, KD)
            pe.wait_ge(o_evac, NB)
            for t in range(NT):
                tok = slice(t * P, (t + 1) * P)
                claim(pe, "wo1", t)
                fill(product3(bank("wo1", t), [(both(OT, all_p, k, tok), both(wo1, all_p, k)) for k in range(KD)]),
                     "wo1", t)
                if t >= 2:
                    pe.wait_ge(xn_ready[1], t - 1)
                    transposes("T2", t - 2, xn[:, t - 2, :])
            for t in range(NT):
                tok = slice(t * P, (t + 1) * P)
                for what, w, there, late in (("k", wk2, wk2_split, NT - 2), ("v", wv2, wv2_split, NT - 1)):
                    claim(pe, what, t)
                    if t == 0:
                        pe.wait_ge(there, KD)
                    taken(pe, "T2", t)
                    fill(product3(bank(what, t), [(both(xnT2, all_p, k, tok), both(w, all_p, k))
                                                  for k in range(KD)]), what, t)
                    if t == 0:
                        pe.wait_ge(xn_ready[1], late + 1)
                        transposes("T2", late, xn[:, late, :])
                if t == 0:
                    pe.wait_ge(small_split, 1)
                    for u in (NT - 2, NT - 1):
                        taken(pe, "T2", u)
                    for half in range(2):
                        toks = slice(half * 512, (half + 1) * 512)
                        claim(pe, "t1", half)
                        fill(product3(bank("t1", half)[0:GF, :],
                                      [(both(wgf, all_p, k), both(xnT2, all_p, k, toks)) for k in range(KD)]),
                             "t1", half)
                if t == 1:
                    claim(pe, "z")
                    taken(pe, "t1", 1)
                    for u in range(NT):
                        last = pe.transpose(bank("z")[:, u * H:(u + 1) * H], zT[96:GF, u * P:(u + 1) * P],
                                            ident[96:GF, 96:GF])
                    fill(last, "z")
                if t % 4 == 3:
                    pe.wait_ge(wq2_split, KD)
                    toks = slice((t - 3) * P, (t + 1) * P)
                    for c in range(KD):
                        claim(pe, "q", t // 4, c)
                        fill(product3(bank("q", t // 4, c),
                                      [(both(wq2, all_p, k, slice(c * P, (c + 1) * P)), both(xnT2, all_p, k, toks))
                                       for k in range(KD)]), "q", t // 4, c)
            for half in range(2):
                taken(pe, "t1", half)
            for t in range(NT):
                claim(pe, "gate", t)
                fill(product(bank("gate", t), [(t1T[:, t * P:(t + 1) * P], wg2[:])]), "gate", t)
                taken(pe, "k", t)
                transposes("kT", t, ksil[:, t, :])
            pe.wait_ge(masks_r, 1)
            def decays(t):
                for r in range(HR):
                    claim(pe, "seg", t, r)
                    pe.wait_ge(gates_ready, 2 * (HR * t + r + 1))
                    fill(product(bank("seg", t, r),
                                 [(ident_r[:], unseen[:].unsqueeze(1).to_broadcast([P, HR, P])),
                                  (after_r[:], gates[0][:, r]), (after_r[:], gates[1][:, r])]), "seg", t, r)

            def turn_gated(u):
                pe.wait_ge(xn_ready[2], u + 1)
                transposes("T4", u, xn[:, u, :])

            def turn_last(u):
                pe.wait_ge(xn_ready[3], u + 1)
                transposes("T5", u, xn[:, u, :])

            def head_outputs(u, c):
                if c == 0:
                    claim(pe, "o", u)
                    for r in range(HR):
                        taken(pe, "A", u, r)
                    pe.wait_ge(v_scaled, u + 1)
                for r in range(HR):
                    h = slice((HR * c + r) * HD, (HR * c + r + 1) * HD)
                    last = pe.matmul(bank("o", u)[:, h], Wt[:, r, c, :], vt[:, u, h], start=True, stop=True)
                if c == HR - 1:
                    fill(last, "o", u)

            def projected(u, c):
                if c == 0:
                    claim(pe, "wo2", u)
                    taken(pe, "T4", u)
                    pe.wait_ge(wo2_split, 1)
                high, lo = xnT2[0][:, c, u * P:(u + 1) * P], gatedT[u % 2][:, c, :]
                for n, (a, b) in enumerate(((high, wo2[0]), (lo, wo2[0]), (high, wo2[1]))):
                    last = pe.matmul(bank("wo2", u), a, b[:, c, :],
                                     start=(c == 0 and n == 0), stop=(c == KD - 1 and n == 2))
                if c == KD - 1:
                    fill(last, "wo2", u)

            def scored(t, r):
                if r == 0:
                    for c in range(KD):
                        taken(pe, "q", t // 4, c)
                    taken(pe, "kT", t)
                claim(pe, "A", t, r)
                h, tok = slice(r * HD, (r + 1) * HD), slice(t * P, (t + 1) * P)
                for c in range(HR):
                    last = pe.matmul(bank("A", t, r)[:, c * P:(c + 1) * P], kT2[h, c, tok], qT2[h, c, tok],
                                     start=True, stop=True)
                fill(last, "A", t, r)

            def logits(u, k):
                if k == 0:
                    claim(pe, "logit", u)
                    taken(pe, "T5", u)
                last = pe.matmul(bank("logit", u)[:, 0:E], xnT[:, k, u * P:(u + 1) * P], gw[:, k, :],
                                 start=(k == 0), stop=(k == KD - 1))
                if k == KD - 1:
                    fill(last, "logit", u)

            def whole(part, u):
                for k in range(KD):
                    part(u, k)

            def ranks(n):
                a, b = SENT[n]
                pe.wait_ge(sel_ready, n + 1)
                rows = selm[:, a:b].rearrange("p t e -> p (t e)")
                for key, m in (("prefix", before), ("total", ones)):
                    claim(pe, key, n)
                    fill(product(bank(key, n)[:, 0:(b - a) * E], [(m[:], rows)]), key, n)

            for t in range(NT):
                decays(t)
                if t >= 2:
                    turn_gated(t - 2)
                if t >= 3:
                    turn_last(t - 3)
                for c in range(HR):
                    if t >= 1:
                        head_outputs(t - 1, c)
                    if t >= 2:
                        projected(t - 2, c)
                for r in range(HR):
                    scored(t, r)
                if t >= 3:
                    whole(logits, t - 3)
            turn_gated(NT - 2)
            turn_last(NT - 3)
            whole(head_outputs, NT - 1)
            whole(logits, NT - 3)
            ranks(0)
            whole(projected, NT - 2)
            turn_gated(NT - 1)
            whole(projected, NT - 1)
            turn_last(NT - 2)
            whole(logits, NT - 2)
            ranks(1)
            turn_last(NT - 1)
            whole(logits, NT - 1)

            ranks(2)
            for b in range(8):
                pe.wait_ge(emptied[b], RING2[b])

            def turn_x():
                for k in range(KD):
                    last = pe.transpose(ps[:, 1, k * P:(k + 1) * P], xrow[:, k * P:(k + 1) * P], ident[:])
                last.then_inc(x_turned, 1)

            def expert_tile(u, e, i, loads):
                pe.wait_ge(w1_in[u], loads)
                pe.wait_ge(xT_ready, i + 1)
                for g in range(NG):
                    for j in range(FG):
                        f = FG * g + j
                        last = product(ps[:, 4 + g, j * P:(j + 1) * P],
                                       [(W1[u][:, k, f * P:(f + 1) * P], xT[:, k, :]) for k in range(KD)])
                    last.then_inc(up_done, 1)
                pe.wait_ge(x_copied, i + 2)
                turn_x()
                pe.wait_ge(y_evac, i + 1)
                for g in range(NG):
                    pe.wait_ge(w2_split, e * NG + (g + 1))
                    pe.wait_ge(h_split, i * NG + (g + 3))
                    for f in range(FG * g, FG * (g + 1)):
                        for n, (a, b) in enumerate(((1, 0), (0, 0), (0, 1))):
                            last = pe.matmul(ps[:, 0, :], hT[a][:, f, :], W2[b][:, f, :],
                                             start=(f == 0 and n == 0), stop=(f == KF - 1 and n == 2))
                last.then_inc(down_done, 1)

            pe.wait_ge(bounds_ready, 1)
            pe.wait_ge(x_copied, 1)
            turn_x()
            with pe.Fori(0, E // 2) as p:
                for u in range(2):
                    first = pe.value_load(bounds[0:1, bass.ds(2 * p + u, 1)], min_val=0, max_val=MAX_TILES - 1)
                    end = pe.value_load(bounds[0:1, bass.ds(2 * p + u + 1, 1)], min_val=1, max_val=MAX_TILES)
                    with pe.Fori(first, end) as i:
                        expert_tile(u, 2 * p + u, i, p * 16 + 16)

            total = pe.value_load(bounds[0:1, E:E + 1], min_val=E, max_val=MAX_TILES)
            pe.wait_ge(y_evac, total + 1)
            pe.wait_ge(comb_ready, 1)
            for half in range(2):
                claim(pe, "combT", half)
                for j in range(4):
                    last = pe.transpose(bank("combT", half)[0:E, j * P:(j + 1) * P], comb[:, 4 * half + j, :],
                                        ident[:])
                fill(last, "combT", half)
            for t in range(NT):
                claim(pe, "b2", t)
                taken(pe, "combT", t // 4)
                fill(product(bank("b2", t), [(combT[:, t * P:(t + 1) * P], b2_sb[:])]), "b2", t)


_INS = ["x", "ctxT", "xWq", "xWk", "xWv", "xWo", "xbo", "aWqT", "aWkT", "aWvT", "aWfT", "aWg1T", "aWg2T",
        "a_ln_w", "aWoT", "gate_w", "w1", "b1T", "w2", "b2"]


def kernel(**inputs):
    import numpy as np
    import concourse.bacc as bacc
    from concourse.bass_utils import run_bass_kernel_spmd

    g = {k: np.asarray(v) for k, v in inputs.items()}
    B, S, D = g["x"].shape
    E, _, F = g["L0_ffn_w1"].shape
    host = {
        "x": g["x"].reshape(B * S, D),
        "ctxT": g["ctx_768"].transpose(0, 2, 1),
        "xWq": g["L0_xattn_Wq"], "xWk": g["L0_xattn_Wk"], "xWv": g["L0_xattn_Wv"], "xWo": g["L0_xattn_Wo"],
        "xbo": g["L0_xattn_bo"].reshape(1, D),
        "aWqT": g["L0_attn_Wq"].T, "aWkT": g["L0_attn_Wk"].T, "aWvT": g["L0_attn_Wv"].T,
        "aWfT": g["L0_attn_Wf"].T, "aWg1T": g["L0_attn_Wg1"].T, "aWg2T": g["L0_attn_Wg2"].T,
        "a_ln_w": g["L0_attn_ln_w"].reshape(1, D), "aWoT": g["L0_attn_Wo"].T,
        "gate_w": g["L0_ffn_gate_w"], "w1": g["L0_ffn_w1"],
        "b1T": g["L0_ffn_b1"].reshape(E, F // 128, 128).transpose(2, 0, 1),
        "w2": g["L0_ffn_w2"], "b2": g["L0_ffn_b2"],
    }
    nc = bacc.Bacc("TRN2", target_bir_lowering=False, num_devices=1)
    arrays, args = {}, []
    for name in _INS:
        a = np.ascontiguousarray(host[name])
        arrays[f"in_{name}"] = a
        args.append(nc.dram_tensor(f"in_{name}", a.shape, mybir.dt.from_np(a.dtype), kind="ExternalInput").ap())
    fp32 = mybir.dt.float32
    args.append(nc.dram_tensor("out_rows", (B * S, D), fp32, kind="ExternalOutput").ap())
    rows = E * B * S
    args.append(nc.dram_tensor("slots", (rows, D), fp32, kind="Internal").ap())
    perceiver_layer(nc, *args)
    r = run_bass_kernel_spmd(nc, [arrays], core_ids=[0])
    return r.results[0]["out_rows"].reshape(B, S, D)
```
